# Optimizing a Trainium2 kernel written in Bass

```python
import numpy as np
import jax
import jax.numpy as jnp

def _softmax(x, axis=-1):
    return jax.nn.softmax(x, axis=axis)

def _gelu(x):
    return jax.nn.gelu(x, approximate=True)

def _silu(x):
    return jax.nn.silu(x)

def _sigmoid(x):
    return jax.nn.sigmoid(x)

def _layernorm(x, axis=-1, eps=1e-05):
    m = jnp.mean(x, axis=axis, keepdims=True)
    v = jnp.var(x, axis=axis, keepdims=True)
    return (x - m) / jnp.sqrt(v + eps)

def _scatter_add(tgt, idx, src, axis=0):
    return tgt.at[idx].add(src)

def _segment_sum(src, seg, n):
    return jax.ops.segment_sum(src, seg, n)
kernel_name = 'mk_seq_postln_d1_jaxref_r8_5508ad'

def setup_inputs(seed: int=0):
    np.random.seed(seed)
    _w = jnp.asarray

    def _L0_attn_setup():
        import jax, jax.numpy as jnp
        import numpy as np
        B, T, NE, H = (4, 128, 128, 16)
        HS = NE // H
        EPS = 0.00064

        def _forward(x, time_maa_x, time_maa, maa_w1, maa_w2, decay_w1, decay_w2, aaa_w1, aaa_w2, kkk_w1, kkk_w2, gate_w1, gate_w2, ma_w1, ma_w2, mk_w1, mk_w2, time_decay, time_faaaa, time_aaaaa, time_misc_a, time_misc_k, Wr, Wk, Wv, Wo, ln_w, ln_b):
            Bx, Tx, C = x.shape
            xx = jnp.pad(x, ((0, 0), (1, 0), (0, 0)))[:, :Tx] - x
            mix = x + xx * time_maa_x
            lo = jnp.tanh(jnp.einsum('btc,dc->btd', mix, maa_w1)).reshape(Bx, Tx, 4, 32)
            lo = jnp.einsum('btgk,gkc->gbtc', lo, maa_w2)
            xm = x[None] + xx[None] * (lo + time_maa)
            xrg, xwa, xk, xv = (xm[0], xm[1], xm[2], xm[3])
            r = xrg @ Wr.T
            g = jnp.tanh(xrg @ gate_w1.T) @ gate_w2
            k = xk @ Wk.T
            v = xv @ Wv.T
            w2 = jnp.tanh(xwa @ decay_w1.T) @ decay_w2
            w = -jax.nn.softplus(-(time_decay + w2)) - 0.5
            kk = k + jnp.tanh(xk @ kkk_w1.T) @ kkk_w2
            kkh = kk.reshape(Bx, Tx, H, HS)
            kk = (kkh / jnp.maximum(jnp.linalg.norm(kkh, axis=-1, keepdims=True), 1e-12)).reshape(Bx, Tx, C)
            a = jax.nn.sigmoid(time_aaaaa + xwa @ aaa_w1.T @ aaa_w2)
            ma = jax.nn.sigmoid(time_misc_a + xwa @ ma_w1.T @ ma_w2)
            k = k * ma + k * a * (1.0 - ma)
            mk = jax.nn.sigmoid(time_misc_k + xk @ mk_w1.T @ mk_w2)
            k = k * jnp.exp(w * mk)
            b = -kk * a

            def to_th(t):
                return t.reshape(Bx, Tx, H, HS).transpose(1, 0, 2, 3)
            qt, wt, kt, vt, at, bt = map(to_th, (r, w, k, v, kk, b))
            wt = jnp.exp(-jnp.exp(wt))

            def step(s, inp):
                q_, w_, k_, v_, a_, b_ = inp
                sa = jnp.einsum('bhij,bhj->bhi', s, a_)
                s = s * w_[:, :, None, :] + sa[..., None] * b_[:, :, None, :] + v_[..., None] * k_[:, :, None, :]
                return (s, jnp.einsum('bhij,bhj->bhi', s, q_))
            s0 = jnp.zeros((Bx, H, HS, HS), x.dtype)
            _, y = jax.lax.scan(step, s0, (qt, wt, kt, vt, at, bt))
            y = y.transpose(1, 0, 2, 3).reshape(Bx, Tx, C)
            yg = y.reshape(Bx, Tx, H, HS)
            mu = yg.mean(-1, keepdims=True)
            var = ((yg - mu) ** 2).mean(-1, keepdims=True)
            y = ((yg - mu) / jnp.sqrt(var + EPS)).reshape(Bx, Tx, C) * ln_w + ln_b
            rk = (r.reshape(Bx, Tx, H, HS) * k.reshape(Bx, Tx, H, HS) * time_faaaa.reshape(H, HS)).sum(-1, keepdims=True)
            y = y + (rk * v.reshape(Bx, Tx, H, HS)).reshape(Bx, Tx, C)
            return y * g @ Wo.T
        key = jax.random.key(seed)
        ks = jax.random.split(key, 30)

        def rn(k, shape, s):
            return jax.random.normal(k, shape, jnp.float32) * s
        d = {}
        d['x'] = jax.random.normal(ks[0], (B, T, NE), jnp.float32)
        d['time_maa_x'] = jax.random.uniform(ks[1], (NE,), jnp.float32)
        d['time_maa'] = jax.random.uniform(ks[2], (4, 1, 1, NE), jnp.float32)
        d['maa_w1'] = rn(ks[3], (128, NE), 0.02)
        d['maa_w2'] = rn(ks[4], (4, 32, NE), 0.02)
        d['decay_w1'] = rn(ks[5], (64, NE), 0.02)
        d['decay_w2'] = rn(ks[6], (64, NE), 0.02)
        d['aaa_w1'] = rn(ks[7], (16, NE), 0.02)
        d['aaa_w2'] = rn(ks[8], (16, NE), 0.02)
        d['kkk_w1'] = rn(ks[9], (16, NE), 0.02)
        d['kkk_w2'] = rn(ks[10], (16, NE), 0.02)
        d['gate_w1'] = rn(ks[11], (128, NE), 0.02)
        d['gate_w2'] = rn(ks[12], (128, NE), 0.02)
        d['ma_w1'] = rn(ks[13], (16, NE), 0.02)
        d['ma_w2'] = rn(ks[14], (16, NE), 0.02)
        d['mk_w1'] = rn(ks[15], (16, NE), 0.02)
        d['mk_w2'] = rn(ks[16], (16, NE), 0.02)
        d['time_decay'] = jnp.linspace(-6.5, -1.5, NE, dtype=jnp.float32)
        d['time_faaaa'] = rn(ks[17], (NE,), 0.02)
        d['time_aaaaa'] = rn(ks[18], (NE,), 0.02)
        d['time_misc_a'] = rn(ks[19], (NE,), 0.02)
        d['time_misc_k'] = rn(ks[20], (NE,), 0.02)
        d['Wr'] = rn(ks[21], (NE, NE), 0.5 / NE ** 0.5)
        d['Wk'] = rn(ks[22], (NE, NE), 0.05 / NE ** 0.5)
        d['Wv'] = rn(ks[23], (NE, NE), 0.5 / NE ** 0.5)
        d['Wo'] = rn(ks[24], (NE, NE), 1.0 / NE ** 0.5)
        d['ln_w'] = jnp.ones((NE,), jnp.float32)
        d['ln_b'] = jnp.zeros((NE,), jnp.float32)
        return d
    _L0_attn_in = _L0_attn_setup()

    def _L0_ffn_setup():
        import jax, jax.numpy as jnp
        import numpy as np
        DIM = 128
        DEPTH = 6
        HEADS = 16
        DIM_HEAD = 64
        WINDOW = 32
        INNER = HEADS * DIM_HEAD
        DIM_INNER = int(DIM * 4 * 2 / 3)
        QK_SCALE = 8.0

        def shift_tokens(t):
            a, s = jnp.split(t, 2, -1)
            s = jnp.pad(s, ((0, 0), (1, 0), (0, 0)))[:, :-1]
            return jnp.concatenate([a, s], -1)

        def l2norm(t):
            return t / jnp.maximum(jnp.linalg.norm(t, axis=-1, keepdims=True), 1e-12)

        def rotate_half(x):
            x1, x2 = jnp.split(x, 2, -1)
            return jnp.concatenate([-x2, x1], -1)

        def rotary_tables(n):
            half = jnp.arange(0, DIM_HEAD, 2, dtype=jnp.float32)
            inv_freq = 1.0 / 10000.0 ** (half / DIM_HEAD)
            t = jnp.arange(n, dtype=jnp.float32)
            freqs = t[:, None] * inv_freq[None, :]
            freqs = jnp.concatenate([freqs, freqs], -1)
            base_scale = (half + 0.4 * DIM_HEAD) / (1.4 * DIM_HEAD)
            power = (t - n // 2) / (WINDOW // 2)
            scale = base_scale[None, :] ** power[:, None]
            scale = jnp.concatenate([scale, scale], -1)
            return (freqs, scale)

        def local_attention(q, k, v):
            b, h, n, d = q.shape
            w = WINDOW
            nw = n // w
            bq = q.reshape(b, h, nw, w, d)
            bk = k.reshape(b, h, nw, w, d)
            bv = v.reshape(b, h, nw, w, d)

            def look(t):
                p = jnp.pad(t, ((0, 0), (0, 0), (1, 0), (0, 0), (0, 0)))
                return jnp.concatenate([p[:, :, :nw], p[:, :, 1:]], axis=3)
            bk2, bv2 = (look(bk), look(bv))
            seq = jnp.arange(n).reshape(nw, w)
            seq_p = jnp.pad(seq, ((1, 0), (0, 0)), constant_values=-1)
            jt = jnp.concatenate([seq_p[:nw], seq_p[1:]], axis=1)
            it = seq[:, :, None]
            jb = jt[:, None, :]
            mask = (it < jb) | (it > jb + w) | (jb == -1)
            sim = jnp.einsum('bhwie,bhwje->bhwij', bq, bk2) * QK_SCALE
            sim = jnp.where(mask, -jnp.finfo(sim.dtype).max, sim)
            attn = jax.nn.softmax(sim, -1)
            out = jnp.einsum('bhwij,bhwje->bhwie', attn, bv2)
            return out.reshape(b, h, n, d)

        def attn_layer(x, Wqkv, qs, ksc, Wo):
            b, n, _ = x.shape
            qkv = x @ Wqkv
            q, k, v = jnp.split(qkv, 3, -1)
            sh = lambda t: t.reshape(b, n, HEADS, DIM_HEAD).transpose(0, 2, 1, 3)
            q, k, v = (sh(q), sh(k), sh(v))
            q = l2norm(q) * qs
            k = l2norm(k) * ksc
            freqs, scale = rotary_tables(n)
            cos, sin = (jnp.cos(freqs), jnp.sin(freqs))
            q = q * cos * scale + rotate_half(q) * sin * scale
            inv = 1.0 / scale
            k = k * cos * inv + rotate_half(k) * sin * inv
            out = local_attention(q, k, v)
            out = out.transpose(0, 2, 1, 3).reshape(b, n, INNER)
            return out @ Wo

        def ffn_layer(x, g, bln, W1, b1, W2, b2):
            mu = x.mean(-1, keepdims=True)
            var = ((x - mu) ** 2).mean(-1, keepdims=True)
            xn = (x - mu) / jnp.sqrt(var + 1e-05) * g + bln
            hg = xn @ W1 + b1
            a, gate = jnp.split(hg, 2, -1)
            return a * jax.nn.gelu(gate, approximate=False) @ W2 + b2
        key = jax.random.key(seed)
        ks = jax.random.split(key, 8)
        B, N = (2, 256)
        init = lambda k, shape: jax.random.normal(k, shape, jnp.float32) * 0.02
        return {'x': jax.random.normal(ks[0], (B, N, DIM), jnp.float32), 'Wqkv': init(ks[1], (DEPTH, DIM, 3 * INNER)), 'q_scale': jnp.ones((DEPTH, DIM_HEAD), jnp.float32), 'k_scale': jnp.ones((DEPTH, DIM_HEAD), jnp.float32), 'Wo': init(ks[2], (DEPTH, INNER, DIM)), 'ln_g': jnp.ones((DEPTH, DIM), jnp.float32), 'ln_b': jnp.zeros((DEPTH, DIM), jnp.float32), 'W1': init(ks[3], (DEPTH, DIM, 2 * DIM_INNER)), 'b1': jnp.zeros((DEPTH, 2 * DIM_INNER), jnp.float32), 'W2': init(ks[4], (DEPTH, DIM_INNER, DIM)), 'b2': jnp.zeros((DEPTH, DIM), jnp.float32)}
    _L0_ffn_in = _L0_ffn_setup()
    _d = {'L0_attn_x': _L0_attn_in['x'], 'L0_attn_time_maa_x': _L0_attn_in['time_maa_x'], 'L0_attn_time_maa': _L0_attn_in['time_maa'], 'L0_attn_maa_w1': _L0_attn_in['maa_w1'], 'L0_attn_maa_w2': _L0_attn_in['maa_w2'], 'L0_attn_decay_w1': _L0_attn_in['decay_w1'], 'L0_attn_decay_w2': _L0_attn_in['decay_w2'], 'L0_attn_aaa_w1': _L0_attn_in['aaa_w1'], 'L0_attn_aaa_w2': _L0_attn_in['aaa_w2'], 'L0_attn_kkk_w1': _L0_attn_in['kkk_w1'], 'L0_attn_kkk_w2': _L0_attn_in['kkk_w2'], 'L0_attn_gate_w1': _L0_attn_in['gate_w1'], 'L0_attn_gate_w2': _L0_attn_in['gate_w2'], 'L0_attn_ma_w1': _L0_attn_in['ma_w1'], 'L0_attn_ma_w2': _L0_attn_in['ma_w2'], 'L0_attn_mk_w1': _L0_attn_in['mk_w1'], 'L0_attn_mk_w2': _L0_attn_in['mk_w2'], 'L0_attn_time_decay': _L0_attn_in['time_decay'], 'L0_attn_time_faaaa': _L0_attn_in['time_faaaa'], 'L0_attn_time_aaaaa': _L0_attn_in['time_aaaaa'], 'L0_attn_time_misc_a': _L0_attn_in['time_misc_a'], 'L0_attn_time_misc_k': _L0_attn_in['time_misc_k'], 'L0_attn_Wr': _L0_attn_in['Wr'], 'L0_attn_Wk': _L0_attn_in['Wk'], 'L0_attn_Wv': _L0_attn_in['Wv'], 'L0_attn_Wo': _L0_attn_in['Wo'], 'L0_attn_ln_w': _L0_attn_in['ln_w'], 'L0_attn_ln_b': _L0_attn_in['ln_b'], 'L0_ffn_Wqkv': _L0_ffn_in['Wqkv'], 'L0_ffn_q_scale': _L0_ffn_in['q_scale'], 'L0_ffn_k_scale': _L0_ffn_in['k_scale'], 'L0_ffn_Wo': _L0_ffn_in['Wo'], 'L0_ffn_ln_g': _L0_ffn_in['ln_g'], 'L0_ffn_ln_b': _L0_ffn_in['ln_b'], 'L0_ffn_W1': _L0_ffn_in['W1'], 'L0_ffn_b1': _L0_ffn_in['b1'], 'L0_ffn_W2': _L0_ffn_in['W2'], 'L0_ffn_b2': _L0_ffn_in['b2']}
    _x0 = _d['L0_attn_x']
    _d['L0_attn_x'] = jax.random.normal(jax.random.fold_in(jax.random.key(seed), 1), (2, 1024, 128), dtype=_x0.dtype)
    del _x0
    return _d

def reference(L0_attn_x, L0_attn_time_maa_x, L0_attn_time_maa, L0_attn_maa_w1, L0_attn_maa_w2, L0_attn_decay_w1, L0_attn_decay_w2, L0_attn_aaa_w1, L0_attn_aaa_w2, L0_attn_kkk_w1, L0_attn_kkk_w2, L0_attn_gate_w1, L0_attn_gate_w2, L0_attn_ma_w1, L0_attn_ma_w2, L0_attn_mk_w1, L0_attn_mk_w2, L0_attn_time_decay, L0_attn_time_faaaa, L0_attn_time_aaaaa, L0_attn_time_misc_a, L0_attn_time_misc_k, L0_attn_Wr, L0_attn_Wk, L0_attn_Wv, L0_attn_Wo, L0_attn_ln_w, L0_attn_ln_b, L0_ffn_Wqkv, L0_ffn_q_scale, L0_ffn_k_scale, L0_ffn_Wo, L0_ffn_ln_g, L0_ffn_ln_b, L0_ffn_W1, L0_ffn_b1, L0_ffn_W2, L0_ffn_b2):

    def _L0_attn_ref(x, time_maa_x, time_maa, maa_w1, maa_w2, decay_w1, decay_w2, aaa_w1, aaa_w2, kkk_w1, kkk_w2, gate_w1, gate_w2, ma_w1, ma_w2, mk_w1, mk_w2, time_decay, time_faaaa, time_aaaaa, time_misc_a, time_misc_k, Wr, Wk, Wv, Wo, ln_w, ln_b):
        import jax, jax.numpy as jnp
        import numpy as np
        B, T, NE, H = (4, 128, 128, 16)
        HS = NE // H
        EPS = 0.00064

        def _forward(x, time_maa_x, time_maa, maa_w1, maa_w2, decay_w1, decay_w2, aaa_w1, aaa_w2, kkk_w1, kkk_w2, gate_w1, gate_w2, ma_w1, ma_w2, mk_w1, mk_w2, time_decay, time_faaaa, time_aaaaa, time_misc_a, time_misc_k, Wr, Wk, Wv, Wo, ln_w, ln_b):
            Bx, Tx, C = x.shape
            xx = jnp.pad(x, ((0, 0), (1, 0), (0, 0)))[:, :Tx] - x
            mix = x + xx * time_maa_x
            lo = jnp.tanh(jnp.einsum('btc,dc->btd', mix, maa_w1)).reshape(Bx, Tx, 4, 32)
            lo = jnp.einsum('btgk,gkc->gbtc', lo, maa_w2)
            xm = x[None] + xx[None] * (lo + time_maa)
            xrg, xwa, xk, xv = (xm[0], xm[1], xm[2], xm[3])
            r = xrg @ Wr.T
            g = jnp.tanh(xrg @ gate_w1.T) @ gate_w2
            k = xk @ Wk.T
            v = xv @ Wv.T
            w2 = jnp.tanh(xwa @ decay_w1.T) @ decay_w2
            w = -jax.nn.softplus(-(time_decay + w2)) - 0.5
            kk = k + jnp.tanh(xk @ kkk_w1.T) @ kkk_w2
            kkh = kk.reshape(Bx, Tx, H, HS)
            kk = (kkh / jnp.maximum(jnp.linalg.norm(kkh, axis=-1, keepdims=True), 1e-12)).reshape(Bx, Tx, C)
            a = jax.nn.sigmoid(time_aaaaa + xwa @ aaa_w1.T @ aaa_w2)
            ma = jax.nn.sigmoid(time_misc_a + xwa @ ma_w1.T @ ma_w2)
            k = k * ma + k * a * (1.0 - ma)
            mk = jax.nn.sigmoid(time_misc_k + xk @ mk_w1.T @ mk_w2)
            k = k * jnp.exp(w * mk)
            b = -kk * a

            def to_th(t):
                return t.reshape(Bx, Tx, H, HS).transpose(1, 0, 2, 3)
            qt, wt, kt, vt, at, bt = map(to_th, (r, w, k, v, kk, b))
            wt = jnp.exp(-jnp.exp(wt))

            def step(s, inp):
                q_, w_, k_, v_, a_, b_ = inp
                sa = jnp.einsum('bhij,bhj->bhi', s, a_)
                s = s * w_[:, :, None, :] + sa[..., None] * b_[:, :, None, :] + v_[..., None] * k_[:, :, None, :]
                return (s, jnp.einsum('bhij,bhj->bhi', s, q_))
            s0 = jnp.zeros((Bx, H, HS, HS), x.dtype)
            _, y = jax.lax.scan(step, s0, (qt, wt, kt, vt, at, bt))
            y = y.transpose(1, 0, 2, 3).reshape(Bx, Tx, C)
            yg = y.reshape(Bx, Tx, H, HS)
            mu = yg.mean(-1, keepdims=True)
            var = ((yg - mu) ** 2).mean(-1, keepdims=True)
            y = ((yg - mu) / jnp.sqrt(var + EPS)).reshape(Bx, Tx, C) * ln_w + ln_b
            rk = (r.reshape(Bx, Tx, H, HS) * k.reshape(Bx, Tx, H, HS) * time_faaaa.reshape(H, HS)).sum(-1, keepdims=True)
            y = y + (rk * v.reshape(Bx, Tx, H, HS)).reshape(Bx, Tx, C)
            return y * g @ Wo.T
        return _forward(x, time_maa_x, time_maa, maa_w1, maa_w2, decay_w1, decay_w2, aaa_w1, aaa_w2, kkk_w1, kkk_w2, gate_w1, gate_w2, ma_w1, ma_w2, mk_w1, mk_w2, time_decay, time_faaaa, time_aaaaa, time_misc_a, time_misc_k, Wr, Wk, Wv, Wo, ln_w, ln_b)

    def _L0_ffn_ref(x, Wqkv, q_scale, k_scale, Wo, ln_g, ln_b, W1, b1, W2, b2):
        import jax, jax.numpy as jnp
        import numpy as np
        DIM = 128
        DEPTH = 6
        HEADS = 16
        DIM_HEAD = 64
        WINDOW = 32
        INNER = HEADS * DIM_HEAD
        DIM_INNER = int(DIM * 4 * 2 / 3)
        QK_SCALE = 8.0

        def shift_tokens(t):
            a, s = jnp.split(t, 2, -1)
            s = jnp.pad(s, ((0, 0), (1, 0), (0, 0)))[:, :-1]
            return jnp.concatenate([a, s], -1)

        def l2norm(t):
            return t / jnp.maximum(jnp.linalg.norm(t, axis=-1, keepdims=True), 1e-12)

        def rotate_half(x):
            x1, x2 = jnp.split(x, 2, -1)
            return jnp.concatenate([-x2, x1], -1)

        def rotary_tables(n):
            half = jnp.arange(0, DIM_HEAD, 2, dtype=jnp.float32)
            inv_freq = 1.0 / 10000.0 ** (half / DIM_HEAD)
            t = jnp.arange(n, dtype=jnp.float32)
            freqs = t[:, None] * inv_freq[None, :]
            freqs = jnp.concatenate([freqs, freqs], -1)
            base_scale = (half + 0.4 * DIM_HEAD) / (1.4 * DIM_HEAD)
            power = (t - n // 2) / (WINDOW // 2)
            scale = base_scale[None, :] ** power[:, None]
            scale = jnp.concatenate([scale, scale], -1)
            return (freqs, scale)

        def local_attention(q, k, v):
            b, h, n, d = q.shape
            w = WINDOW
            nw = n // w
            bq = q.reshape(b, h, nw, w, d)
            bk = k.reshape(b, h, nw, w, d)
            bv = v.reshape(b, h, nw, w, d)

            def look(t):
                p = jnp.pad(t, ((0, 0), (0, 0), (1, 0), (0, 0), (0, 0)))
                return jnp.concatenate([p[:, :, :nw], p[:, :, 1:]], axis=3)
            bk2, bv2 = (look(bk), look(bv))
            seq = jnp.arange(n).reshape(nw, w)
            seq_p = jnp.pad(seq, ((1, 0), (0, 0)), constant_values=-1)
            jt = jnp.concatenate([seq_p[:nw], seq_p[1:]], axis=1)
            it = seq[:, :, None]
            jb = jt[:, None, :]
            mask = (it < jb) | (it > jb + w) | (jb == -1)
            sim = jnp.einsum('bhwie,bhwje->bhwij', bq, bk2) * QK_SCALE
            sim = jnp.where(mask, -jnp.finfo(sim.dtype).max, sim)
            attn = jax.nn.softmax(sim, -1)
            out = jnp.einsum('bhwij,bhwje->bhwie', attn, bv2)
            return out.reshape(b, h, n, d)

        def attn_layer(x, Wqkv, qs, ksc, Wo):
            b, n, _ = x.shape
            qkv = x @ Wqkv
            q, k, v = jnp.split(qkv, 3, -1)
            sh = lambda t: t.reshape(b, n, HEADS, DIM_HEAD).transpose(0, 2, 1, 3)
            q, k, v = (sh(q), sh(k), sh(v))
            q = l2norm(q) * qs
            k = l2norm(k) * ksc
            freqs, scale = rotary_tables(n)
            cos, sin = (jnp.cos(freqs), jnp.sin(freqs))
            q = q * cos * scale + rotate_half(q) * sin * scale
            inv = 1.0 / scale
            k = k * cos * inv + rotate_half(k) * sin * inv
            out = local_attention(q, k, v)
            out = out.transpose(0, 2, 1, 3).reshape(b, n, INNER)
            return out @ Wo

        def ffn_layer(x, g, bln, W1, b1, W2, b2):
            mu = x.mean(-1, keepdims=True)
            var = ((x - mu) ** 2).mean(-1, keepdims=True)
            xn = (x - mu) / jnp.sqrt(var + 1e-05) * g + bln
            hg = xn @ W1 + b1
            a, gate = jnp.split(hg, 2, -1)
            return a * jax.nn.gelu(gate, approximate=False) @ W2 + b2
        for i in range(DEPTH):
            x = attn_layer(shift_tokens(x), Wqkv[i], q_scale[i], k_scale[i], Wo[i]) + x
            x = ffn_layer(shift_tokens(x), ln_g[i], ln_b[i], W1[i], b1[i], W2[i], b2[i]) + x
        return x
    x = L0_attn_x
    x = _layernorm(x + _L0_attn_ref(x, L0_attn_time_maa_x, L0_attn_time_maa, L0_attn_maa_w1, L0_attn_maa_w2, L0_attn_decay_w1, L0_attn_decay_w2, L0_attn_aaa_w1, L0_attn_aaa_w2, L0_attn_kkk_w1, L0_attn_kkk_w2, L0_attn_gate_w1, L0_attn_gate_w2, L0_attn_ma_w1, L0_attn_ma_w2, L0_attn_mk_w1, L0_attn_mk_w2, L0_attn_time_decay, L0_attn_time_faaaa, L0_attn_time_aaaaa, L0_attn_time_misc_a, L0_attn_time_misc_k, L0_attn_Wr, L0_attn_Wk, L0_attn_Wv, L0_attn_Wo, L0_attn_ln_w, L0_attn_ln_b), axis=-1)
    x = _layernorm(x + _L0_ffn_ref(x, L0_ffn_Wqkv, L0_ffn_q_scale, L0_ffn_k_scale, L0_ffn_Wo, L0_ffn_ln_g, L0_ffn_ln_b, L0_ffn_W1, L0_ffn_b1, L0_ffn_W2, L0_ffn_b2), axis=-1)
    return x

_drawn_inputs = setup_inputs


def setup_inputs(seed=0):
    import zlib

    import numpy as np

    out = dict(_drawn_inputs(seed))
    spreads = {'L0_attn_ln_w': (1.0, 0.6),
     'L0_attn_ln_b': (0.0, 2.0),
     'L0_ffn_q_scale': (1.0, 0.6),
     'L0_ffn_k_scale': (1.0, 0.6),
     'L0_ffn_ln_g': (1.0, 0.6),
     'L0_ffn_ln_b': (0.0, 0.8),
     'L0_ffn_b1': (0.0, 0.8),
     'L0_ffn_b2': (0.0, 0.1)}
    factors = {'L0_attn_time_maa_x': 8.0,
     'L0_attn_time_maa': 7.903,
     'L0_attn_maa_w1': 8.0,
     'L0_attn_maa_w2': 8.0,
     'L0_attn_decay_w1': 26.143,
     'L0_attn_decay_w2': 26.29,
     'L0_attn_aaa_w1': 8.0,
     'L0_attn_aaa_w2': 8.0,
     'L0_attn_kkk_w1': 49.213,
     'L0_attn_kkk_w2': 49.735,
     'L0_attn_gate_w1': 5.973,
     'L0_attn_gate_w2': 6.015,
     'L0_attn_ma_w1': 8.0,
     'L0_attn_ma_w2': 8.0,
     'L0_attn_mk_w1': 8.0,
     'L0_attn_mk_w2': 8.0,
     'L0_attn_time_decay': 8.0,
     'L0_attn_time_faaaa': 8.0,
     'L0_attn_time_aaaaa': 25.483,
     'L0_attn_time_misc_a': 22.786,
     'L0_attn_time_misc_k': 8.0,
     'L0_attn_Wr': 6.708,
     'L0_attn_Wk': 6.732,
     'L0_attn_Wv': 6.708,
     'L0_attn_Wo': 5.989,
     'L0_ffn_W1': 3.674,
     'L0_ffn_W2': 3.607}
    for name, (base, spread) in spreads.items():
        noise = np.random.default_rng([zlib.crc32(name.encode()), seed]).standard_normal(out[name].shape)
        drawn = base * np.exp(spread * noise) if base else spread * noise
        out[name] = jnp.asarray(drawn.astype(out[name].dtype))
    for name, factor in factors.items():
        out[name] = (out[name] * factor).astype(out[name].dtype)
    return out
```

```python
from contextlib import ExitStack

import numpy as np

import concourse.bass as bass
from concourse import mybir
from concourse.bass import ds

F32 = mybir.dt.float32
BF16 = mybir.dt.bfloat16
ALU = mybir.AluOpType
ACT = mybir.ActivationFunctionType
AX = mybir.AxisListType.X

P = 128
B, T, C = 2, 1024, 128
N = B * T
HEADS, HS = 16, 8
GROUP = 512
GROUPS = N // GROUP
CHUNK = 32
CHUNKS = N // CHUNK
SEQ_CHUNKS = T // CHUNK
Y_EPS, NORM_FLOOR, LN_EPS = 0.00064, 1e-12, 1e-5

DEPTH, DH, WINDOW = 6, 64, 32
AH = 16
INNER = AH * DH
PAIRS = AH // 2
FF = int(C * 4 * 2 / 3)
FF_PARTS = [(at, min(P, FF - at)) for at in range(0, FF, P)]
BLOCKS = N // P
SEQ_BLOCKS = T // P
WINDOWS = P // WINDOW
QK_SCALE = 8.0
MASKED = -1e30
STREAM = DEPTH * BLOCKS


class Signal:

    def __init__(self, signals, name, per=1, credit=0):
        self.sem, self.per, self.credit = signals.semaphore(name), per, credit

    def after(self, turn, part=None):
        return (turn + self.credit) * self.per + (self.per if part is None else part)


class PhaseSignals(ExitStack):

    def __init__(self, nc):
        super().__init__()
        self.nc, self.sems = nc, []

    def semaphore(self, name):
        self.sems.append(self.enter_context(self.nc.semaphore(name)))
        return self.sems[-1]

    def carrier(self, engine, name):
        sem = self.semaphore(name)
        return lambda: engine.sem_inc(sem, 1)

    def __exit__(self, *raised):
        if raised[0] is None:
            with self.nc.Block() as block:
                @block.sync
                def _(sp):
                    for sem in self.sems:
                        sp.sem_clear(sem)
        return super().__exit__(*raised)


def mix_inputs(sb):
    t = {}
    for name, shape in (("xT", (P, N)), ("vecs", (P, 16)), ("ident", (P, P)), ("w_lo", (P, P)), ("w_maa", (P, P)),
                        ("w_r", (P, P)), ("w_g1", (P, P)), ("w_g2", (P, P)), ("w_xwa", (P, P)), ("w_k", (P, P)),
                        ("w_xk", (P, 64)), ("w_v", (P, P)), ("w_second", (P, P)), ("w_xk2", (64, P)),
                        ("w_o", (P, P)), ("headones", (P, P)), ("spread", (P, HS * P)), ("collect", (P, HS * P)),
                        ("headmask", (P, HEADS)), ("rowmask", (P, HS))):
        t[name] = sb(name, shape)
    return t


V_MAAX, V_MAA, V_DECAY, V_AAAAA, V_MISCA, V_MISCK, V_FAAAA, V_LNW, V_LNB, V_ONE, V_YEPS, V_LNEPS = \
    0, 1, 5, 6, 7, 8, 9, 10, 11, 12, 13, 14
AAA_AT, MA_AT = 64, 96
MK_AT = 32


def build_projections(nc, a, t, loads, banks):
    with PhaseSignals(nc) as sems, ExitStack() as ctx:
        def sig(name, **kw):
            return Signal(sems, name, **kw)

        xx, mix, lo, gt, h1, h2 = (ctx.enter_context(nc.sbuf_tensor(n, [P, N], F32))
                                   for n in ("xx", "mix", "lo", "gt", "h1", "h2"))
        xm = [ctx.enter_context(nc.sbuf_tensor(f"xm{g}", [P, N], F32)) for g in range(4)]
        xT, vecs = t["xT"], t["vecs"]
        loaded = sig("p_loaded")
        loaded_x = sig("p_loaded_x")
        xx_made, mix_made, lo_made, gt_made = sig("xx_made"), sig("mix_made"), sig("lo_made"), sig("gt_made")
        h1_made, h2_made, k_made = sig("h1_made", per=2), sig("h2_made", per=2), sig("k_made")
        xm_scaled = [sig(f"xm_scaled{g}") for g in range(4)]
        xm_made = [sig(f"xm_made{g}") for g in range(4)]
        r_made, v_made, g_made, z_made = sig("r_made"), sig("v_made"), sig("g_made"), sig("z_made", per=2)
        a_made, ma_made, mk_made, kk_made = sig("a_made"), sig("ma_made"), sig("mk_made"), sig("kk_made")

        products = [("lo", t["w_lo"], mix, (0, P), mix_made, lo_made)]
        products += [(f"maa{g}", t["w_maa"], lo, (32 * g, 32 * g + 32), lo_made, xm_scaled[g]) for g in range(4)]
        products += [("r", t["w_r"], xm[0], (0, P), xm_made[0], r_made),
                     ("g1", t["w_g1"], xm[0], (0, P), xm_made[0], gt_made),
                     ("xwa", t["w_xwa"], xm[1], (0, P), xm_made[1], h1_made),
                     ("k", t["w_k"], xm[2], (0, P), xm_made[2], k_made),
                     ("xk", t["w_xk"], xm[2], (0, P), xm_made[2], h2_made),
                     ("v", t["w_v"], xm[3], (0, P), xm_made[3], v_made),
                     ("g2", t["w_g2"], gt, (0, P), gt_made, g_made),
                     ("z", t["w_second"], h1, (0, 64), h1_made, z_made),
                     ("a", t["w_second"], h1, (AAA_AT, AAA_AT + 16), h1_made, a_made),
                     ("ma", t["w_second"], h1, (MA_AT, MA_AT + 16), h1_made, ma_made),
                     ("kk", t["w_xk2"], h2, (0, 16), h2_made, kk_made),
                     ("mk", t["w_xk2"], h2, (MK_AT, MK_AT + 16), h2_made, mk_made)]
        done = {p[0]: sig(f"{p[0]}_product") for p in products}
        at = {p[0]: 4 * i for i, p in enumerate(products)}
        g_of = [slice(GROUP * j, GROUP * (j + 1)) for j in range(GROUPS)]

        def bank(name, j):
            return banks[(at[name] + j) % 8]

        block = ctx.enter_context(nc.Block())
        small = [n for n in loads if n != "xT"]

        @block.sync
        def _(sp):
            sp.dma_start(t["vecs"][:, :], a["vecs"]).then_inc(loaded.sem, 16)
            sp.dma_start(xT[:, :], a["xT"]).then_inc(loaded_x.sem, 16)
            for name in small:
                if name != "vecs":
                    sp.dma_start(t[name][:, :], a[name]).then_inc(loaded.sem, 16)

        @block.tensor
        def _(pe):
            pe.wait_ge(loaded.sem, 16 * len(small))
            for i, (name, w, moving, (r0, r1), ready, _free) in enumerate(products):
                m = w.shape[1]
                for j in range(GROUPS):
                    pe.wait_ge(ready.sem, ready.after(j))
                    if i >= 2:
                        freed = products[i - 2][5]
                        pe.wait_ge(freed.sem, freed.after(j))
                    nc.tensor.matmul(bank(name, j)[0:m, :], w[r0:r1, :], moving[r0:r1, g_of[j]],
                                     start=True, stop=True).then_inc(done[name].sem, 1)

        @block.vector
        def _(dve):
            dve.wait_ge(loaded_x.sem, 16)
            dve.wait_ge(loaded.sem, 16 * len(small))
            for s in range(B):
                lo_, hi = s * T, (s + 1) * T
                nc.vector.tensor_scalar(xx[:, lo_:lo_ + 1], xT[:, lo_:lo_ + 1], -1.0, None, ALU.mult).then_inc(xx_made.sem, 1)
                nc.vector.tensor_tensor(xx[:, lo_ + 1:hi], xT[:, lo_:hi - 1], xT[:, lo_ + 1:hi],
                                        ALU.subtract).then_inc(xx_made.sem, 1)
            dve.wait_ge(xx_made.sem, 2 * B)
            for j in range(GROUPS):
                nc.vector.scalar_tensor_tensor(out=mix[:, g_of[j]], in0=xx[:, g_of[j]], scalar=vecs[:, V_MAAX:V_MAAX + 1],
                                               in1=xT[:, g_of[j]], op0=ALU.mult, op1=ALU.add).then_inc(mix_made.sem, 1)
            for g in range(4):
                for j in range(GROUPS):
                    dve.wait_ge(done[f"maa{g}"].sem, j + 1)
                    nc.vector.scalar_tensor_tensor(out=xm[g][:, g_of[j]], in0=bank(f"maa{g}", j)[:, :],
                                                   scalar=vecs[:, V_MAA + g:V_MAA + g + 1], in1=xx[:, g_of[j]],
                                                   op0=ALU.add, op1=ALU.mult).then_inc(xm_scaled[g].sem, 1)
            for j in range(GROUPS):
                dve.wait_ge(done["kk"].sem, j + 1)
                dve.wait_ge(k_made.sem, k_made.after(j))
                nc.vector.tensor_tensor(t["kkraw"][:, g_of[j]], bank("kk", j)[:, :], t["k"][:, g_of[j]],
                                        ALU.add).then_inc(kk_made.sem, 1)

        @block.gpsimd
        def _(pool):
            for g in range(4):
                for j in range(GROUPS):
                    pool.wait_ge(xm_scaled[g].sem, j + 1)
                    nc.gpsimd.tensor_tensor(out=xm[g][:, g_of[j]], in0=xm[g][:, g_of[j]], in1=xT[:, g_of[j]],
                                            op=ALU.add).then_inc(xm_made[g].sem, 1)

        @block.scalar
        def _(act):
            act.wait_ge(loaded.sem, 16 * len(small))

            def read_out(name, out, func, made, rows=(0, P), bias=None):
                r0, r1 = rows
                for j in range(GROUPS):
                    act.wait_ge(done[name].sem, j + 1)
                    b = 0.0 if bias is None else vecs[r0:r1, bias:bias + 1]
                    nc.scalar.activation(out[r0:r1, g_of[j]], bank(name, j)[r0:r1, :], func, bias=b).then_inc(made.sem, 1)

            read_out("lo", lo, ACT.Tanh, lo_made)
            read_out("r", t["r"], ACT.Copy, r_made)
            read_out("g1", gt, ACT.Tanh, gt_made)
            for j in range(GROUPS):
                act.wait_ge(done["xwa"].sem, j + 1)
                nc.scalar.activation(h1[0:64, g_of[j]], bank("xwa", j)[0:64, :], ACT.Tanh).then_inc(h1_made.sem, 1)
                nc.scalar.activation(h1[64:P, g_of[j]], bank("xwa", j)[64:P, :], ACT.Copy).then_inc(h1_made.sem, 1)
            read_out("k", t["k"], ACT.Copy, k_made)
            for j in range(GROUPS):
                act.wait_ge(done["xk"].sem, j + 1)
                nc.scalar.activation(h2[0:32, g_of[j]], bank("xk", j)[0:32, :], ACT.Tanh).then_inc(h2_made.sem, 1)
                nc.scalar.activation(h2[32:64, g_of[j]], bank("xk", j)[32:64, :], ACT.Copy).then_inc(h2_made.sem, 1)
            read_out("v", t["v"], ACT.Copy, v_made)
            read_out("g2", t["g"], ACT.Copy, g_made)
            for j in range(GROUPS):
                act.wait_ge(done["z"].sem, j + 1)
                nc.scalar.activation(t["z"][:, g_of[j]], bank("z", j)[:, :], ACT.Identity,
                                     bias=vecs[:, V_DECAY:V_DECAY + 1]).then_inc(z_made.sem, 1)
                nc.scalar.activation(t["w"][:, g_of[j]], bank("z", j)[:, :], ACT.Sigmoid,
                                     bias=vecs[:, V_DECAY:V_DECAY + 1]).then_inc(z_made.sem, 1)
            read_out("a", t["a"], ACT.Sigmoid, a_made, bias=V_AAAAA)
            read_out("ma", t["ma"], ACT.Sigmoid, ma_made, bias=V_MISCA)
            read_out("mk", t["mk"], ACT.Sigmoid, mk_made, bias=V_MISCK)


def build_gates(nc, t, banks, vk):
    with PhaseSignals(nc) as sems, ExitStack() as ctx:
        def sig(name, **kw):
            return Signal(sems, name, **kw)

        vecs = t["vecs"]
        e, sp_ = (ctx.enter_context(nc.sbuf_tensor(n, [P, N], F32)) for n in ("gate_e", "gate_sp"))
        sq, norm = e, sp_
        squared, ss_product, root_made, decay_made = sig("kk_squared"), sig("ss_product"), sig("root_made"), sig("decay_made")
        kk_norm, soft, act_step = sig("kk_norm"), sig("soft"), sig("act_step")
        gain_made, k_scaled, key_gain = sig("gain_made"), sig("k_scaled"), sig("key_gain")
        v_spread, vk_made = sig("v_spread"), sig("vk_made")
        block = ctx.enter_context(nc.Block())
        g_of = [slice(GROUP * j, GROUP * (j + 1)) for j in range(GROUPS)]

        @block.scalar
        def _(act):
            nc.scalar.activation(sq[:, :], t["kkraw"][:, :], ACT.Square).then_inc(squared.sem, 1)
            for j in range(GROUPS):
                act.wait_ge(ss_product.sem, j + 1)
                nc.scalar.activation(norm[:, g_of[j]], banks[j][:, :], ACT.Sqrt).then_inc(root_made.sem, 1)
            nc.scalar.activation(t["w"][:, :], t["w"][:, :], ACT.Exp, scale=-float(np.exp(-0.5))).then_inc(decay_made.sem, 1)
            nc.scalar.activation(e[:, :], t["z"][:, :], ACT.Abs).then_inc(act_step.sem, 1)
            act.wait_ge(act_step.sem, 1)
            nc.scalar.activation(e[:, :], e[:, :], ACT.Exp, scale=-1.0).then_inc(act_step.sem, 1)
            act.wait_ge(act_step.sem, 2)
            nc.scalar.activation(e[:, :], e[:, :], ACT.Ln, bias=vecs[:, V_ONE:V_ONE + 1]).then_inc(act_step.sem, 1)
            act.wait_ge(soft.sem, 3)
            nc.scalar.activation(e[:, :], e[:, :], ACT.Exp, scale=-1.0).then_inc(key_gain.sem, 1)

        @block.tensor
        def _(pe):
            pe.wait_ge(squared.sem, 1)
            for j in range(GROUPS):
                nc.tensor.matmul(banks[j][:, :], t["headones"][:, :], sq[:, g_of[j]], start=True, stop=True).then_inc(ss_product.sem, 1)
            for i in range(HS):
                for j in range(GROUPS):
                    n = i * GROUPS + j
                    if n >= 4:
                        pe.wait_ge(vk_made.sem, n - 3)
                    nc.tensor.matmul(banks[4 + n % 4][:, :], t["spread"][:, P * i:P * (i + 1)], t["v"][:, g_of[j]],
                                     start=True, stop=True).then_inc(v_spread.sem, 1)

        @block.vector
        def _(dve):
            nc.vector.tensor_scalar(vk[:, 0:N], t["a"][:, :], -1.0, 1.0, ALU.mult, ALU.add).then_inc(gain_made.sem, 1)
            dve.wait_ge(gain_made.sem, 1)
            nc.vector.tensor_tensor(vk[:, 0:N], vk[:, 0:N], t["ma"][:, :], ALU.mult).then_inc(gain_made.sem, 1)
            dve.wait_ge(gain_made.sem, 2)
            nc.vector.tensor_tensor(vk[:, 0:N], vk[:, 0:N], t["a"][:, :], ALU.add).then_inc(gain_made.sem, 1)
            dve.wait_ge(gain_made.sem, 3)
            nc.vector.tensor_tensor(t["k"][:, :], t["k"][:, :], vk[:, 0:N], ALU.mult).then_inc(k_scaled.sem, 1)
            dve.wait_ge(root_made.sem, GROUPS)
            nc.vector.tensor_scalar(norm[:, :], norm[:, :], NORM_FLOOR, None, ALU.max).then_inc(kk_norm.sem, 1)
            dve.wait_ge(kk_norm.sem, 1)
            nc.vector.reciprocal(norm[:, :], norm[:, :]).then_inc(kk_norm.sem, 1)
            dve.wait_ge(kk_norm.sem, 2)
            nc.vector.tensor_tensor(t["kkraw"][:, :], t["kkraw"][:, :], norm[:, :], ALU.mult).then_inc(kk_norm.sem, 1)
            dve.wait_ge(kk_norm.sem, 3)
            nc.vector.scalar_tensor_tensor(out=t["b"][:, :], in0=t["kkraw"][:, :], scalar=-1.0, in1=t["a"][:, :],
                                           op0=ALU.mult, op1=ALU.mult).then_inc(kk_norm.sem, 1)
            dve.wait_ge(act_step.sem, 3)
            nc.vector.tensor_scalar(t["z"][:, :], t["z"][:, :], -1.0, 0.0, ALU.mult, ALU.max).then_inc(soft.sem, 1)
            dve.wait_ge(soft.sem, 1)
            nc.vector.tensor_tensor(e[:, :], e[:, :], t["z"][:, :], ALU.add).then_inc(soft.sem, 1)
            dve.wait_ge(soft.sem, 2)
            nc.vector.scalar_tensor_tensor(out=e[:, :], in0=e[:, :], scalar=0.5, in1=t["mk"][:, :],
                                           op0=ALU.add, op1=ALU.mult).then_inc(soft.sem, 1)
            dve.wait_ge(key_gain.sem, 1)
            dve.wait_ge(k_scaled.sem, 1)
            nc.vector.tensor_tensor(t["k"][:, :], t["k"][:, :], e[:, :], ALU.mult).then_inc(k_scaled.sem, 1)
            dve.wait_ge(k_scaled.sem, 2)
            per = GROUP // CHUNK
            view = vk[:, :].rearrange("p (l i c) -> p l i c", i=HS, c=CHUNKS)
            for i in range(HS):
                for j in range(GROUPS):
                    n = i * GROUPS + j
                    dve.wait_ge(v_spread.sem, n + 1)
                    nc.vector.tensor_tensor(view[:, :, i, per * j:per * (j + 1)],
                                            banks[4 + n % 4][:, :].rearrange("p (c l) -> p l c", l=CHUNK),
                                            t["k"][:, g_of[j]].rearrange("p (c l) -> p l c", l=CHUNK),
                                            ALU.mult).then_inc(vk_made.sem, 1)


def build_scan(nc, t, banks, vk, state):
    with PhaseSignals(nc) as sems, ExitStack() as ctx:
        def sig(name, **kw):
            return Signal(sems, name, **kw)

        W = HS * CHUNKS
        m, sw, m2, ub = (ctx.enter_context(nc.sbuf_tensor(n, [P, 2, W], F32)) for n in ("sc_m", "sc_sw", "sc_m2", "sc_ub"))
        s_set = sig("s_set", per=2)
        s_new = [sig(f"s_new{p}", credit=1) for p in range(2)]
        s_kk = [sig(f"s_kk{p}", credit=1) for p in range(2)]
        u_product = [sig(f"u_product{p}", credit=1) for p in range(2)]
        ub_made = [sig(f"ub_made{p}", credit=1) for p in range(2)]
        decayed = [sig(f"decayed{p}", credit=1) for p in range(2)]
        s_sum = sig("s_sum")
        s_r = [sig(f"s_r{p}", credit=1) for p in range(2)]
        y_product = [sig(f"y_product{p}", credit=1) for p in range(2)]
        y_read = [sig(f"y_read{p}", credit=1) for p in range(2)]
        set_rows = sig("set_rows")
        block = ctx.enter_context(nc.Block())

        def step(name, l):
            v = t[name][:, :].rearrange("p (c l) -> p l c", l=CHUNK)[:, ds(l, 1), :]
            return v.to_broadcast([P, HS, CHUNKS])

        def rows(buf, p):
            return buf[:, p, :].rearrange("p (r c) -> p r c", c=CHUNKS)

        y_of = (t["y"], t["zy"])

        @block.vector
        def _(dve):
            nc.vector.memset(state[:, 0, :], 0.0).then_inc(s_set.sem, 1)
            nc.vector.tensor_copy(rows(state, 1), t["rowmask"][:, :].unsqueeze(2).to_broadcast([P, HS, CHUNKS])).then_inc(s_set.sem, 1)
            dve.wait_ge(s_set.sem, 2)
            for p in range(2):
                for s in (s_new[p], s_kk[p], ub_made[p]):
                    nc.vector.engine_nop().then_inc(s.sem, 1)
            with dve.Fori(0, CHUNK) as l:
                for p in range(2):
                    dve.wait_ge(s_new[p].sem, s_new[p].after(l - 1))
                    dve.wait_ge(u_product[p].sem, u_product[p].after(l - 1))
                    nc.vector.tensor_tensor(rows(m, p), rows(state, p), step("kkraw", l), ALU.mult).then_inc(s_kk[p].sem, 1)
                for p in range(2):
                    dve.wait_ge(u_product[p].sem, u_product[p].after(l))
                    nc.vector.tensor_tensor(rows(ub, p), banks[p][:, :].rearrange("p (r c) -> p r c", c=CHUNKS),
                                            step("b", l), ALU.mult).then_inc(ub_made[p].sem, 1)
                    if p == 0:
                        dve.wait_ge(ub_made[p].sem, ub_made[p].after(l))
                        nc.vector.tensor_tensor(ub[:, p, :], ub[:, p, :], vk[:, ds(l * W, W)], ALU.add).then_inc(s_sum.sem, 1)
                        dve.wait_ge(s_sum.sem, s_sum.after(l))
                    else:
                        dve.wait_ge(ub_made[p].sem, ub_made[p].after(l))
                    dve.wait_ge(decayed[p].sem, decayed[p].after(l - 1))
                    dve.wait_ge(s_r[p].sem, s_r[p].after(l - 1))
                    nc.vector.tensor_tensor(state[:, p, :], sw[:, p, :], ub[:, p, :], ALU.add).then_inc(s_new[p].sem, 1)

        @block.gpsimd
        def _(pool):
            for p in range(2):
                nc.gpsimd.engine_nop().then_inc(s_r[p].sem, 1)
            carry = sems.carrier(pool, "pool_carried")
            pool.wait_ge(s_set.sem, 2)
            for p in range(2):
                nc.gpsimd.tensor_tensor(out=rows(sw, p), in0=rows(state, p), in1=step("w", 0), op=ALU.mult).then_inc(decayed[p].sem, 1)
            with pool.Fori(0, CHUNK) as l:
                for p in range(2):
                    pool.wait_ge(s_new[p].sem, s_new[p].after(l))
                    carry()
                    nc.gpsimd.tensor_tensor(out=rows(sw, p), in0=rows(state, p), in1=step("w", (l + 1) % CHUNK),
                                            op=ALU.mult).then_inc(decayed[p].sem, 1)
                    pool.wait_ge(y_product[p].sem, y_product[p].after(l - 1))
                    carry()
                    nc.gpsimd.tensor_tensor(out=rows(m2, p), in0=rows(state, p), in1=step("r", l),
                                            op=ALU.mult).then_inc(s_r[p].sem, 1)

        @block.tensor
        def _(pe):
            for p in range(2):
                nc.tensor.drain().then_inc(u_product[p].sem, 1)
                nc.tensor.drain().then_inc(y_product[p].sem, 1)
            with pe.Fori(0, CHUNK) as l:
                for p in range(2):
                    pe.wait_ge(s_kk[p].sem, s_kk[p].after(l))
                    pe.wait_ge(ub_made[p].sem, ub_made[p].after(l - 1))
                    nc.tensor.matmul(banks[p][:, :], t["headones"][:, :], m[:, p, :], start=True, stop=True).then_inc(u_product[p].sem, 1)
                for p in range(2):
                    pe.wait_ge(s_r[p].sem, s_r[p].after(l))
                    pe.wait_ge(y_read[p].sem, y_read[p].after(l - 1))
                    for i in range(HS):
                        last = nc.tensor.matmul(banks[2 + p][:, 0:CHUNKS], t["collect"][:, P * i:P * (i + 1)],
                                                m2[:, p, CHUNKS * i:CHUNKS * (i + 1)], start=(i == 0), stop=(i == HS - 1))
                    last.then_inc(y_product[p].sem, 1)

        @block.scalar
        def _(act):
            for p in range(2):
                nc.scalar.drain().then_inc(y_read[p].sem, 1)
            with act.Fori(0, CHUNK) as l:
                for p in range(2):
                    act.wait_ge(y_product[p].sem, y_product[p].after(l))
                    out = y_of[p][:, :].rearrange("p (c l) -> p l c", l=CHUNK)[:, ds(l, 1), :]
                    nc.scalar.activation(out, banks[2 + p][:, 0:CHUNKS].unsqueeze(1), ACT.Copy).then_inc(y_read[p].sem, 1)


def build_mix_output(nc, a, t, banks, state, x_mid, x_all):
    with PhaseSignals(nc) as sems, ExitStack() as ctx:
        def sig(name, **kw):
            return Signal(sems, name, **kw)

        vecs, y = t["vecs"], t["y"]
        spreadG, prop = (ctx.enter_context(nc.sbuf_tensor(n, [P, CHUNKS, P], F32)) for n in ("spreadG", "prop"))
        start = ctx.enter_context(nc.sbuf_tensor("start", [P, CHUNKS, HS], F32))
        stats = ctx.enter_context(nc.sbuf_tensor("ln_stats", [P, BLOCKS, 6], F32))
        mv = ctx.enter_context(nc.sbuf_tensor("ln_mv", [P, BLOCKS, 2], F32))
        x_tok = ctx.enter_context(nc.sbuf_tensor("x_tok_sb", [P, BLOCKS, C], F32))
        yc, ysq, bonus = t["z"], t["w"], t["kkraw"]
        EIGHT = 8
        expanded, turned, prop_read = sig("expanded"), sig("turned"), sig("prop_read")
        start_set, chain_product, started = sig("start_set"), sig("chain_product"), sig("started")
        s_expanded, y_part, y_full = sig("s_expanded"), sig("y_part"), sig("y_full")
        mean_product, centred, y_squared, var_product, y_root = (sig(n) for n in ("mean_product", "centred", "y_squared", "var_product", "y_root"))
        y_recip, y_step, rk_made, rk_product = sig("y_recip"), sig("y_step"), sig("rk_made"), sig("rk_product")
        bonus_made, gated, o_product, summed = sig("bonus_made"), sig("gated"), sig("o_product"), sig("summed")
        stat_step, ln_root, ln_recip, normed, copied, x_loaded = (sig(n) for n in ("stat_step", "ln_root", "ln_recip", "normed", "copied", "x_loaded"))
        g_of = [slice(GROUP * j, GROUP * (j + 1)) for j in range(GROUPS)]
        hm = t["headmask"][:, :].unsqueeze(1).unsqueeze(3).to_broadcast([P, EIGHT, HEADS, HS])
        block = ctx.enter_context(nc.Block())

        @block.sync
        def _(sp):
            sp.dma_start(x_tok[:, :, :], a["x_tok"]).then_inc(x_loaded.sem, 16)

        @block.gpsimd
        def _(pool):
            nc.gpsimd.tensor_tensor(out=bonus[:, :], in0=t["r"][:, :], in1=t["k"][:, :], op=ALU.mult).then_inc(rk_made.sem, 1)
            pool.wait_ge(rk_made.sem, 1)
            nc.gpsimd.tensor_scalar(bonus[:, :], bonus[:, :], vecs[:, V_FAAAA:V_FAAAA + 1], None, ALU.mult).then_inc(rk_made.sem, 1)
            for n in range(BLOCKS):
                pool.wait_ge(normed.sem, n + 1)
                nc.gpsimd.tensor_copy(x_all[:, n, :], x_mid[:, n, :]).then_inc(copied.sem, 1)

        @block.vector
        def _(dve):
            G = state[:, 1, :].rearrange("p (r c) -> p c r", c=CHUNKS)
            for e in range(CHUNKS // EIGHT):
                cs = slice(EIGHT * e, EIGHT * (e + 1))
                nc.vector.tensor_tensor(spreadG[:, cs, :].rearrange("p c (h r) -> p c h r", h=HEADS),
                                        G[:, cs, :].unsqueeze(2).to_broadcast([P, EIGHT, HEADS, HS]), hm,
                                        ALU.mult).then_inc(expanded.sem, 1)
            for s in range(B):
                nc.vector.memset(start[:, s * SEQ_CHUNKS, :], 0.0).then_inc(start_set.sem, 1)
            H = state[:, 0, :].rearrange("p (r c) -> p c r", c=CHUNKS)
            for n in range(SEQ_CHUNKS - 1):
                for s in range(B):
                    c = s * SEQ_CHUNKS + n
                    dve.wait_ge(chain_product.sem, B * n + s + 1)
                    nc.vector.tensor_tensor(start[:, c + 1, :], banks[6 + s][:, 0:HS], H[:, c, :], ALU.add).then_inc(started.sem, 1)
            dve.wait_ge(start_set.sem, B)
            dve.wait_ge(started.sem, B * (SEQ_CHUNKS - 1))
            dve.wait_ge(turned.sem, CHUNKS)
            for e in range(CHUNKS // EIGHT):
                cs = slice(EIGHT * e, EIGHT * (e + 1))
                nc.vector.tensor_tensor(spreadG[:, cs, :].rearrange("p c (h r) -> p c h r", h=HEADS),
                                        start[:, cs, :].unsqueeze(2).to_broadcast([P, EIGHT, HEADS, HS]), hm,
                                        ALU.mult).then_inc(s_expanded.sem, 1)
            for j in range(GROUPS):
                dve.wait_ge(y_part.sem, j + 1)
                nc.vector.tensor_tensor(y[:, g_of[j]], banks[j][:, :], y[:, g_of[j]], ALU.add).then_inc(y_full.sem, 1)
            for j in range(GROUPS):
                dve.wait_ge(mean_product.sem, j + 1)
                dve.wait_ge(y_full.sem, j + 1)
                nc.vector.scalar_tensor_tensor(out=yc[:, g_of[j]], in0=banks[4 + j % 2][:, :], scalar=-1.0 / HS,
                                               in1=y[:, g_of[j]], op0=ALU.mult, op1=ALU.add).then_inc(centred.sem, 1)
            for j in range(GROUPS):
                dve.wait_ge(rk_product.sem, j + 1)
                nc.vector.tensor_tensor(bonus[:, g_of[j]], banks[4 + j % 2][:, :], t["v"][:, g_of[j]],
                                        ALU.mult).then_inc(bonus_made.sem, 1)
            dve.wait_ge(y_root.sem, GROUPS)
            nc.vector.reciprocal(ysq[:, :], ysq[:, :]).then_inc(y_recip.sem, 1)
            dve.wait_ge(y_recip.sem, 1)
            nc.vector.tensor_tensor(yc[:, :], yc[:, :], ysq[:, :], ALU.mult).then_inc(y_step.sem, 1)
            dve.wait_ge(y_step.sem, 1)
            nc.vector.tensor_scalar(yc[:, :], yc[:, :], vecs[:, V_LNW:V_LNW + 1], vecs[:, V_LNB:V_LNB + 1],
                                    ALU.mult, ALU.add).then_inc(y_step.sem, 1)
            dve.wait_ge(y_step.sem, 2)
            dve.wait_ge(bonus_made.sem, GROUPS)
            nc.vector.tensor_tensor(yc[:, :], yc[:, :], bonus[:, :], ALU.add).then_inc(y_step.sem, 1)
            dve.wait_ge(y_step.sem, 3)
            nc.vector.tensor_tensor(yc[:, :], yc[:, :], t["g"][:, :], ALU.mult).then_inc(gated.sem, 1)
            dve.wait_ge(x_loaded.sem, 16)
            for n in range(BLOCKS):
                dve.wait_ge(o_product.sem, n + 1)
                nc.vector.tensor_tensor(x_tok[:, n, :], banks[n % 4][:, 0:C], x_tok[:, n, :], ALU.add).then_inc(summed.sem, 1)
                dve.wait_ge(summed.sem, n + 1)
                nc.vector.bn_stats(stats[:, n, :], x_tok[:, n, :]).then_inc(stat_step.sem, 1)
                dve.wait_ge(stat_step.sem, 2 * n + 1)
                nc.vector.bn_aggr(mv[:, n, :], stats[:, n, :]).then_inc(stat_step.sem, 1)
            dve.wait_ge(ln_root.sem, 1)
            nc.vector.reciprocal(mv[:, :, 1], mv[:, :, 1]).then_inc(ln_recip.sem, 1)
            dve.wait_ge(ln_recip.sem, 1)
            for n in range(BLOCKS):
                nc.vector.tensor_scalar(x_mid[:, n, :], x_tok[:, n, :], mv[:, n, 0:1], mv[:, n, 1:2],
                                        ALU.subtract, ALU.mult).then_inc(normed.sem, 1)

        @block.tensor
        def _(pe):
            for c in range(CHUNKS):
                pe.wait_ge(expanded.sem, c // EIGHT + 1)
                if c >= 4 and c % 4 == 0 and c >= 16:
                    pe.wait_ge(prop_read.sem, c // 4 - 3)
                nc.tensor.transpose(banks[(c // 4) % 4][:, P * (c % 4):P * (c % 4 + 1)], spreadG[:, c, :], t["ident"][:, :]).then_inc(turned.sem, 1)
            pe.wait_ge(start_set.sem, B)
            pe.wait_ge(prop_read.sem, CHUNKS // 4)
            for n in range(SEQ_CHUNKS - 1):
                for s in range(B):
                    c = s * SEQ_CHUNKS + n
                    if n:
                        pe.wait_ge(started.sem, B * (n - 1) + s + 1)
                    nc.tensor.matmul(banks[6 + s][:, 0:HS], prop[:, c, :], start[:, c, :], start=True, stop=True).then_inc(chain_product.sem, 1)
            for c in range(CHUNKS):
                pe.wait_ge(s_expanded.sem, c // EIGHT + 1)
                at = CHUNK * c
                mm = nc.tensor.matmul(banks[at // GROUP][:, at % GROUP:at % GROUP + CHUNK], spreadG[:, c, :],
                                      t["zy"][:, at:at + CHUNK], start=True, stop=True)
                if (at + CHUNK) % GROUP == 0:
                    mm.then_inc(y_part.sem, 1)
            for j in range(GROUPS):
                pe.wait_ge(y_full.sem, j + 1)
                if j >= 2:
                    pe.wait_ge(centred.sem, j - 1)
                nc.tensor.matmul(banks[4 + j % 2][:, :], t["headones"][:, :], y[:, g_of[j]], start=True, stop=True).then_inc(mean_product.sem, 1)
            for j in range(GROUPS):
                pe.wait_ge(y_squared.sem, j + 1)
                nc.tensor.matmul(banks[j][:, :], t["headones"][:, :], ysq[:, g_of[j]], start=True, stop=True).then_inc(var_product.sem, 1)
            pe.wait_ge(rk_made.sem, 2)
            for j in range(GROUPS):
                pe.wait_ge(centred.sem, j + 3 if j < 2 else GROUPS)
                if j >= 2:
                    pe.wait_ge(bonus_made.sem, j - 1)
                nc.tensor.matmul(banks[4 + j % 2][:, :], t["headones"][:, :], bonus[:, g_of[j]], start=True, stop=True).then_inc(rk_product.sem, 1)
            pe.wait_ge(gated.sem, 1)
            for n in range(BLOCKS):
                if n >= 4:
                    pe.wait_ge(summed.sem, n - 3)
                nc.tensor.matmul(banks[n % 4][:, 0:C], yc[:, P * n:P * (n + 1)], t["w_o"][:, :], start=True, stop=True).then_inc(o_product.sem, 1)

        @block.scalar
        def _(act):
            for q in range(CHUNKS // 4):
                act.wait_ge(turned.sem, 4 * q + 4)
                nc.scalar.activation(prop[:, 4 * q:4 * q + 4, :].rearrange("p c m -> p (c m)"), banks[q % 4][:, :], ACT.Copy).then_inc(prop_read.sem, 1)
            for j in range(GROUPS):
                act.wait_ge(centred.sem, j + 1)
                nc.scalar.activation(ysq[:, g_of[j]], yc[:, g_of[j]], ACT.Square).then_inc(y_squared.sem, 1)
            for j in range(GROUPS):
                act.wait_ge(var_product.sem, j + 1)
                nc.scalar.activation(ysq[:, g_of[j]], banks[j][:, :], ACT.Sqrt, scale=1.0 / HS,
                                     bias=vecs[:, V_YEPS:V_YEPS + 1]).then_inc(y_root.sem, 1)
            act.wait_ge(stat_step.sem, 2 * BLOCKS)
            nc.scalar.activation(mv[:, :, 1], mv[:, :, 1], ACT.Sqrt, bias=vecs[:, V_LNEPS:V_LNEPS + 1]).then_inc(ln_root.sem, 1)


def build_mixing(nc, a, banks, x_mid, x_all):
    with ExitStack() as ctx:
        def sb(name, shape):
            return ctx.enter_context(nc.sbuf_tensor(name + "_sb", list(shape), F32))

        t = mix_inputs(sb)
        loads = list(t)
        for name in ("r", "k", "v", "g", "z", "w", "a", "ma", "mk", "kkraw"):
            t[name] = sb(name, (P, N))
        state = sb("state", (P, 2, HS * CHUNKS))
        build_projections(nc, a, t, loads, banks)
        t["b"], t["y"], t["zy"] = t["ma"], t["a"], t["mk"]
        with nc.sbuf_tensor("vk_sb", [P, CHUNK * HS * CHUNKS], F32) as vk:
            build_gates(nc, t, banks, vk)
            build_scan(nc, t, banks, vk, state)
        build_mix_output(nc, a, t, banks, state, x_mid, x_all)


def build_stream(nc, a, banks, x_all, masks_f):
    with PhaseSignals(nc) as sems, ExitStack() as ctx:
        def sb(name, shape, dt=F32):
            return ctx.enter_context(nc.sbuf_tensor(name, list(shape), dt))

        def sig(name, per=1, credit=2):
            return Signal(sems, name, per, credit)

        def two(name, shape):
            return [sb(f"{name}{u}", shape) for u in range(2)]

        ident, ident16 = sb("st_ident", (P, P)), sb("st_ident16", (P, P), BF16)
        mask16 = sb("mask16", (P, SEQ_BLOCKS, 2 * WINDOW), BF16)
        tables = sb("tables", (P, SEQ_BLOCKS, 4 * DH))
        follows = sb("follows", (P, SEQ_BLOCKS))
        norm_gb = sb("norm_gb", (P, 2 * DEPTH))
        eps = sb("eps", (P, 1))
        wqkv, wo, w1 = sb("wqkv", (P, 2 * 3 * INNER)), sb("wo", (P, 2 * INNER)), sb("w1", (P, 2 * 2 * FF))
        w2, b1, b2 = sb("w2", (P, 2 * len(FF_PARTS) * C)), sb("b1", (P, 2 * 2 * FF)), sb("b2", (P, 2 * C))
        qk_gain = sb("qk_gain", (P, 2 * 4 * DH))
        x_in, xs_T, gains, v_tok = two("x_in", (P, C)), two("xs_T", (P, P)), two("gains", (P, 4, DH)), two("v_tok", (P, INNER))
        edge, edge2 = two("edge", (P, 1)), two("edge2", (P, 1))
        squares, turnedhalf = sb("squares", (P, 2 * INNER)), sb("turnedhalf", (P, 2 * INNER))
        qk, rnorm = two("qk", (P, 2 * INNER)), two("rnorm", (P, 2 * AH))
        q_T, k_T = two("q_T", (P, PAIRS, P)), two("k_T", (P, PAIRS, WINDOW + P))
        v_win = two("v_win", (P, WINDOWS, INNER // 2))
        probs, p_T, o_T = two("probs", (P, PAIRS, 2, DH)), two("p_T", (P, PAIRS, P)), two("o_T", (P, PAIRS, P))
        peak, total = two("peak", (P, 2, PAIRS)), two("total", (P, AH))
        x_att = two("x_att", (P, C))
        ms_T, xn, xn_T, x_res = two("ms_T", (P, P)), two("xn", (P, C)), two("xn_T", (P, P)), two("x_res", (P, C))
        stats, mv = two("st_stats", (P, 6)), two("st_mv", (P, 2))
        gate, act_in = two("gate", (P, FF)), two("act_in", (P, FF))
        ff_T = two("ff_T", (P, len(FF_PARTS), P))

        const_loaded, masks_made = sig("const_loaded", credit=0), sig("masks_made", credit=0)
        LAYER_LOADS = 7
        w_loaded = sig("w_loaded", per=16 * LAYER_LOADS, credit=0)
        cleared = sig("cleared", credit=0)
        x_ready = sig("x_ready", credit=BLOCKS)
        x_taken, gains_made, x_turned, xs_made = sig("x_taken"), sig("gains_made"), sig("x_turned"), sig("xs_made", per=4)
        qk_product, v_product, squared = sig("qk_product", per=4), sig("st_v_product", per=2), sig("squared", per=4)
        rotated, rot_added, ss_made, root_made = sig("rotated", per=12), sig("rot_added", per=2), sig("ss_made"), sig("st_root_made")
        rnorm_made, qk_made, v_read = sig("rnorm_made", per=2), sig("qk_made", per=2), sig("v_read", per=2)
        v_placed = sig("v_placed", per=16 * 16)
        q_turned, qT_made, k_turned, kT_made, halo_made = sig("q_turned", per=2), sig("qT_made", per=2), sig("k_turned", per=2), sig("kT_made", per=2), sig("halo_made")
        s_product, peak_made, shifted, exp_made = sig("s_product"), sig("peak_made", per=2), sig("shifted", per=2), sig("exp_made")
        total_made, p_made, p_turned, pT_made = sig("total_made", per=2), sig("p_made"), sig("p_turned", per=2), sig("pT_made", per=2)
        o_product, o_made, o_turned, oT_made = sig("st_o_product"), sig("o_made", per=2), sig("o_turned", per=2), sig("oT_made", per=2)
        y_product, att_sum = sig("st_y_product"), sig("att_sum")
        m_turned, ms_made, ms_back = sig("m_turned"), sig("ms_made", per=4), sig("ms_back")
        stat_made, sigma_made, rsigma_made, x_normed = sig("stat_made", per=2), sig("sigma_made"), sig("rsigma_made"), sig("x_normed")
        xn_turned, xnT_made, gate_product, a_product = sig("xn_turned"), sig("xnT_made"), sig("up_gate_product"), sig("up_a_product")
        gate_biased, gate_made, a_biased, ff_made = sig("gate_biased"), sig("gate_made"), sig("a_biased"), sig("ff_made")
        ff_turned, ffT_made, y2_product, res_made = sig("ff_turned"), sig("ffT_made", per=2), sig("y2_product"), sig("res_made")

        Q_BANKS, K_BANKS, V_BANKS, X_BANK, FF_BANK = (banks[1], banks[2]), (banks[0], banks[1]), (banks[2], banks[0]), banks[0], banks[3]
        QK_BANKS = Q_BANKS + K_BANKS
        S_BANKS, T_BANKS = (banks[4], banks[5]), (banks[6], banks[7])
        FF_T_FULL = sum(m == P for _, m in FF_PARTS)
        TAIL = FF_PARTS[-1][1]
        TURNED = {"q": (S_BANKS, q_turned), "k": (T_BANKS, k_turned), "p": (T_BANKS, p_turned), "o": (T_BANKS, o_turned)}

        def layer_cols(tile, n, width, at=0, size=None):
            slot = (n // BLOCKS) % 2
            return tile[:, ds(slot * width + at, width if size is None else size)]

        def by_head(ap):
            return ap.rearrange("p (h d) -> p h d", d=DH)

        block = ctx.enter_context(nc.Block())


        def stream(engine, turn):
            turn(0, 0, True, False, False)
            turn(1, 1, True, True, False)
            with engine.Fori(2, STREAM, 2) as n:
                turn(n, 0, True, True, True)
                turn(n + 1, 1, True, True, True)
            turn(STREAM, 0, False, True, True)
            turn(STREAM + 1, 1, False, False, True)

        @block.sync
        def _(sp):
            carry = sems.carrier(sp, "st_sp_carried")
            for tile, name in ((ident, "ident"), (masks_f, "mask"), (follows, "follows"), (norm_gb, "norm_gb"), (eps, "eps")):
                sp.dma_start(tile[:, :], a[name]).then_inc(const_loaded.sem, 16)
            sp.dma_start(tables[:, :, :], a["tables"]).then_inc(const_loaded.sem, 16)

            def load_layer(layer, slot):
                for tile, name, width in ((wqkv, "wqkv", 3 * INNER), (wo, "wo", INNER), (w1, "w1", 2 * FF), (w2, "w2", len(FF_PARTS) * C)):
                    sp.dma_start(tile[:, slot * width:(slot + 1) * width], a[name][ds(layer, 1), :, :].rearrange("l p n -> p (l n)")).then_inc(w_loaded.sem, 16)
                for tile, name, width in ((b1, "b1", 2 * FF), (b2, "b2", C), (qk_gain, "qk_gain", 4 * DH)):
                    sp.dma_start(tile[:, slot * width:(slot + 1) * width],
                                 a[name][ds(layer, 1), :].to_broadcast([P, width])).then_inc(w_loaded.sem, 16)

            def place_v(n, u):
                sp.wait_ge(v_read.sem, v_read.after(n))
                carry()
                sp.wait_ge(o_product.sem, o_product.after(n - 2))
                carry()
                sp.wait_ge(v_placed.sem, v_placed.after(n - 1))
                for p in range(2):
                    cols = slice(p * INNER // 2, (p + 1) * INNER // 2)
                    for w in range(WINDOWS):
                        own, before = slice(WINDOW * w, WINDOW * (w + 1)), slice(WINDOW * (w - 1), WINDOW * w)
                        sp.dma_start(v_win[u][DH * p + WINDOW:DH * (p + 1), w, :], v_tok[u][own, cols]).then_inc(v_placed.sem, 16)
                        src = v_tok[u][before, cols] if w else v_tok[1 - u][P - WINDOW:P, cols]
                        sp.dma_start(v_win[u][DH * p:DH * p + WINDOW, w, :], src).then_inc(v_placed.sem, 16)

            sp.wait_ge(cleared.sem, 4)
            sp.sem_inc(v_placed.sem, v_placed.credit * v_placed.per)
            load_layer(0, 0)
            sp.wait_ge(w_loaded.sem, w_loaded.after(0))
            load_layer(1, 1)
            EARLY = 4
            for n in range(BLOCKS):
                place_v(n, n % 2)
            with sp.Fori(0, DEPTH // 2 - 1) as pair:
                for half in range(2):
                    layer = pair * 2 + 1 + half
                    for n in range(EARLY):
                        place_v(layer * BLOCKS + n, n % 2)
                    sp.wait_ge(x_ready.sem, x_ready.after(layer * BLOCKS - 1))
                    sp.wait_ge(w_loaded.sem, w_loaded.after(layer))
                    carry()
                    load_layer(layer + 1, half)
                    for n in range(EARLY, BLOCKS):
                        place_v(layer * BLOCKS + n, n % 2)
            for n in range(BLOCKS):
                place_v((DEPTH - 1) * BLOCKS + n, n % 2)

        @block.gpsimd
        def _(pool):
            carry = sems.carrier(pool, "st_pool_carried")
            for s in (x_taken, gains_made, rot_added, qk_made, halo_made, p_made, res_made, ff_made):
                for _ in range(s.credit * s.per):
                    nc.gpsimd.engine_nop().then_inc(s.sem, 1)
            pool.wait_ge(const_loaded.sem, 16 * 6)
            nc.gpsimd.tensor_copy(ident16[:, :], ident[:, :]).then_inc(masks_made.sem, 1)
            nc.gpsimd.tensor_copy(mask16[:, :, :].rearrange("p n k -> p (n k)"), masks_f[:, :]).then_inc(masks_made.sem, 1)
            pool.wait_ge(cleared.sem, 4)

            def take(n, u):
                pool.wait_ge(x_ready.sem, x_ready.after(n - BLOCKS))
                pool.wait_ge(att_sum.sem, att_sum.after(n - 2))
                carry()
                nc.gpsimd.tensor_copy(x_in[u][:, :], x_all[:, ds(n % BLOCKS, 1), :].rearrange("p n c -> p (n c)")).then_inc(x_taken.sem, 1)
                pool.wait_ge(w_loaded.sem, w_loaded.after(n // BLOCKS))
                pool.wait_ge(rotated.sem, rotated.after(n - 2))
                carry()
                nc.gpsimd.tensor_tensor(out=gains[u][:, :, :].rearrange("p f d -> p (f d)"),
                                        in0=tables[:, ds(n % SEQ_BLOCKS, 1), :].rearrange("p n c -> p (n c)"),
                                        in1=layer_cols(qk_gain, n, 4 * DH), op=ALU.mult).then_inc(gains_made.sem, 1)

            def rotate(n, u):
                for i in range(2):
                    half = slice(INNER * i, INNER * (i + 1))
                    pool.wait_ge(rotated.sem, rotated.after(n, 6 * (i + 1)))
                    nc.gpsimd.tensor_tensor(out=qk[u][:, half], in0=qk[u][:, half], in1=turnedhalf[:, half], op=ALU.add).then_inc(rot_added.sem, 1)
                pool.wait_ge(rnorm_made.sem, rnorm_made.after(n))
                for i in range(2):
                    half = slice(INNER * i, INNER * (i + 1))
                    pool.wait_ge(rot_added.sem, rot_added.after(n, i + 1))
                    nc.gpsimd.tensor_tensor(out=by_head(qk[u][:, half]), in0=by_head(qk[u][:, half]),
                                            in1=rnorm[u][:, AH * i:AH * (i + 1)].unsqueeze(2).to_broadcast([P, AH, DH]),
                                            op=ALU.mult).then_inc(qk_made.sem, 1)

            def halo(n, u):
                pool.wait_ge(kT_made.sem, kT_made.after(n - 1))
                pool.wait_ge(s_product.sem, s_product.after(n - 2))
                carry()
                nc.gpsimd.tensor_tensor(out=k_T[u][:, :, 0:WINDOW], in0=k_T[1 - u][:, :, P:P + WINDOW],
                                        in1=follows[:, ds(n % SEQ_BLOCKS, 1)].unsqueeze(2).to_broadcast([P, PAIRS, WINDOW]),
                                        op=ALU.mult).then_inc(halo_made.sem, 1)

            def normalise(n, u):
                pool.wait_ge(total_made.sem, total_made.after(n))
                pr = probs[u][:, :, :, :].rearrange("p a b d -> p (a b) d")
                nc.gpsimd.tensor_tensor(out=pr, in0=pr, in1=total[u][:, :].unsqueeze(2).to_broadcast([P, AH, DH]), op=ALU.mult).then_inc(p_made.sem, 1)

            def residual(n, u):
                pool.wait_ge(att_sum.sem, att_sum.after(n))
                pool.wait_ge(x_ready.sem, x_ready.after(n - 2))
                carry()
                nc.gpsimd.tensor_tensor(out=x_res[u][:, :], in0=x_att[u][:, :], in1=layer_cols(b2, n, C), op=ALU.add).then_inc(res_made.sem, 1)

            def glu(n, u):
                pool.wait_ge(gate_made.sem, gate_made.after(n))
                pool.wait_ge(a_biased.sem, a_biased.after(n))
                nc.gpsimd.tensor_tensor(out=gate[u][:, :], in0=gate[u][:, :], in1=act_in[u][:, :], op=ALU.mult).then_inc(ff_made.sem, 1)

            def turn(n, u, project, attend, feed):
                if attend:
                    halo(n - 1, 1 - u)
                if project:
                    take(n, u)
                if feed:
                    residual(n - 2, u)
                if attend:
                    normalise(n - 1, 1 - u)
                if feed:
                    glu(n - 2, u)
                if project:
                    rotate(n, u)

            stream(pool, turn)

        @block.tensor
        def _(pe):
            carry = sems.carrier(pe, "st_pe_carried")
            for s in (x_turned, qk_product, v_product, q_turned, k_turned, s_product, p_turned, o_product, o_turned, y_product,
                      m_turned, ms_back, xn_turned, gate_product, a_product, ff_turned, y2_product):
                for _ in range(s.credit * s.per):
                    nc.tensor.drain().then_inc(s.sem, 1)
            pe.wait_ge(masks_made.sem, 2)

            def turn_x(n, u):
                pe.wait_ge(x_taken.sem, x_taken.after(n))
                pe.wait_ge(v_read.sem, v_read.after(n - 1))
                nc.tensor.transpose(X_BANK[:, 0:P], x_in[u][:, :], ident[:, :]).then_inc(x_turned.sem, 1)

            def project_qk(n, u):
                pe.wait_ge(xs_made.sem, xs_made.after(n))
                pe.wait_ge(w_loaded.sem, w_loaded.after(n // BLOCKS))
                pe.wait_ge(rotated.sem, rotated.after(n - 1))
                for i in range(4):
                    if i == 3:
                        pe.wait_ge(rotated.sem, rotated.after(n, 3))
                    nc.tensor.matmul(QK_BANKS[i][:, :], xs_T[u][:, :], layer_cols(wqkv, n, 3 * INNER, 512 * i, 512),
                                     start=True, stop=True).then_inc(qk_product.sem, 1)

            def project_v(n, u):
                for i in range(2):
                    pe.wait_ge(rotated.sem, rotated.after(n, 6 + 3 * i))
                    nc.tensor.matmul(V_BANKS[i][:, :], xs_T[u][:, :], layer_cols(wqkv, n, 3 * INNER, 2 * INNER + 512 * i, 512),
                                     start=True, stop=True).then_inc(v_product.sem, 1)

            def transposes(which, n, source):
                outs, turned = TURNED[which]
                for i in range(PAIRS):
                    mm = nc.tensor.transpose(outs[i // 4][:, P * (i % 4):P * (i % 4 + 1)], source[:, P * i:P * (i + 1)], ident[:, :])
                    if i % 4 == 3:
                        mm.then_inc(turned.sem, 1)

            def turn_qk(n, u):
                pe.wait_ge(qk_made.sem, qk_made.after(n, 1))
                pe.wait_ge(att_sum.sem, att_sum.after(n - 1))
                transposes("q", n, qk[u][:, 0:INNER])
                pe.wait_ge(qk_made.sem, qk_made.after(n, 2))
                pe.wait_ge(oT_made.sem, oT_made.after(n - 1))
                transposes("k", n, qk[u][:, INNER:2 * INNER])

            def scores(n, u):
                pe.wait_ge(qT_made.sem, qT_made.after(n))
                pe.wait_ge(kT_made.sem, kT_made.after(n))
                pe.wait_ge(halo_made.sem, halo_made.after(n))
                mask = mask16[:, ds(n % SEQ_BLOCKS, 1), :].to_broadcast([P, PAIRS, 2 * WINDOW])
                for p in range(2):
                    nc.tensor.matmul(S_BANKS[p][:, :].rearrange("p (a k) -> p a k", a=PAIRS), ident16[:, :], mask,
                                     start=True, stop=False, skip_group_check=True)
                for a_ in range(PAIRS):
                    for w in range(WINDOWS):
                        for p in range(2):
                            at, rows = WINDOW * w, slice(DH * p, DH * (p + 1))
                            mm = nc.tensor.matmul(S_BANKS[p][at:at + WINDOW, 2 * WINDOW * a_:2 * WINDOW * (a_ + 1)],
                                                  q_T[u][rows, a_, at:at + WINDOW], k_T[u][rows, a_, at:at + 2 * WINDOW],
                                                  start=False, stop=True, skip_group_check=True)
                mm.then_inc(s_product.sem, 1)

            def turn_p(n, u):
                pe.wait_ge(p_made.sem, p_made.after(n))
                transposes("p", n, probs[u][:, :, :, :].rearrange("p a b d -> p (a b d)"))

            def outputs(n, u):
                pe.wait_ge(pT_made.sem, pT_made.after(n))
                pe.wait_ge(shifted.sem, shifted.after(n))
                pe.wait_ge(v_placed.sem, v_placed.after(n))
                carry()
                for a_ in range(PAIRS):
                    for w in range(WINDOWS):
                        for p in range(2):
                            at, rows = WINDOW * w, slice(DH * p, DH * (p + 1))
                            mm = nc.tensor.matmul(S_BANKS[p][at:at + WINDOW, DH * a_:DH * (a_ + 1)],
                                                  p_T[u][rows, a_, at:at + WINDOW], v_win[u][rows, w, DH * a_:DH * (a_ + 1)],
                                                  start=True, stop=True, skip_group_check=True)
                mm.then_inc(o_product.sem, 1)

            def turn_o(n, u):
                pe.wait_ge(o_made.sem, o_made.after(n))
                transposes("o", n, probs[u][:, :, :, :].rearrange("p a b d -> p (a b d)"))

            def project_o(n, u):
                pe.wait_ge(oT_made.sem, oT_made.after(n))
                for i in range(PAIRS):
                    mm = nc.tensor.matmul(S_BANKS[0][:, 0:C], o_T[u][:, i, :], layer_cols(wo, n, INNER, C * i, C),
                                          start=(i == 0), stop=(i == PAIRS - 1))
                mm.then_inc(y_product.sem, 1)

            def turn_m(n, u):
                pe.wait_ge(att_sum.sem, att_sum.after(n))
                pe.wait_ge(x_ready.sem, x_ready.after(n - 1))
                nc.tensor.transpose(FF_BANK[:, 0:P], x_att[u][:, :], ident[:, :]).then_inc(m_turned.sem, 1)

            def turn_back(n, u):
                pe.wait_ge(ms_made.sem, ms_made.after(n))
                nc.tensor.transpose(FF_BANK[:, 0:P], ms_T[u][:, :], ident[:, :]).then_inc(ms_back.sem, 1)

            def turn_xn(n, u):
                pe.wait_ge(x_normed.sem, x_normed.after(n))
                nc.tensor.transpose(FF_BANK[:, 0:P], xn[u][:, :], ident[:, :]).then_inc(xn_turned.sem, 1)

            def up_gate(n, u):
                pe.wait_ge(xnT_made.sem, xnT_made.after(n))
                nc.tensor.matmul(FF_BANK[:, 0:FF], xn_T[u][:, :], layer_cols(w1, n, 2 * FF, FF, FF), start=True, stop=True).then_inc(gate_product.sem, 1)

            def up_a(n, u):
                pe.wait_ge(gate_biased.sem, gate_biased.after(n))
                nc.tensor.matmul(FF_BANK[:, 0:FF], xn_T[u][:, :], layer_cols(w1, n, 2 * FF, 0, FF), start=True, stop=True).then_inc(a_product.sem, 1)

            def turn_ff(n, u):
                pe.wait_ge(ff_made.sem, ff_made.after(n))
                for i, (at, m) in enumerate(FF_PARTS):
                    mm = nc.tensor.transpose(FF_BANK[0:m, P * i:P * (i + 1)], gate[u][:, at:at + m], ident[:, :])
                mm.then_inc(ff_turned.sem, 1)

            def down(n, u):
                pe.wait_ge(ffT_made.sem, ffT_made.after(n))
                for i, (_, m) in enumerate(FF_PARTS):
                    w = layer_cols(w2, n, len(FF_PARTS) * C, C * i, C)
                    mm = nc.tensor.matmul(FF_BANK[:, 0:C], ff_T[u][0:m, i, :], w[0:m], start=(i == 0), stop=(i == len(FF_PARTS) - 1))
                mm.then_inc(y2_product.sem, 1)

            def turn(n, u, project, attend, feed):
                v, m, l = 1 - u, n - 1, n - 2
                if project:
                    turn_x(n, u)
                if attend:
                    turn_qk(m, v)
                if feed:
                    turn_m(l, u)
                if project:
                    project_qk(n, u)
                if attend:
                    scores(m, v)
                if feed:
                    turn_back(l, u)
                if project:
                    project_v(n, u)
                if feed:
                    turn_xn(l, u)
                    up_gate(l, u)
                if attend:
                    turn_p(m, v)
                if feed:
                    up_a(l, u)
                if attend:
                    outputs(m, v)
                if attend:
                    turn_o(m, v)
                if feed:
                    turn_ff(l, u)
                if attend:
                    project_o(m, v)
                if feed:
                    down(l, u)

            stream(pe, turn)

        @block.scalar
        def _(act):
            for s in (xs_made, squared, root_made, v_read, qT_made, kT_made, exp_made, pT_made, o_made, oT_made,
                      ms_made, sigma_made, xnT_made, gate_made, ffT_made):
                for _ in range(s.credit * s.per):
                    nc.scalar.drain().then_inc(s.sem, 1)
            act.wait_ge(const_loaded.sem, 16 * 6)
            act.wait_ge(cleared.sem, 4)

            def shift(n, u, bank, out, last, made):
                nc.scalar.activation(out[u][0:64, :], bank[0:64, 0:P], ACT.Copy).then_inc(made.sem, 1)
                nc.scalar.activation(out[u][64:P, 1:P], bank[64:P, 0:P - 1], ACT.Copy).then_inc(made.sem, 1)
                act.wait_ge(made.sem, made.after(n - 1))
                nc.scalar.activation(out[u][64:P, 0:1], last[1 - u][64:P, :], ACT.Copy,
                                     scale=follows[64:P, ds(n % SEQ_BLOCKS, 1)]).then_inc(made.sem, 1)
                nc.scalar.activation(last[u][64:P, :], bank[64:P, P - 1:P], ACT.Copy).then_inc(made.sem, 1)

            def shift_x(n, u):
                act.wait_ge(x_turned.sem, x_turned.after(n))
                act.wait_ge(v_product.sem, v_product.after(n - 2))
                shift(n, u, X_BANK, xs_T, edge, xs_made)

            def square(n, u):
                act.wait_ge(ss_made.sem, ss_made.after(n - 1))
                for i in range(4):
                    act.wait_ge(qk_product.sem, qk_product.after(n, i + 1))
                    nc.scalar.activation(squares[:, 512 * i:512 * (i + 1)], QK_BANKS[i][:, :], ACT.Square).then_inc(squared.sem, 1)

            def root(n, u):
                act.wait_ge(ss_made.sem, ss_made.after(n))
                nc.scalar.activation(rnorm[u][:, :], rnorm[u][:, :], ACT.Sqrt).then_inc(root_made.sem, 1)

            def read_v(n, u):
                act.wait_ge(v_placed.sem, v_placed.after(n - 1))
                for i in range(2):
                    act.wait_ge(v_product.sem, v_product.after(n, i + 1))
                    out = v_tok[u][:, :].rearrange("p (b a d) -> p b a d", b=2, d=DH)[:, :, 4 * i:4 * i + 4, :]
                    nc.scalar.activation(out, V_BANKS[i][:, :].rearrange("p (a b d) -> p b a d", b=2, d=DH), ACT.Copy).then_inc(v_read.sem, 1)

            def read_qk(n, u):
                act.wait_ge(s_product.sem, s_product.after(n - 2))
                for i in range(2):
                    act.wait_ge(q_turned.sem, q_turned.after(n, i + 1))
                    nc.scalar.activation(q_T[u][:, 4 * i:4 * i + 4, :].rearrange("p a t -> p (a t)"), S_BANKS[i][:, :], ACT.Copy).then_inc(qT_made.sem, 1)
                act.wait_ge(halo_made.sem, halo_made.after(n - 1))
                for i in range(2):
                    act.wait_ge(k_turned.sem, k_turned.after(n, i + 1))
                    nc.scalar.activation(k_T[u][:, 4 * i:4 * i + 4, WINDOW:], T_BANKS[i][:, :].rearrange("p (a t) -> p a t", a=4), ACT.Copy).then_inc(kT_made.sem, 1)

            def exponent(n, u):
                act.wait_ge(shifted.sem, shifted.after(n))
                pr = probs[u][:, :, :, :].rearrange("p a b d -> p (a b d)")
                nc.scalar.activation(pr, pr, ACT.Exp, scale=QK_SCALE).then_inc(exp_made.sem, 1)

            def read_turned(n, u, banks_, turned, out, made):
                for i in range(2):
                    act.wait_ge(turned.sem, turned.after(n, i + 1))
                    nc.scalar.activation(out[u][:, 4 * i:4 * i + 4, :].rearrange("p a t -> p (a t)"), banks_[i][:, :], ACT.Copy).then_inc(made.sem, 1)

            def read_p(n, u):
                act.wait_ge(o_product.sem, o_product.after(n - 2))
                read_turned(n, u, T_BANKS, p_turned, p_T, pT_made)

            def read_o(n, u):
                act.wait_ge(o_product.sem, o_product.after(n))
                for p in range(2):
                    nc.scalar.activation(probs[u][:, :, p, :], S_BANKS[p][:, :].rearrange("p (a d) -> p a d", d=DH), ACT.Copy).then_inc(o_made.sem, 1)

            def read_oT(n, u):
                act.wait_ge(y_product.sem, y_product.after(n - 2))
                read_turned(n, u, T_BANKS, o_turned, o_T, oT_made)

            def shift_m(n, u):
                act.wait_ge(m_turned.sem, m_turned.after(n))
                act.wait_ge(ms_back.sem, ms_back.after(n - 2))
                shift(n, u, FF_BANK, ms_T, edge2, ms_made)

            def sigma(n, u):
                act.wait_ge(stat_made.sem, stat_made.after(n))
                nc.scalar.activation(mv[u][:, 1:2], mv[u][:, 1:2], ACT.Sqrt, bias=eps[:, :]).then_inc(sigma_made.sem, 1)

            def affine(n, u):
                act.wait_ge(xn_turned.sem, xn_turned.after(n))
                act.wait_ge(a_product.sem, a_product.after(n - 2))
                layer = n // BLOCKS
                nc.scalar.activation(xn_T[u][:, :], FF_BANK[:, 0:P], ACT.Identity, scale=norm_gb[:, ds(layer, 1)],
                                     bias=norm_gb[:, ds(layer + DEPTH, 1)]).then_inc(xnT_made.sem, 1)

            def gelu(n, u):
                act.wait_ge(gate_biased.sem, gate_biased.after(n))
                nc.scalar.activation(gate[u][:, :], gate[u][:, :], ACT.Gelu).then_inc(gate_made.sem, 1)

            def read_ff(n, u):
                act.wait_ge(ff_turned.sem, ff_turned.after(n))
                act.wait_ge(y2_product.sem, y2_product.after(n - 2))
                nc.scalar.activation(ff_T[u][:, 0:FF_T_FULL, :].rearrange("p i t -> p (i t)"), FF_BANK[:, 0:FF_T_FULL * P], ACT.Copy).then_inc(ffT_made.sem, 1)
                nc.scalar.activation(ff_T[u][0:TAIL, FF_T_FULL, :], FF_BANK[0:TAIL, FF_T_FULL * P:(FF_T_FULL + 1) * P], ACT.Copy).then_inc(ffT_made.sem, 1)

            def turn(n, u, project, attend, feed):
                v, m, l = 1 - u, n - 1, n - 2
                if project:
                    shift_x(n, u)
                if attend:
                    read_qk(m, v)
                if feed:
                    shift_m(l, u)
                if project:
                    square(n, u)
                if feed:
                    sigma(l, u)
                if project:
                    root(n, u)
                if attend:
                    exponent(m, v)
                if project:
                    read_v(n, u)
                if feed:
                    affine(l, u)
                if attend:
                    read_p(m, v)
                if feed:
                    gelu(l, u)
                if attend:
                    read_o(m, v)
                    read_oT(m, v)
                if feed:
                    read_ff(l, u)

            stream(act, turn)

        @block.vector
        def _(dve):
            carry = sems.carrier(dve, "st_dve_carried")
            for tile in (edge[1][64:P, :], edge2[1][64:P, :], v_tok[1][P - WINDOW:P, :]):
                nc.vector.memset(tile, 0.0).then_inc(cleared.sem, 1)
            nc.vector.memset(k_T[1][:, :, P:P + WINDOW], 0.0).then_inc(cleared.sem, 1)
            for s in (x_ready, rotated, ss_made, rnorm_made, peak_made, shifted, total_made, att_sum, stat_made, rsigma_made,
                      x_normed, gate_biased, a_biased):
                for _ in range(s.credit * s.per):
                    nc.vector.engine_nop().then_inc(s.sem, 1)

            def rotate(n, u, i):
                dve.wait_ge(squared.sem, squared.after(n, i + 1))
                if i == 0:
                    dve.wait_ge(gains_made.sem, gains_made.after(n))
                    dve.wait_ge(k_turned.sem, k_turned.after(n - 2))
                if i % 2 == 0:
                    dve.wait_ge(rot_added.sem, rot_added.after(n - 1, i // 2 + 1))
                cols, src = slice(512 * i, 512 * (i + 1)), by_head(QK_BANKS[i][:, :])
                cos, sin = (gains[u][:, 2 * (i // 2) + f:2 * (i // 2) + f + 1, :] for f in range(2))
                nc.vector.tensor_tensor(by_head(qk[u][:, cols]), src, cos.to_broadcast([P, 8, DH]), ALU.mult).then_inc(rotated.sem, 1)
                half = DH // 2
                for f in range(2):
                    to, frm = slice(half * f, half * (f + 1)), slice(half * (1 - f), half * (2 - f))
                    nc.vector.tensor_tensor(by_head(turnedhalf[:, cols])[:, :, to], src[:, :, frm],
                                            sin[:, :, to].to_broadcast([P, 8, half]), ALU.mult).then_inc(rotated.sem, 1)

            def norms(n, u):
                dve.wait_ge(squared.sem, squared.after(n))
                dve.wait_ge(qk_made.sem, qk_made.after(n - 2))
                nc.vector.reduce_sum(rnorm[u][:, :], by_head(squares[:, :]), AX).then_inc(ss_made.sem, 1)

            def rnorms(n, u):
                dve.wait_ge(root_made.sem, root_made.after(n))
                nc.vector.tensor_scalar(rnorm[u][:, :], rnorm[u][:, :], NORM_FLOOR, None, ALU.max).then_inc(rnorm_made.sem, 1)
                dve.wait_ge(rnorm_made.sem, rnorm_made.after(n, 1))
                nc.vector.reciprocal(rnorm[u][:, :], rnorm[u][:, :]).then_inc(rnorm_made.sem, 1)

            def peaks(n, u):
                dve.wait_ge(s_product.sem, s_product.after(n))
                dve.wait_ge(o_turned.sem, o_turned.after(n - 2))
                for p in range(2):
                    s = S_BANKS[p][:, :].rearrange("p (a k) -> p a k", a=PAIRS)
                    nc.vector.reduce_max(peak[u][:, p, :], s, AX).then_inc(peak_made.sem, 1)
                for p in range(2):
                    s = S_BANKS[p][:, :].rearrange("p (a k) -> p a k", a=PAIRS)
                    dve.wait_ge(peak_made.sem, peak_made.after(n, p + 1))
                    nc.vector.tensor_tensor(probs[u][:, :, p, :], s, peak[u][:, p, :].unsqueeze(2).to_broadcast([P, PAIRS, DH]),
                                            ALU.subtract).then_inc(shifted.sem, 1)

            def totals(n, u):
                dve.wait_ge(exp_made.sem, exp_made.after(n))
                nc.vector.reduce_sum(total[u][:, :], probs[u][:, :, :, :].rearrange("p a b d -> p (a b) d"), AX).then_inc(total_made.sem, 1)
                dve.wait_ge(total_made.sem, total_made.after(n, 1))
                nc.vector.reciprocal(total[u][:, :], total[u][:, :]).then_inc(total_made.sem, 1)

            def add_attention(n, u):
                dve.wait_ge(y_product.sem, y_product.after(n))
                dve.wait_ge(res_made.sem, res_made.after(n - 2))
                dve.wait_ge(m_turned.sem, m_turned.after(n - 2))
                nc.vector.tensor_tensor(x_att[u][:, :], S_BANKS[0][:, 0:C], x_in[u][:, :], ALU.add).then_inc(att_sum.sem, 1)

            def moments(n, u):
                dve.wait_ge(ms_back.sem, ms_back.after(n))
                nc.vector.bn_stats(stats[u][:, :], FF_BANK[:, 0:C]).then_inc(stat_made.sem, 1)
                dve.wait_ge(stat_made.sem, stat_made.after(n, 1))
                carry()
                nc.vector.bn_aggr(mv[u][:, :], stats[u][:, :]).then_inc(stat_made.sem, 1)

            def norm_x(n, u):
                dve.wait_ge(sigma_made.sem, sigma_made.after(n))
                nc.vector.reciprocal(mv[u][:, 1:2], mv[u][:, 1:2]).then_inc(rsigma_made.sem, 1)
                dve.wait_ge(rsigma_made.sem, rsigma_made.after(n))
                nc.vector.tensor_scalar(xn[u][:, :], FF_BANK[:, 0:C], mv[u][:, 0:1], mv[u][:, 1:2],
                                        ALU.subtract, ALU.mult).then_inc(x_normed.sem, 1)

            def bias_gate(n, u):
                dve.wait_ge(gate_product.sem, gate_product.after(n))
                dve.wait_ge(ff_turned.sem, ff_turned.after(n - 2))
                nc.vector.tensor_tensor(gate[u][:, :], FF_BANK[:, 0:FF], layer_cols(b1, n, 2 * FF, FF, FF), ALU.add).then_inc(gate_biased.sem, 1)

            def bias_a(n, u):
                dve.wait_ge(a_product.sem, a_product.after(n))
                dve.wait_ge(ff_made.sem, ff_made.after(n - 2))
                nc.vector.tensor_tensor(act_in[u][:, :], FF_BANK[:, 0:FF], layer_cols(b1, n, 2 * FF, 0, FF), ALU.add).then_inc(a_biased.sem, 1)

            def add_ffn(n, u):
                dve.wait_ge(y2_product.sem, y2_product.after(n))
                dve.wait_ge(res_made.sem, res_made.after(n))
                nc.vector.tensor_tensor(x_all[:, ds(n % BLOCKS, 1), :].rearrange("p n c -> p (n c)"), FF_BANK[:, 0:C], x_res[u][:, :],
                                        ALU.add).then_inc(x_ready.sem, 1)

            def turn(n, u, project, attend, feed):
                v, m, l = 1 - u, n - 1, n - 2
                if project:
                    rotate(n, u, 0)
                    rotate(n, u, 1)
                if feed:
                    moments(l, u)
                if project:
                    rotate(n, u, 2)
                    rotate(n, u, 3)
                    norms(n, u)
                if feed:
                    norm_x(l, u)
                if attend:
                    peaks(m, v)
                if project:
                    rnorms(n, u)
                if feed:
                    bias_gate(l, u)
                if attend:
                    totals(m, v)
                if feed:
                    bias_a(l, u)
                if attend:
                    add_attention(m, v)
                if feed:
                    add_ffn(l, u)

            stream(dve, turn)


def build_final(nc, banks, a, x_mid, x_all, out):
    with PhaseSignals(nc) as sems, ExitStack() as ctx:
        def sig(name):
            return Signal(sems, name)

        stats = ctx.enter_context(nc.sbuf_tensor("fi_stats", [P, BLOCKS, 6], F32))
        mv = ctx.enter_context(nc.sbuf_tensor("fi_mv", [P, BLOCKS, 2], F32))
        eps = ctx.enter_context(nc.sbuf_tensor("fi_eps", [P, 1], F32))
        added, counted, gathered, rooted, inverted, normed, loaded, stored = (
            sig(n) for n in ("fi_added", "fi_counted", "fi_gathered", "fi_rooted", "fi_inverted", "fi_normed", "fi_loaded", "fi_stored"))
        block = ctx.enter_context(nc.Block())

        @block.sync
        def _(sp):
            sp.dma_start(eps[:, :], a["eps"]).then_inc(loaded.sem, 16)
            halves = 2
            for h in range(halves):
                part = slice(BLOCKS // halves * h, BLOCKS // halves * (h + 1))
                sp.wait_ge(normed.sem, BLOCKS // halves * (h + 1))
                sp.dma_start(out.rearrange("(n p) c -> p n c", p=P)[:, part, :], x_all[:, part, :]).then_inc(stored.sem, 16)
            sp.wait_ge(stored.sem, 16 * halves)

        @block.vector
        def _(dve):
            nc.vector.tensor_tensor(x_all[:, :, :], x_all[:, :, :], x_mid[:, :, :], ALU.add).then_inc(added.sem, 1)
            dve.wait_ge(added.sem, 1)
            for n in range(BLOCKS):
                nc.vector.bn_stats(stats[:, n, :], x_all[:, n, :]).then_inc(counted.sem, 1)
            for n in range(BLOCKS):
                dve.wait_ge(counted.sem, n + 1)
                nc.vector.bn_aggr(mv[:, n, :], stats[:, n, :]).then_inc(gathered.sem, 1)
            dve.wait_ge(rooted.sem, 1)
            nc.vector.reciprocal(mv[:, :, 1], mv[:, :, 1]).then_inc(inverted.sem, 1)
            dve.wait_ge(inverted.sem, 1)
            for n in range(BLOCKS):
                nc.vector.tensor_scalar(x_all[:, n, :], x_all[:, n, :], mv[:, n, 0:1], mv[:, n, 1:2],
                                        ALU.subtract, ALU.mult).then_inc(normed.sem, 1)

        @block.scalar
        def _(act):
            act.wait_ge(loaded.sem, 16)
            act.wait_ge(gathered.sem, BLOCKS)
            nc.scalar.activation(mv[:, :, 1], mv[:, :, 1], ACT.Sqrt, bias=eps[:, :]).then_inc(rooted.sem, 1)


def build_program(nc, a, out):
    with ExitStack() as ctx:
        banks = [ctx.enter_context(nc.psum_tensor(f"bank{i}", [P, GROUP], F32)) for i in range(8)]
        x_mid, x_all = (ctx.enter_context(nc.sbuf_tensor(n, [P, BLOCKS, C], F32)) for n in ("x_mid", "x_all"))
        build_mixing(nc, a, banks, x_mid, x_all)
        with nc.sbuf_tensor("masks_f", [P, SEQ_BLOCKS * 2 * WINDOW], F32) as masks_f:
            build_stream(nc, a, banks, x_all, masks_f)
        build_final(nc, banks, a, x_mid, x_all, out)


def layouts(L):
    f = np.float32

    def asn(name, shape=None):
        v = np.asarray(L[name])
        return v if shape is None else v.reshape(shape)

    out = {}
    x = asn("L0_attn_x")
    out["xT"] = np.ascontiguousarray(x.reshape(N, C).T)
    out["x_tok"] = np.ascontiguousarray(x.reshape(BLOCKS, P, C).transpose(1, 0, 2))
    vecs = np.zeros((P, 16), f)
    vecs[:, V_MAAX] = asn("L0_attn_time_maa_x")
    vecs[:, V_MAA:V_MAA + 4] = asn("L0_attn_time_maa", (4, C)).T
    for col, name in ((V_DECAY, "time_decay"), (V_AAAAA, "time_aaaaa"), (V_MISCA, "time_misc_a"), (V_MISCK, "time_misc_k"),
                      (V_FAAAA, "time_faaaa"), (V_LNW, "ln_w"), (V_LNB, "ln_b")):
        vecs[:, col] = asn("L0_attn_" + name)
    vecs[:, V_ONE], vecs[:, V_YEPS], vecs[:, V_LNEPS] = 1.0, Y_EPS, LN_EPS
    out["vecs"] = vecs
    out["ident"] = np.eye(P, dtype=f)
    for name, src in (("w_lo", "maa_w1"), ("w_r", "Wr"), ("w_g1", "gate_w1"), ("w_k", "Wk"), ("w_v", "Wv"), ("w_o", "Wo")):
        out[name] = np.ascontiguousarray(asn("L0_attn_" + src).T)
    out["w_maa"] = np.ascontiguousarray(asn("L0_attn_maa_w2", (P, C)))
    out["w_g2"] = np.ascontiguousarray(asn("L0_attn_gate_w2"))
    w = np.zeros((P, P), f)
    w[:, 0:64], w[:, AAA_AT:AAA_AT + 16], w[:, MA_AT:MA_AT + 16] = (asn("L0_attn_" + n).T for n in ("decay_w1", "aaa_w1", "ma_w1"))
    out["w_xwa"] = w
    w = np.zeros((P, P), f)
    w[0:64], w[AAA_AT:AAA_AT + 16], w[MA_AT:MA_AT + 16] = (asn("L0_attn_" + n) for n in ("decay_w2", "aaa_w2", "ma_w2"))
    out["w_second"] = w
    w = np.zeros((P, 64), f)
    w[:, 0:16], w[:, MK_AT:MK_AT + 16] = (asn("L0_attn_" + n).T for n in ("kkk_w1", "mk_w1"))
    out["w_xk"] = w
    w = np.zeros((64, P), f)
    w[0:16], w[MK_AT:MK_AT + 16] = (asn("L0_attn_" + n) for n in ("kkk_w2", "mk_w2"))
    out["w_xk2"] = w
    head, row = np.arange(P) // HS, np.arange(P) % HS
    same = head[:, None] == head[None, :]
    out["headones"] = same.astype(f)
    out["spread"] = np.concatenate([(same & (row == i)[:, None]).astype(f) for i in range(HS)], 1)
    out["collect"] = np.concatenate([(same & (row == i)[None, :]).astype(f) for i in range(HS)], 1)
    out["headmask"] = (head[:, None] == np.arange(HEADS)[None, :]).astype(f)
    out["rowmask"] = (row[:, None] == np.arange(HS)[None, :]).astype(f)
    return out


def stream_layouts(L):
    f = np.float32
    out = {}

    def asn(name):
        return np.asarray(L["L0_ffn_" + name])

    out["wqkv"] = np.ascontiguousarray(asn("Wqkv"))
    out["wo"] = np.ascontiguousarray(asn("Wo").reshape(DEPTH, PAIRS, P, C).transpose(0, 2, 1, 3).reshape(DEPTH, P, INNER))
    out["w1"] = np.ascontiguousarray(asn("W1"))
    w2 = np.zeros((DEPTH, len(FF_PARTS) * P, C), f)
    w2[:, 0:FF] = asn("W2")
    out["w2"] = np.ascontiguousarray(w2.reshape(DEPTH, len(FF_PARTS), P, C).transpose(0, 2, 1, 3).reshape(DEPTH, P, len(FF_PARTS) * C))
    out["b1"], out["b2"] = np.ascontiguousarray(asn("b1")), np.ascontiguousarray(asn("b2"))
    qs, ks, half = asn("q_scale"), asn("k_scale"), DH // 2

    def swapped(v):
        return np.concatenate([v[:, half:], v[:, :half]], 1)

    out["qk_gain"] = np.ascontiguousarray(np.concatenate([qs, swapped(qs), ks, swapped(ks)], 1))
    out["norm_gb"] = np.ascontiguousarray(np.concatenate([asn("ln_g"), asn("ln_b")], 0).T)
    ar = np.arange(0, DH, 2, dtype=f)
    freqs = np.arange(T, dtype=f)[:, None] * (f(1.0) / f(10000.0) ** (ar / f(DH)))[None, :]
    base = (ar + f(0.4 * DH)) / f(1.4 * DH)
    scale = base[None, :] ** ((np.arange(T, dtype=f) - T // 2) / f(WINDOW // 2))[:, None]
    cos, sin = np.cos(freqs), np.sin(freqs)
    parts = []
    for s in (scale, f(1.0) / scale):
        parts += [cos * s, cos * s, -sin * s, sin * s]
    tab = np.concatenate(parts, 1).astype(f)
    out["tables"] = np.ascontiguousarray(tab.reshape(SEQ_BLOCKS, P, 4 * DH).transpose(1, 0, 2))
    i, j = (np.arange(P) % WINDOW)[:, None], np.arange(2 * WINDOW)[None, :]
    allowed = (j >= i) & (j <= i + WINDOW)
    mask = np.where(allowed, 0.0, MASKED).astype(f)
    full = np.repeat(mask[:, None, :], SEQ_BLOCKS, 1)
    full[0:WINDOW, 0, 0:WINDOW] = MASKED
    out["mask"] = np.ascontiguousarray(full.reshape(P, -1))
    follows = np.ones((P, SEQ_BLOCKS), f)
    follows[:, 0] = 0.0
    out["follows"] = follows
    out["eps"] = np.full((P, 1), LN_EPS, f)
    return out


def kernel(**inputs):
    from concourse import bacc
    from concourse.bass_utils import run_bass_kernel_spmd

    arrays = {**layouts(inputs), **stream_layouts(inputs)}
    nc = bacc.Bacc("TRN2", target_bir_lowering=False, num_devices=1)
    a = {name: nc.dram_tensor(f"in_{name}", list(v.shape), mybir.dt.from_np(v.dtype), kind="ExternalInput").ap()
         for name, v in arrays.items()}
    out = nc.dram_tensor("out", [N, C], F32, kind="ExternalOutput").ap()
    build_program(nc, a, out)
    r = run_bass_kernel_spmd(nc, [{f"in_{name}": v for name, v in arrays.items()}], core_ids=[0])
    return r.results[0]["out"].reshape(B, T, C)
```

```python
from contextlib import ExitStack

import numpy as np

import concourse.bass as bass
from concourse import mybir
from concourse.bass import ds

F32 = mybir.dt.float32
BF16 = mybir.dt.bfloat16
ALU = mybir.AluOpType
ACT = mybir.ActivationFunctionType
AX = mybir.AxisListType.X

P = 128
B, T, C = 2, 1024, 128
N = B * T
HEADS, HS = 16, 8
GROUP = 512
GROUPS = N // GROUP
CHUNK = 32
CHUNKS = N // CHUNK
SEQ_CHUNKS = T // CHUNK
Y_EPS, NORM_FLOOR, LN_EPS = 0.00064, 1e-12, 1e-5

DEPTH, DH, WINDOW = 6, 64, 32
AH = 16
INNER = AH * DH
PAIRS = AH // 2
FF = int(C * 4 * 2 / 3)
FF_PARTS = [(at, min(P, FF - at)) for at in range(0, FF, P)]
BLOCKS = N // P
SEQ_BLOCKS = T // P
WINDOWS = P // WINDOW
QK_SCALE = 8.0
MASKED = -1e30
STREAM = DEPTH * BLOCKS


class Signal:

    def __init__(self, signals, name, per=1, credit=0):
        self.sem, self.per, self.credit = signals.semaphore(name), per, credit

    def after(self, turn, part=None):
        return (turn + self.credit) * self.per + (self.per if part is None else part)


class PhaseSignals(ExitStack):

    def __init__(self, nc):
        super().__init__()
        self.nc, self.sems = nc, []

    def semaphore(self, name):
        self.sems.append(self.enter_context(self.nc.semaphore(name)))
        return self.sems[-1]

    def carrier(self, engine, name):
        sem = self.semaphore(name)
        return lambda: engine.sem_inc(sem, 1)

    def __exit__(self, *raised):
        if raised[0] is None:
            with self.nc.Block() as block:
                @block.sync
                def _(sp):
                    for sem in self.sems:
                        sp.sem_clear(sem)
        return super().__exit__(*raised)


def mix_inputs(sb):
    t = {}
    for name, shape in (("xT", (P, N)), ("vecs", (P, 16)), ("ident", (P, P)), ("w_lo", (P, P)), ("w_maa", (P, P)),
                        ("w_r", (P, P)), ("w_g1", (P, P)), ("w_g2", (P, P)), ("w_xwa", (P, P)), ("w_k", (P, P)),
                        ("w_xk", (P, 64)), ("w_v", (P, P)), ("w_second", (P, P)), ("w_xk2", (64, P)),
                        ("w_o", (P, P)), ("headones", (P, P)), ("spread", (P, HS * P)), ("collect", (P, HS * P)),
                        ("headmask", (P, HEADS)), ("rowmask", (P, HS))):
        t[name] = sb(name, shape)
    return t


V_MAAX, V_MAA, V_DECAY, V_AAAAA, V_MISCA, V_MISCK, V_FAAAA, V_LNW, V_LNB, V_ONE, V_YEPS, V_LNEPS = \
    0, 1, 5, 6, 7, 8, 9, 10, 11, 12, 13, 14
AAA_AT, MA_AT = 64, 96
MK_AT = 32


def build_projections(nc, a, t, loads, banks):
    with PhaseSignals(nc) as sems, ExitStack() as ctx:
        def sig(name, **kw):
            return Signal(sems, name, **kw)

        xx, mix, lo, gt, h1, h2 = (ctx.enter_context(nc.sbuf_tensor(n, [P, N], F32))
                                   for n in ("xx", "mix", "lo", "gt", "h1", "h2"))
        xm = [ctx.enter_context(nc.sbuf_tensor(f"xm{g}", [P, N], F32)) for g in range(4)]
        xT, vecs = t["xT"], t["vecs"]
        loaded = sig("p_loaded")
        loaded_x = sig("p_loaded_x")
        xx_made, mix_made, lo_made, gt_made = sig("xx_made"), sig("mix_made"), sig("lo_made"), sig("gt_made")
        h1_made, h2_made, k_made = sig("h1_made", per=2), sig("h2_made", per=2), sig("k_made")
        xm_scaled = [sig(f"xm_scaled{g}") for g in range(4)]
        xm_made = [sig(f"xm_made{g}") for g in range(4)]
        r_made, v_made, g_made, z_made = sig("r_made"), sig("v_made"), sig("g_made"), sig("z_made", per=2)
        a_made, ma_made, mk_made, kk_made = sig("a_made"), sig("ma_made"), sig("mk_made"), sig("kk_made")

        products = [("lo", t["w_lo"], mix, (0, P), mix_made, lo_made)]
        products += [(f"maa{g}", t["w_maa"], lo, (32 * g, 32 * g + 32), lo_made, xm_scaled[g]) for g in range(4)]
        products += [("r", t["w_r"], xm[0], (0, P), xm_made[0], r_made),
                     ("g1", t["w_g1"], xm[0], (0, P), xm_made[0], gt_made),
                     ("xwa", t["w_xwa"], xm[1], (0, P), xm_made[1], h1_made),
                     ("k", t["w_k"], xm[2], (0, P), xm_made[2], k_made),
                     ("xk", t["w_xk"], xm[2], (0, P), xm_made[2], h2_made),
                     ("v", t["w_v"], xm[3], (0, P), xm_made[3], v_made),
                     ("g2", t["w_g2"], gt, (0, P), gt_made, g_made),
                     ("z", t["w_second"], h1, (0, 64), h1_made, z_made),
                     ("a", t["w_second"], h1, (AAA_AT, AAA_AT + 16), h1_made, a_made),
                     ("ma", t["w_second"], h1, (MA_AT, MA_AT + 16), h1_made, ma_made),
                     ("kk", t["w_xk2"], h2, (0, 16), h2_made, kk_made),
                     ("mk", t["w_xk2"], h2, (MK_AT, MK_AT + 16), h2_made, mk_made)]
        done = {p[0]: sig(f"{p[0]}_product") for p in products}
        at = {p[0]: 4 * i for i, p in enumerate(products)}
        g_of = [slice(GROUP * j, GROUP * (j + 1)) for j in range(GROUPS)]

        def bank(name, j):
            return banks[(at[name] + j) % 8]

        block = ctx.enter_context(nc.Block())
        small = [n for n in loads if n != "xT"]

        @block.sync
        def _(sp):
            sp.dma_start(t["vecs"][:, :], a["vecs"]).then_inc(loaded.sem, 16)
            sp.dma_start(xT[:, :], a["xT"]).then_inc(loaded_x.sem, 16)
            for name in small:
                if name != "vecs":
                    sp.dma_start(t[name][:, :], a[name]).then_inc(loaded.sem, 16)

        @block.tensor
        def _(pe):
            pe.wait_ge(loaded.sem, 16 * len(small))
            for i, (name, w, moving, (r0, r1), ready, _free) in enumerate(products):
                m = w.shape[1]
                for j in range(GROUPS):
                    pe.wait_ge(ready.sem, ready.after(j))
                    if i >= 2:
                        freed = products[i - 2][5]
                        pe.wait_ge(freed.sem, freed.after(j))
                    nc.tensor.matmul(bank(name, j)[0:m, :], w[r0:r1, :], moving[r0:r1, g_of[j]],
                                     start=True, stop=True).then_inc(done[name].sem, 1)

        @block.vector
        def _(dve):
            dve.wait_ge(loaded_x.sem, 16)
            dve.wait_ge(loaded.sem, 16 * len(small))
            for s in range(B):
                lo_, hi = s * T, (s + 1) * T
                nc.vector.tensor_scalar(xx[:, lo_:lo_ + 1], xT[:, lo_:lo_ + 1], -1.0, None, ALU.mult).then_inc(xx_made.sem, 1)
                nc.vector.tensor_tensor(xx[:, lo_ + 1:hi], xT[:, lo_:hi - 1], xT[:, lo_ + 1:hi],
                                        ALU.subtract).then_inc(xx_made.sem, 1)
            dve.wait_ge(xx_made.sem, 2 * B)
            for j in range(GROUPS):
                nc.vector.scalar_tensor_tensor(out=mix[:, g_of[j]], in0=xx[:, g_of[j]], scalar=vecs[:, V_MAAX:V_MAAX + 1],
                                               in1=xT[:, g_of[j]], op0=ALU.mult, op1=ALU.add).then_inc(mix_made.sem, 1)
            for g in range(4):
                for j in range(GROUPS):
                    dve.wait_ge(done[f"maa{g}"].sem, j + 1)
                    nc.vector.scalar_tensor_tensor(out=xm[g][:, g_of[j]], in0=bank(f"maa{g}", j)[:, :],
                                                   scalar=vecs[:, V_MAA + g:V_MAA + g + 1], in1=xx[:, g_of[j]],
                                                   op0=ALU.add, op1=ALU.mult).then_inc(xm_scaled[g].sem, 1)
            for j in range(GROUPS):
                dve.wait_ge(done["kk"].sem, j + 1)
                dve.wait_ge(k_made.sem, k_made.after(j))
                nc.vector.tensor_tensor(t["kkraw"][:, g_of[j]], bank("kk", j)[:, :], t["k"][:, g_of[j]],
                                        ALU.add).then_inc(kk_made.sem, 1)

        @block.gpsimd
        def _(pool):
            for g in range(4):
                for j in range(GROUPS):
                    pool.wait_ge(xm_scaled[g].sem, j + 1)
                    nc.gpsimd.tensor_tensor(out=xm[g][:, g_of[j]], in0=xm[g][:, g_of[j]], in1=xT[:, g_of[j]],
                                            op=ALU.add).then_inc(xm_made[g].sem, 1)

        @block.scalar
        def _(act):
            act.wait_ge(loaded.sem, 16 * len(small))

            def read_out(name, out, func, made, rows=(0, P), bias=None):
                r0, r1 = rows
                for j in range(GROUPS):
                    act.wait_ge(done[name].sem, j + 1)
                    b = 0.0 if bias is None else vecs[r0:r1, bias:bias + 1]
                    nc.scalar.activation(out[r0:r1, g_of[j]], bank(name, j)[r0:r1, :], func, bias=b).then_inc(made.sem, 1)

            read_out("lo", lo, ACT.Tanh, lo_made)
            read_out("r", t["r"], ACT.Copy, r_made)
            read_out("g1", gt, ACT.Tanh, gt_made)
            for j in range(GROUPS):
                act.wait_ge(done["xwa"].sem, j + 1)
                nc.scalar.activation(h1[0:64, g_of[j]], bank("xwa", j)[0:64, :], ACT.Tanh).then_inc(h1_made.sem, 1)
                nc.scalar.activation(h1[64:P, g_of[j]], bank("xwa", j)[64:P, :], ACT.Copy).then_inc(h1_made.sem, 1)
            read_out("k", t["k"], ACT.Copy, k_made)
            for j in range(GROUPS):
                act.wait_ge(done["xk"].sem, j + 1)
                nc.scalar.activation(h2[0:32, g_of[j]], bank("xk", j)[0:32, :], ACT.Tanh).then_inc(h2_made.sem, 1)
                nc.scalar.activation(h2[32:64, g_of[j]], bank("xk", j)[32:64, :], ACT.Copy).then_inc(h2_made.sem, 1)
            read_out("v", t["v"], ACT.Copy, v_made)
            read_out("g2", t["g"], ACT.Copy, g_made)
            for j in range(GROUPS):
                act.wait_ge(done["z"].sem, j + 1)
                nc.scalar.activation(t["z"][:, g_of[j]], bank("z", j)[:, :], ACT.Identity,
                                     bias=vecs[:, V_DECAY:V_DECAY + 1]).then_inc(z_made.sem, 1)
                nc.scalar.activation(t["w"][:, g_of[j]], bank("z", j)[:, :], ACT.Sigmoid,
                                     bias=vecs[:, V_DECAY:V_DECAY + 1]).then_inc(z_made.sem, 1)
            read_out("a", t["a"], ACT.Sigmoid, a_made, bias=V_AAAAA)
            read_out("ma", t["ma"], ACT.Sigmoid, ma_made, bias=V_MISCA)
            read_out("mk", t["mk"], ACT.Sigmoid, mk_made, bias=V_MISCK)


def build_gates(nc, t, banks, vk):
    with PhaseSignals(nc) as sems, ExitStack() as ctx:
        def sig(name, **kw):
            return Signal(sems, name, **kw)

        vecs = t["vecs"]
        e, sp_ = (ctx.enter_context(nc.sbuf_tensor(n, [P, N], F32)) for n in ("gate_e", "gate_sp"))
        sq, norm = e, sp_
        squared, floored, ss_product, log_made, decay_made = sig("kk_squared"), sig("floored"), sig("ss_product"), sig("log_made"), sig("decay_made")
        kk_norm, soft, act_step = sig("kk_norm"), sig("soft"), sig("act_step")
        gain_made, k_scaled, key_gain = sig("gain_made"), sig("k_scaled"), sig("key_gain")
        v_spread, vk_made = sig("v_spread"), sig("vk_made")
        block = ctx.enter_context(nc.Block())
        g_of = [slice(GROUP * j, GROUP * (j + 1)) for j in range(GROUPS)]

        @block.scalar
        def _(act):
            nc.scalar.activation(sq[:, :], t["kkraw"][:, :], ACT.Square).then_inc(squared.sem, 1)
            for j in range(GROUPS):
                act.wait_ge(floored.sem, j + 1)
                nc.scalar.activation(norm[:, g_of[j]], norm[:, g_of[j]], ACT.Ln).then_inc(log_made.sem, 1)
            act.wait_ge(log_made.sem, GROUPS)
            nc.scalar.activation(norm[:, :], norm[:, :], ACT.Exp, scale=-0.5).then_inc(kk_norm.sem, 1)
            nc.scalar.activation(t["w"][:, :], t["w"][:, :], ACT.Exp, scale=-float(np.exp(-0.5))).then_inc(decay_made.sem, 1)
            nc.scalar.activation(e[:, :], t["z"][:, :], ACT.Abs).then_inc(act_step.sem, 1)
            act.wait_ge(act_step.sem, 1)
            nc.scalar.activation(e[:, :], e[:, :], ACT.Exp, scale=-1.0).then_inc(act_step.sem, 1)
            act.wait_ge(act_step.sem, 2)
            nc.scalar.activation(e[:, :], e[:, :], ACT.Ln, bias=vecs[:, V_ONE:V_ONE + 1]).then_inc(act_step.sem, 1)
            act.wait_ge(soft.sem, 3)
            nc.scalar.activation(e[:, :], e[:, :], ACT.Exp, scale=-1.0).then_inc(key_gain.sem, 1)

        @block.tensor
        def _(pe):
            pe.wait_ge(squared.sem, 1)
            for j in range(GROUPS):
                nc.tensor.matmul(banks[j][:, :], t["headones"][:, :], sq[:, g_of[j]], start=True, stop=True).then_inc(ss_product.sem, 1)
            for i in range(HS):
                for j in range(GROUPS):
                    n = i * GROUPS + j
                    if n >= 4:
                        pe.wait_ge(vk_made.sem, n - 3)
                    nc.tensor.matmul(banks[4 + n % 4][:, :], t["spread"][:, P * i:P * (i + 1)], t["v"][:, g_of[j]],
                                     start=True, stop=True).then_inc(v_spread.sem, 1)

        @block.vector
        def _(dve):
            for j in range(GROUPS):
                dve.wait_ge(ss_product.sem, j + 1)
                nc.vector.tensor_scalar(norm[:, g_of[j]], banks[j][:, :], NORM_FLOOR ** 2, None, ALU.max).then_inc(floored.sem, 1)
            nc.vector.tensor_scalar(vk[:, 0:N], t["a"][:, :], -1.0, 1.0, ALU.mult, ALU.add).then_inc(gain_made.sem, 1)
            dve.wait_ge(gain_made.sem, 1)
            nc.vector.tensor_tensor(vk[:, 0:N], vk[:, 0:N], t["ma"][:, :], ALU.mult).then_inc(gain_made.sem, 1)
            dve.wait_ge(gain_made.sem, 2)
            nc.vector.tensor_tensor(vk[:, 0:N], vk[:, 0:N], t["a"][:, :], ALU.add).then_inc(gain_made.sem, 1)
            dve.wait_ge(gain_made.sem, 3)
            nc.vector.tensor_tensor(t["k"][:, :], t["k"][:, :], vk[:, 0:N], ALU.mult).then_inc(k_scaled.sem, 1)
            dve.wait_ge(kk_norm.sem, 1)
            nc.vector.tensor_tensor(t["kkraw"][:, :], t["kkraw"][:, :], norm[:, :], ALU.mult).then_inc(kk_norm.sem, 1)
            dve.wait_ge(kk_norm.sem, 2)
            nc.vector.scalar_tensor_tensor(out=t["b"][:, :], in0=t["kkraw"][:, :], scalar=-1.0, in1=t["a"][:, :],
                                           op0=ALU.mult, op1=ALU.mult).then_inc(kk_norm.sem, 1)
            dve.wait_ge(act_step.sem, 3)
            nc.vector.tensor_scalar(t["z"][:, :], t["z"][:, :], -1.0, 0.0, ALU.mult, ALU.max).then_inc(soft.sem, 1)
            dve.wait_ge(soft.sem, 1)
            nc.vector.tensor_tensor(e[:, :], e[:, :], t["z"][:, :], ALU.add).then_inc(soft.sem, 1)
            dve.wait_ge(soft.sem, 2)
            nc.vector.scalar_tensor_tensor(out=e[:, :], in0=e[:, :], scalar=0.5, in1=t["mk"][:, :],
                                           op0=ALU.add, op1=ALU.mult).then_inc(soft.sem, 1)
            dve.wait_ge(key_gain.sem, 1)
            dve.wait_ge(k_scaled.sem, 1)
            nc.vector.tensor_tensor(t["k"][:, :], t["k"][:, :], e[:, :], ALU.mult).then_inc(k_scaled.sem, 1)
            dve.wait_ge(k_scaled.sem, 2)
            per = GROUP // CHUNK
            view = vk[:, :].rearrange("p (l i c) -> p l i c", i=HS, c=CHUNKS)
            for i in range(HS):
                for j in range(GROUPS):
                    n = i * GROUPS + j
                    dve.wait_ge(v_spread.sem, n + 1)
                    nc.vector.tensor_tensor(view[:, :, i, per * j:per * (j + 1)],
                                            banks[4 + n % 4][:, :].rearrange("p (c l) -> p l c", l=CHUNK),
                                            t["k"][:, g_of[j]].rearrange("p (c l) -> p l c", l=CHUNK),
                                            ALU.mult).then_inc(vk_made.sem, 1)


def build_scan(nc, t, banks, vk, state):
    with PhaseSignals(nc) as sems, ExitStack() as ctx:
        def sig(name, **kw):
            return Signal(sems, name, **kw)

        W = HS * CHUNKS
        at_end = (CHUNK - 1) % 2
        ahead = ctx.enter_context(nc.sbuf_tensor("sc_ahead", [P, 2, W], F32))
        states = (ahead, state) if at_end else (state, ahead)
        m, sw, m2, ub = (ctx.enter_context(nc.sbuf_tensor(n, [P, 2, W], F32)) for n in ("sc_m", "sc_sw", "sc_m2", "sc_ub"))
        s_set = sig("s_set", per=2)
        s_new = [sig(f"s_new{p}", credit=1) for p in range(2)]
        s_kk = [sig(f"s_kk{p}", credit=1) for p in range(2)]
        u_product = [sig(f"u_product{p}", credit=1) for p in range(2)]
        ub_made = [sig(f"ub_made{p}", credit=1) for p in range(2)]
        decayed = [sig(f"decayed{p}") for p in range(2)]
        s_sum = sig("s_sum")
        s_r = [sig(f"s_r{p}", credit=1) for p in range(2)]
        y_product = [sig(f"y_product{p}", credit=1) for p in range(2)]
        y_read = [sig(f"y_read{p}", credit=1) for p in range(2)]
        block = ctx.enter_context(nc.Block())

        def step(name, l):
            v = t[name][:, :].rearrange("p (c l) -> p l c", l=CHUNK)[:, ds(l, 1), :]
            return v.to_broadcast([P, HS, CHUNKS])

        def rows(buf, p):
            return buf[:, p, :].rearrange("p (r c) -> p r c", c=CHUNKS)

        y_of = (t["y"], t["zy"])

        def unrolled(engine, stage):
            with engine.Fori(0, CHUNK - 4, 2) as k:
                for odd in range(2):
                    stage(k + 2 + odd, odd)

        @block.vector
        def _(dve):
            nc.vector.memset(states[1][:, 0, :], 0.0).then_inc(s_set.sem, 1)
            nc.vector.tensor_copy(rows(states[1], 1), t["rowmask"][:, :].unsqueeze(2).to_broadcast([P, HS, CHUNKS])).then_inc(s_set.sem, 1)
            dve.wait_ge(s_set.sem, 2)
            for p in range(2):
                for s in (s_new[p], s_kk[p], ub_made[p]):
                    nc.vector.engine_nop().then_inc(s.sem, 1)
            nc.vector.engine_nop().then_inc(s_r[1].sem, 1)

            def times_kk(p, l, odd):
                dve.wait_ge(s_new[p].sem, s_new[p].after(l - 1))
                dve.wait_ge(u_product[p].sem, u_product[p].after(l - 1))
                nc.vector.tensor_tensor(rows(m, p), rows(states[1 - odd], p), step("kkraw", l), ALU.mult).then_inc(s_kk[p].sem, 1)

            def add_vk(l):
                dve.wait_ge(decayed[0].sem, decayed[0].after(l))
                nc.vector.tensor_tensor(sw[:, 0, :], sw[:, 0, :], vk[:, ds(l * W, W)], ALU.add).then_inc(s_sum.sem, 1)

            def times_b(p, l):
                dve.wait_ge(u_product[p].sem, u_product[p].after(l))
                nc.vector.tensor_tensor(rows(ub, p), banks[p][:, :].rearrange("p (r c) -> p r c", c=CHUNKS),
                                        step("b", l), ALU.mult).then_inc(ub_made[p].sem, 1)

            def renew(p, l, odd):
                dve.wait_ge(ub_made[p].sem, ub_made[p].after(l))
                if p == 0:
                    dve.wait_ge(s_sum.sem, s_sum.after(l))
                else:
                    dve.wait_ge(decayed[p].sem, decayed[p].after(l))
                dve.wait_ge(s_r[p].sem, s_r[p].after(l - 2))
                nc.vector.tensor_tensor(states[odd][:, p, :], sw[:, p, :], ub[:, p, :], ALU.add).then_inc(s_new[p].sem, 1)

            def times_r(l, odd):
                dve.wait_ge(s_new[1].sem, s_new[1].after(l))
                dve.wait_ge(y_product[1].sem, y_product[1].after(l - 1))
                nc.vector.tensor_tensor(rows(m2, 1), rows(states[odd], 1), step("r", l), ALU.mult).then_inc(s_r[1].sem, 1)

            def stage(l, odd, first=False):
                times_kk(1, l, odd)
                times_kk(0, l + 1, 1 - odd)
                if not first:
                    times_r(l - 1, 1 - odd)
                add_vk(l + 1)
                times_b(1, l)
                times_b(0, l + 1)
                renew(1, l, odd)
                renew(0, l + 1, 1 - odd)

            times_kk(0, 0, 0)
            add_vk(0)
            times_b(0, 0)
            renew(0, 0, 0)
            stage(0, 0, first=True)
            stage(1, 1)
            unrolled(dve, stage)
            stage(CHUNK - 2, 0)
            times_kk(1, CHUNK - 1, 1)
            times_r(CHUNK - 2, 0)
            times_b(1, CHUNK - 1)
            renew(1, CHUNK - 1, 1)
            times_r(CHUNK - 1, 1)

        @block.gpsimd
        def _(pool):
            carry = sems.carrier(pool, "pool_carried")
            nc.gpsimd.engine_nop().then_inc(s_r[0].sem, 1)
            pool.wait_ge(s_set.sem, 2)

            def decay(p, l, odd):
                pool.wait_ge(s_new[p].sem, s_new[p].after(l - 1))
                carry()
                nc.gpsimd.tensor_tensor(out=rows(sw, p), in0=rows(states[1 - odd], p), in1=step("w", l), op=ALU.mult).then_inc(decayed[p].sem, 1)

            def times_r(l, odd):
                pool.wait_ge(s_new[0].sem, s_new[0].after(l))
                pool.wait_ge(y_product[0].sem, y_product[0].after(l - 1))
                carry()
                nc.gpsimd.tensor_tensor(out=rows(m2, 0), in0=rows(states[odd], 0), in1=step("r", l), op=ALU.mult).then_inc(s_r[0].sem, 1)

            def stage(l, odd):
                decay(0, l + 1, 1 - odd)
                decay(1, l, odd)
                times_r(l, odd)

            decay(0, 0, 0)
            for l in range(2):
                stage(l, l)
            unrolled(pool, stage)
            stage(CHUNK - 2, 0)
            decay(1, CHUNK - 1, 1)
            times_r(CHUNK - 1, 1)

        @block.tensor
        def _(pe):
            for p in range(2):
                nc.tensor.drain().then_inc(u_product[p].sem, 1)
                nc.tensor.drain().then_inc(y_product[p].sem, 1)

            def products_u(p, l):
                pe.wait_ge(s_kk[p].sem, s_kk[p].after(l))
                pe.wait_ge(ub_made[p].sem, ub_made[p].after(l - 1))
                nc.tensor.matmul(banks[p][:, :], t["headones"][:, :], m[:, p, :], start=True, stop=True).then_inc(u_product[p].sem, 1)

            def products_y(p, l):
                pe.wait_ge(s_r[p].sem, s_r[p].after(l))
                pe.wait_ge(y_read[p].sem, y_read[p].after(l - 1))
                for i in range(HS):
                    last = nc.tensor.matmul(banks[2 + p][:, 0:CHUNKS], t["collect"][:, P * i:P * (i + 1)],
                                            m2[:, p, CHUNKS * i:CHUNKS * (i + 1)], start=(i == 0), stop=(i == HS - 1))
                last.then_inc(y_product[p].sem, 1)

            def stage(l):
                products_u(1, l)
                products_u(0, l + 1)
                for p in range(2):
                    products_y(p, l - 1)

            products_u(0, 0)
            products_u(1, 0)
            products_u(0, 1)
            with pe.Fori(0, CHUNK - 2) as k:
                stage(k + 1)
            products_u(1, CHUNK - 1)
            for l in (CHUNK - 2, CHUNK - 1):
                for p in range(2):
                    products_y(p, l)

        @block.scalar
        def _(act):
            for p in range(2):
                nc.scalar.drain().then_inc(y_read[p].sem, 1)
            with act.Fori(0, CHUNK) as l:
                for p in range(2):
                    act.wait_ge(y_product[p].sem, y_product[p].after(l))
                    out = y_of[p][:, :].rearrange("p (c l) -> p l c", l=CHUNK)[:, ds(l, 1), :]
                    nc.scalar.activation(out, banks[2 + p][:, 0:CHUNKS].unsqueeze(1), ACT.Copy).then_inc(y_read[p].sem, 1)


def build_mix_output(nc, a, t, banks, state, x_mid, x_all):
    with PhaseSignals(nc) as sems, ExitStack() as ctx:
        def sig(name, **kw):
            return Signal(sems, name, **kw)

        vecs, y = t["vecs"], t["y"]
        spreadG, prop = (ctx.enter_context(nc.sbuf_tensor(n, [P, CHUNKS, P], F32)) for n in ("spreadG", "prop"))
        start = ctx.enter_context(nc.sbuf_tensor("start", [P, CHUNKS, HS], F32))
        stats = ctx.enter_context(nc.sbuf_tensor("ln_stats", [P, BLOCKS, 6], F32))
        mv = ctx.enter_context(nc.sbuf_tensor("ln_mv", [P, BLOCKS, 2], F32))
        x_tok = ctx.enter_context(nc.sbuf_tensor("x_tok_sb", [P, BLOCKS, C], F32))
        yc, ysq, bonus = t["z"], t["w"], t["kkraw"]
        EIGHT = 8
        expanded, turned, prop_read = sig("expanded"), sig("turned"), sig("prop_read")
        start_set, chain_product, started = sig("start_set"), sig("chain_product"), sig("started")
        s_expanded, y_part, y_full = sig("s_expanded"), sig("y_part"), sig("y_full")
        mean_product, centred, y_squared, var_product, y_log = (sig(n) for n in ("mean_product", "centred", "y_squared", "var_product", "y_log"))
        y_recip, y_step, rk_made, rk_product = sig("y_recip"), sig("y_step"), sig("rk_made"), sig("rk_product")
        bonus_made, gated, o_product, summed = sig("bonus_made"), sig("gated"), sig("o_product"), sig("summed")
        stat_step, ln_root, ln_recip, normed, copied, x_loaded = (sig(n) for n in ("stat_step", "ln_root", "ln_recip", "normed", "copied", "x_loaded"))
        g_of = [slice(GROUP * j, GROUP * (j + 1)) for j in range(GROUPS)]
        hm = t["headmask"][:, :].unsqueeze(1).unsqueeze(3).to_broadcast([P, EIGHT, HEADS, HS])
        block = ctx.enter_context(nc.Block())

        @block.sync
        def _(sp):
            sp.dma_start(x_tok[:, :, :], a["x_tok"]).then_inc(x_loaded.sem, 16)

        @block.gpsimd
        def _(pool):
            nc.gpsimd.tensor_tensor(out=bonus[:, :], in0=t["r"][:, :], in1=t["k"][:, :], op=ALU.mult).then_inc(rk_made.sem, 1)
            pool.wait_ge(rk_made.sem, 1)
            nc.gpsimd.tensor_scalar(bonus[:, :], bonus[:, :], vecs[:, V_FAAAA:V_FAAAA + 1], None, ALU.mult).then_inc(rk_made.sem, 1)
            for n in range(BLOCKS):
                pool.wait_ge(normed.sem, n + 1)
                nc.gpsimd.tensor_copy(x_all[:, n, :], x_mid[:, n, :]).then_inc(copied.sem, 1)

        @block.vector
        def _(dve):
            G = state[:, 1, :].rearrange("p (r c) -> p c r", c=CHUNKS)
            for e in range(CHUNKS // EIGHT):
                cs = slice(EIGHT * e, EIGHT * (e + 1))
                nc.vector.tensor_tensor(spreadG[:, cs, :].rearrange("p c (h r) -> p c h r", h=HEADS),
                                        G[:, cs, :].unsqueeze(2).to_broadcast([P, EIGHT, HEADS, HS]), hm,
                                        ALU.mult).then_inc(expanded.sem, 1)
            for s in range(B):
                nc.vector.memset(start[:, s * SEQ_CHUNKS, :], 0.0).then_inc(start_set.sem, 1)
            H = state[:, 0, :].rearrange("p (r c) -> p c r", c=CHUNKS)
            for n in range(SEQ_CHUNKS - 1):
                for s in range(B):
                    c = s * SEQ_CHUNKS + n
                    dve.wait_ge(chain_product.sem, B * n + s + 1)
                    nc.vector.tensor_tensor(start[:, c + 1, :], banks[6 + s][:, 0:HS], H[:, c, :], ALU.add).then_inc(started.sem, 1)
                if (n + 2) % EIGHT:
                    continue
                dve.wait_ge(start_set.sem, B)
                dve.wait_ge(started.sem, B * (n + 1))
                dve.wait_ge(turned.sem, CHUNKS)
                for s in range(B):
                    cs = slice(s * SEQ_CHUNKS + n + 2 - EIGHT, s * SEQ_CHUNKS + n + 2)
                    nc.vector.tensor_tensor(spreadG[:, cs, :].rearrange("p c (h r) -> p c h r", h=HEADS),
                                        start[:, cs, :].unsqueeze(2).to_broadcast([P, EIGHT, HEADS, HS]), hm,
                                        ALU.mult).then_inc(s_expanded.sem, 1)
            for j in range(GROUPS):
                dve.wait_ge(y_part.sem, B * (j % (GROUPS // B)) + j // (GROUPS // B) + 1)
                nc.vector.tensor_tensor(y[:, g_of[j]], banks[j][:, :], y[:, g_of[j]], ALU.add).then_inc(y_full.sem, 1)
            for j in range(GROUPS):
                dve.wait_ge(mean_product.sem, j + 1)
                dve.wait_ge(y_full.sem, j + 1)
                nc.vector.scalar_tensor_tensor(out=yc[:, g_of[j]], in0=banks[4 + j % 2][:, :], scalar=-1.0 / HS,
                                               in1=y[:, g_of[j]], op0=ALU.mult, op1=ALU.add).then_inc(centred.sem, 1)
            for j in range(GROUPS):
                dve.wait_ge(rk_product.sem, j + 1)
                nc.vector.tensor_tensor(bonus[:, g_of[j]], banks[4 + j % 2][:, :], t["v"][:, g_of[j]],
                                        ALU.mult).then_inc(bonus_made.sem, 1)
            dve.wait_ge(y_recip.sem, 1)
            nc.vector.tensor_tensor(yc[:, :], yc[:, :], ysq[:, :], ALU.mult).then_inc(y_step.sem, 1)
            dve.wait_ge(y_step.sem, 1)
            nc.vector.tensor_scalar(yc[:, :], yc[:, :], vecs[:, V_LNW:V_LNW + 1], vecs[:, V_LNB:V_LNB + 1],
                                    ALU.mult, ALU.add).then_inc(y_step.sem, 1)
            dve.wait_ge(y_step.sem, 2)
            dve.wait_ge(bonus_made.sem, GROUPS)
            nc.vector.tensor_tensor(yc[:, :], yc[:, :], bonus[:, :], ALU.add).then_inc(y_step.sem, 1)
            dve.wait_ge(y_step.sem, 3)
            nc.vector.tensor_tensor(yc[:, :], yc[:, :], t["g"][:, :], ALU.mult).then_inc(gated.sem, 1)
            dve.wait_ge(x_loaded.sem, 16)
            for n in range(BLOCKS):
                dve.wait_ge(o_product.sem, n + 1)
                nc.vector.tensor_tensor(x_tok[:, n, :], banks[n % 4][:, 0:C], x_tok[:, n, :], ALU.add).then_inc(summed.sem, 1)
                dve.wait_ge(summed.sem, n + 1)
                nc.vector.bn_stats(stats[:, n, :], x_tok[:, n, :]).then_inc(stat_step.sem, 1)
                dve.wait_ge(stat_step.sem, 2 * n + 1)
                nc.vector.bn_aggr(mv[:, n, :], stats[:, n, :]).then_inc(stat_step.sem, 1)
            dve.wait_ge(ln_root.sem, 1)
            nc.vector.reciprocal(mv[:, :, 1], mv[:, :, 1]).then_inc(ln_recip.sem, 1)
            dve.wait_ge(ln_recip.sem, 1)
            for n in range(BLOCKS):
                nc.vector.tensor_scalar(x_mid[:, n, :], x_tok[:, n, :], mv[:, n, 0:1], mv[:, n, 1:2],
                                        ALU.subtract, ALU.mult).then_inc(normed.sem, 1)

        @block.tensor
        def _(pe):
            for c in range(CHUNKS):
                pe.wait_ge(expanded.sem, c // EIGHT + 1)
                if c >= 4 and c % 4 == 0 and c >= 16:
                    pe.wait_ge(prop_read.sem, c // 4 - 3)
                nc.tensor.transpose(banks[(c // 4) % 4][:, P * (c % 4):P * (c % 4 + 1)], spreadG[:, c, :], t["ident"][:, :]).then_inc(turned.sem, 1)
            pe.wait_ge(start_set.sem, B)
            pe.wait_ge(prop_read.sem, CHUNKS // 4)

            def part_of_starts(c):
                at = CHUNK * c
                mm = nc.tensor.matmul(banks[at // GROUP][:, at % GROUP:at % GROUP + CHUNK], spreadG[:, c, :],
                                      t["zy"][:, at:at + CHUNK], start=True, stop=True)
                if (at + CHUNK) % GROUP == 0:
                    mm.then_inc(y_part.sem, 1)

            for n in range(SEQ_CHUNKS - 1 + EIGHT + 1):
                for s in range(B):
                    c = s * SEQ_CHUNKS + n
                    if n < SEQ_CHUNKS - 1:
                        if n:
                            pe.wait_ge(started.sem, B * (n - 1) + s + 1)
                        nc.tensor.matmul(banks[6 + s][:, 0:HS], prop[:, c, :], start[:, c, :], start=True, stop=True).then_inc(chain_product.sem, 1)
                for s in range(B):
                    if n >= EIGHT:
                        pe.wait_ge(s_expanded.sem, B * ((n - EIGHT) // EIGHT + 1))
                        part_of_starts(s * SEQ_CHUNKS + n - EIGHT)
            for j in range(GROUPS):
                pe.wait_ge(y_full.sem, j + 1)
                if j >= 2:
                    pe.wait_ge(centred.sem, j - 1)
                nc.tensor.matmul(banks[4 + j % 2][:, :], t["headones"][:, :], y[:, g_of[j]], start=True, stop=True).then_inc(mean_product.sem, 1)
            for j in range(GROUPS):
                pe.wait_ge(y_squared.sem, j + 1)
                nc.tensor.matmul(banks[j][:, :], t["headones"][:, :], ysq[:, g_of[j]], start=True, stop=True).then_inc(var_product.sem, 1)
            pe.wait_ge(rk_made.sem, 2)
            for j in range(GROUPS):
                pe.wait_ge(centred.sem, j + 3 if j < 2 else GROUPS)
                if j >= 2:
                    pe.wait_ge(bonus_made.sem, j - 1)
                nc.tensor.matmul(banks[4 + j % 2][:, :], t["headones"][:, :], bonus[:, g_of[j]], start=True, stop=True).then_inc(rk_product.sem, 1)
            pe.wait_ge(gated.sem, 1)
            for n in range(BLOCKS):
                if n >= 4:
                    pe.wait_ge(summed.sem, n - 3)
                nc.tensor.matmul(banks[n % 4][:, 0:C], yc[:, P * n:P * (n + 1)], t["w_o"][:, :], start=True, stop=True).then_inc(o_product.sem, 1)

        @block.scalar
        def _(act):
            for q in range(CHUNKS // 4):
                act.wait_ge(turned.sem, 4 * q + 4)
                nc.scalar.activation(prop[:, 4 * q:4 * q + 4, :].rearrange("p c m -> p (c m)"), banks[q % 4][:, :], ACT.Copy).then_inc(prop_read.sem, 1)
            for j in range(GROUPS):
                act.wait_ge(centred.sem, j + 1)
                nc.scalar.activation(ysq[:, g_of[j]], yc[:, g_of[j]], ACT.Square).then_inc(y_squared.sem, 1)
            for j in range(GROUPS):
                act.wait_ge(var_product.sem, j + 1)
                nc.scalar.activation(ysq[:, g_of[j]], banks[j][:, :], ACT.Ln, scale=1.0 / HS,
                                     bias=vecs[:, V_YEPS:V_YEPS + 1]).then_inc(y_log.sem, 1)
            act.wait_ge(y_log.sem, GROUPS)
            nc.scalar.activation(ysq[:, :], ysq[:, :], ACT.Exp, scale=-0.5).then_inc(y_recip.sem, 1)
            act.wait_ge(stat_step.sem, 2 * BLOCKS)
            nc.scalar.activation(mv[:, :, 1], mv[:, :, 1], ACT.Sqrt, bias=vecs[:, V_LNEPS:V_LNEPS + 1]).then_inc(ln_root.sem, 1)


def build_mixing(nc, a, banks, x_mid, x_all):
    with ExitStack() as ctx:
        def sb(name, shape):
            return ctx.enter_context(nc.sbuf_tensor(name + "_sb", list(shape), F32))

        t = mix_inputs(sb)
        loads = list(t)
        for name in ("r", "k", "v", "g", "z", "w", "a", "ma", "mk", "kkraw"):
            t[name] = sb(name, (P, N))
        state = sb("state", (P, 2, HS * CHUNKS))
        build_projections(nc, a, t, loads, banks)
        t["b"], t["y"], t["zy"] = t["ma"], t["a"], t["mk"]
        with nc.sbuf_tensor("vk_sb", [P, CHUNK * HS * CHUNKS], F32) as vk:
            build_gates(nc, t, banks, vk)
            build_scan(nc, t, banks, vk, state)
        build_mix_output(nc, a, t, banks, state, x_mid, x_all)


LAG = 6


def build_stream(nc, a, banks, x_all, masks_f):
    with PhaseSignals(nc) as sems, ExitStack() as ctx:
        def sb(name, shape, dt=F32):
            return ctx.enter_context(nc.sbuf_tensor(name, list(shape), dt))

        def sig(name, per=1, credit=2):
            return Signal(sems, name, per, credit)

        def two(name, shape):
            return [sb(f"{name}{u}", shape) for u in range(2)]

        ident, ident16 = sb("st_ident", (P, P)), sb("st_ident16", (P, P), BF16)
        mask16 = sb("mask16", (P, SEQ_BLOCKS, 2 * WINDOW), BF16)
        tables = sb("tables", (P, SEQ_BLOCKS, 4 * DH))
        follows = sb("follows", (P, SEQ_BLOCKS))
        norm_gb = sb("norm_gb", (P, 2 * DEPTH))
        eps = sb("eps", (P, 1))
        wqkv, wo, w1 = sb("wqkv", (P, 2 * 3 * INNER)), sb("wo", (P, 2 * INNER)), sb("w1", (P, 2 * 2 * FF))
        w2, b1, b2 = sb("w2", (P, 2 * len(FF_PARTS) * C)), sb("b1", (P, 2 * 2 * FF)), sb("b2", (P, 2 * C))
        qk_gain = sb("qk_gain", (P, 2 * 4 * DH))
        x_in, xs_T, gains, v_tok = two("x_in", (P, C)), two("xs_T", (P, P)), two("gains", (P, 4, DH)), two("v_tok", (P, INNER))
        edge, edge2 = two("edge", (P, 1)), two("edge2", (P, 1))
        squares, turnedhalf = sb("squares", (P, 2 * INNER)), sb("turnedhalf", (P, 2 * INNER))
        qk, rnorm = two("qk", (P, 2 * INNER)), two("rnorm", (P, 2 * AH))
        q_T, k_T = two("q_T", (P, PAIRS, P)), two("k_T", (P, PAIRS, WINDOW + P))
        v_win = two("v_win", (P, WINDOWS, INNER // 2))
        probs, p_T, o_T = two("probs", (P, PAIRS, 2, DH)), two("p_T", (P, PAIRS, P)), two("o_T", (P, PAIRS, P))
        peak, total = two("peak", (P, 2, PAIRS)), two("total", (P, AH))
        x_att = two("x_att", (P, C))
        ms_T, xn, xn_T, x_res = two("ms_T", (P, P)), two("xn", (P, C)), two("xn_T", (P, P)), two("x_res", (P, C))
        stats, mv = two("st_stats", (P, 6)), two("st_mv", (P, 2))
        gate, act_in = two("gate", (P, FF)), two("act_in", (P, FF))
        ff_T = two("ff_T", (P, len(FF_PARTS), P))

        const_loaded, masks_made = sig("const_loaded", credit=0), sig("masks_made", credit=0)
        LAYER_LOADS = 7
        w_loaded = sig("w_loaded", per=16 * LAYER_LOADS, credit=0)
        cleared = sig("cleared", credit=0)
        x_ready = sig("x_ready", credit=BLOCKS)
        x_taken, gains_made, x_turned, xs_made = sig("x_taken"), sig("gains_made"), sig("x_turned"), sig("xs_made", per=4)
        qk_product, v_product, squared = sig("qk_product", per=4), sig("st_v_product", per=2), sig("squared", per=4)
        rotated, rot_added, ss_made, root_made = sig("rotated", per=12), sig("rot_added", per=2), sig("ss_made"), sig("st_root_made")
        rnorm_made, qk_made, v_read = sig("rnorm_made", per=2), sig("qk_made", per=2), sig("v_read", per=2)
        v_placed = sig("v_placed", per=16 * 16)
        q_turned, qT_made, k_turned, kT_made, halo_made = sig("q_turned", per=2), sig("qT_made", per=2), sig("k_turned", per=2), sig("kT_made", per=2), sig("halo_made")
        s_product, peak_made, shifted, exp_made = sig("s_product"), sig("peak_made", per=2), sig("shifted", per=2), sig("exp_made")
        total_made, p_turned, pT_made = sig("total_made", per=2), sig("p_turned", per=2), sig("pT_made", per=2)
        o_product, o_made, o_turned, oT_made = sig("st_o_product"), sig("o_made", per=2), sig("o_turned", per=2), sig("oT_made", per=2)
        y_product, att_sum = sig("st_y_product"), sig("att_sum")
        m_turned, ms_made, ms_back = sig("m_turned"), sig("ms_made", per=4), sig("ms_back")
        stat_made, sigma_made, rsigma_made, x_normed = sig("stat_made", per=2), sig("sigma_made"), sig("rsigma_made"), sig("x_normed")
        xn_turned, xnT_made, gate_product, a_product = sig("xn_turned"), sig("xnT_made"), sig("up_gate_product"), sig("up_a_product")
        gate_biased, gate_made, a_biased, ff_made = sig("gate_biased"), sig("gate_made"), sig("a_biased"), sig("ff_made")
        ff_turned, ffT_made, y2_product, res_made = sig("ff_turned"), sig("ffT_made", per=2), sig("y2_product"), sig("res_made")

        Q_BANKS, K_BANKS, V_BANKS, X_BANK, FF_BANK = (banks[1], banks[2]), (banks[0], banks[1]), (banks[2], banks[0]), banks[0], banks[3]
        QK_BANKS = Q_BANKS + K_BANKS
        S_BANKS, T_BANKS = (banks[4], banks[5]), (banks[6], banks[7])
        FF_T_FULL = sum(m == P for _, m in FF_PARTS)
        TAIL = FF_PARTS[-1][1]
        TURNED = {"q": (S_BANKS, q_turned), "k": (T_BANKS, k_turned), "p": (T_BANKS, p_turned), "o": (T_BANKS, o_turned)}

        def layer_cols(tile, n, width, at=0, size=None):
            slot = (n // BLOCKS) % 2
            return tile[:, ds(slot * width + at, width if size is None else size)]

        def by_head(ap):
            return ap.rearrange("p (h d) -> p h d", d=DH)

        block = ctx.enter_context(nc.Block())


        def stream(engine, turn):
            def run(n, parity, peeled):
                def at(lag, stage, *which):
                    if not peeled or 0 <= n - lag < STREAM:
                        stage(n - lag, (parity + lag) % 2, *which)
                turn(at)

            for n in range(LAG):
                run(n, n % 2, True)
            with engine.Fori(LAG, STREAM, 2) as n:
                for parity in range(2):
                    run(n + parity, parity, False)
            for n in range(STREAM, STREAM + LAG):
                run(n, n % 2, True)

        @block.sync
        def _(sp):
            carry = sems.carrier(sp, "st_sp_carried")
            for tile, name in ((ident, "ident"), (masks_f, "mask"), (follows, "follows"), (norm_gb, "norm_gb"), (eps, "eps")):
                sp.dma_start(tile[:, :], a[name]).then_inc(const_loaded.sem, 16)
            sp.dma_start(tables[:, :, :], a["tables"]).then_inc(const_loaded.sem, 16)

            def load_layer(layer, slot):
                for tile, name, width in ((wqkv, "wqkv", 3 * INNER), (wo, "wo", INNER), (w1, "w1", 2 * FF), (w2, "w2", len(FF_PARTS) * C)):
                    sp.dma_start(tile[:, slot * width:(slot + 1) * width], a[name][ds(layer, 1), :, :].rearrange("l p n -> p (l n)")).then_inc(w_loaded.sem, 16)
                for tile, name, width in ((b1, "b1", 2 * FF), (b2, "b2", C), (qk_gain, "qk_gain", 4 * DH)):
                    sp.dma_start(tile[:, slot * width:(slot + 1) * width],
                                 a[name][ds(layer, 1), :].to_broadcast([P, width])).then_inc(w_loaded.sem, 16)

            def place_v(n, u):
                sp.wait_ge(v_read.sem, v_read.after(n))
                carry()
                sp.wait_ge(o_product.sem, o_product.after(n - 2))
                carry()
                sp.wait_ge(v_placed.sem, v_placed.after(n - 1))
                for p in range(2):
                    cols = slice(p * INNER // 2, (p + 1) * INNER // 2)
                    for w in range(WINDOWS):
                        own, before = slice(WINDOW * w, WINDOW * (w + 1)), slice(WINDOW * (w - 1), WINDOW * w)
                        sp.dma_start(v_win[u][DH * p + WINDOW:DH * (p + 1), w, :], v_tok[u][own, cols]).then_inc(v_placed.sem, 16)
                        src = v_tok[u][before, cols] if w else v_tok[1 - u][P - WINDOW:P, cols]
                        sp.dma_start(v_win[u][DH * p:DH * p + WINDOW, w, :], src).then_inc(v_placed.sem, 16)

            sp.wait_ge(cleared.sem, 4)
            sp.sem_inc(v_placed.sem, v_placed.credit * v_placed.per)
            load_layer(0, 0)
            sp.wait_ge(w_loaded.sem, w_loaded.after(0))
            load_layer(1, 1)
            EARLY = 4
            for n in range(BLOCKS):
                place_v(n, n % 2)
            with sp.Fori(0, DEPTH // 2 - 1) as pair:
                for half in range(2):
                    layer = pair * 2 + 1 + half
                    for n in range(EARLY):
                        place_v(layer * BLOCKS + n, n % 2)
                    sp.wait_ge(x_ready.sem, x_ready.after(layer * BLOCKS - 1))
                    sp.wait_ge(w_loaded.sem, w_loaded.after(layer))
                    carry()
                    load_layer(layer + 1, half)
                    for n in range(EARLY, BLOCKS):
                        place_v(layer * BLOCKS + n, n % 2)
            for n in range(BLOCKS):
                place_v((DEPTH - 1) * BLOCKS + n, n % 2)

        @block.gpsimd
        def _(pool):
            carry = sems.carrier(pool, "st_pool_carried")
            for s in (x_taken, gains_made, rot_added, qk_made, halo_made, res_made, ff_made):
                for _ in range(s.credit * s.per):
                    nc.gpsimd.engine_nop().then_inc(s.sem, 1)
            pool.wait_ge(const_loaded.sem, 16 * 6)
            nc.gpsimd.tensor_copy(ident16[:, :], ident[:, :]).then_inc(masks_made.sem, 1)
            nc.gpsimd.tensor_copy(mask16[:, :, :].rearrange("p n k -> p (n k)"), masks_f[:, :]).then_inc(masks_made.sem, 1)
            pool.wait_ge(cleared.sem, 4)

            def take(n, u):
                pool.wait_ge(x_ready.sem, x_ready.after(n - BLOCKS))
                pool.wait_ge(x_turned.sem, x_turned.after(n - 2))
                carry()
                nc.gpsimd.tensor_copy(x_in[u][:, :], x_all[:, ds(n % BLOCKS, 1), :].rearrange("p n c -> p (n c)")).then_inc(x_taken.sem, 1)

            def table_gains(n, u):
                pool.wait_ge(w_loaded.sem, w_loaded.after(n // BLOCKS))
                pool.wait_ge(rotated.sem, rotated.after(n - 2))
                carry()
                nc.gpsimd.tensor_tensor(out=gains[u][:, :, :].rearrange("p f d -> p (f d)"),
                                        in0=tables[:, ds(n % SEQ_BLOCKS, 1), :].rearrange("p n c -> p (n c)"),
                                        in1=layer_cols(qk_gain, n, 4 * DH), op=ALU.mult).then_inc(gains_made.sem, 1)

            def add_turned(n, u, i):
                half = slice(INNER * i, INNER * (i + 1))
                pool.wait_ge(rotated.sem, rotated.after(n, 6 * (i + 1)))
                nc.gpsimd.tensor_tensor(out=qk[u][:, half], in0=qk[u][:, half], in1=turnedhalf[:, half], op=ALU.add).then_inc(rot_added.sem, 1)

            def unit(n, u, i):
                half = slice(INNER * i, INNER * (i + 1))
                pool.wait_ge(rnorm_made.sem, rnorm_made.after(n))
                pool.wait_ge(rot_added.sem, rot_added.after(n, i + 1))
                nc.gpsimd.tensor_tensor(out=by_head(qk[u][:, half]), in0=by_head(qk[u][:, half]),
                                        in1=rnorm[u][:, AH * i:AH * (i + 1)].unsqueeze(2).to_broadcast([P, AH, DH]),
                                        op=ALU.mult).then_inc(qk_made.sem, 1)

            def halo(n, u):
                pool.wait_ge(kT_made.sem, kT_made.after(n - 1))
                pool.wait_ge(s_product.sem, s_product.after(n - 2))
                carry()
                nc.gpsimd.tensor_tensor(out=k_T[u][:, :, 0:WINDOW], in0=k_T[1 - u][:, :, P:P + WINDOW],
                                        in1=follows[:, ds(n % SEQ_BLOCKS, 1)].unsqueeze(2).to_broadcast([P, PAIRS, WINDOW]),
                                        op=ALU.mult).then_inc(halo_made.sem, 1)

            def residual(n, u):
                pool.wait_ge(att_sum.sem, att_sum.after(n))
                pool.wait_ge(x_ready.sem, x_ready.after(n - 2))
                carry()
                nc.gpsimd.tensor_tensor(out=x_res[u][:, :], in0=x_att[u][:, :], in1=layer_cols(b2, n, C), op=ALU.add).then_inc(res_made.sem, 1)

            def glu(n, u):
                pool.wait_ge(gate_made.sem, gate_made.after(n))
                pool.wait_ge(a_biased.sem, a_biased.after(n))
                nc.gpsimd.tensor_tensor(out=gate[u][:, :], in0=gate[u][:, :], in1=act_in[u][:, :], op=ALU.mult).then_inc(ff_made.sem, 1)

            def turn(at):
                at(2, add_turned, 0)
                at(3, unit, 1)
                at(1, table_gains)
                at(0, take)
                at(5, glu)
                at(3, halo)
                at(2, add_turned, 1)
                at(2, unit, 0)
                at(4, residual)

            stream(pool, turn)

        @block.tensor
        def _(pe):
            carry = sems.carrier(pe, "st_pe_carried")
            for s in (x_turned, qk_product, v_product, q_turned, k_turned, s_product, p_turned, o_product, o_turned, y_product,
                      m_turned, ms_back, xn_turned, gate_product, a_product, ff_turned, y2_product):
                for _ in range(s.credit * s.per):
                    nc.tensor.drain().then_inc(s.sem, 1)
            pe.wait_ge(masks_made.sem, 2)

            def turn_x(n, u):
                pe.wait_ge(x_taken.sem, x_taken.after(n))
                pe.wait_ge(v_read.sem, v_read.after(n - 1))
                nc.tensor.transpose(X_BANK[:, 0:P], x_in[u][:, :], ident[:, :]).then_inc(x_turned.sem, 1)

            def project_qk(n, u, i):
                if i == 0:
                    pe.wait_ge(xs_made.sem, xs_made.after(n))
                    pe.wait_ge(w_loaded.sem, w_loaded.after(n // BLOCKS))
                    pe.wait_ge(rotated.sem, rotated.after(n - 1))
                if i == 1:
                    pe.wait_ge(v_read.sem, v_read.after(n - 1, 1))
                if i == 3:
                    pe.wait_ge(rotated.sem, rotated.after(n, 3))
                nc.tensor.matmul(QK_BANKS[i][:, :], xs_T[u][:, :], layer_cols(wqkv, n, 3 * INNER, 512 * i, 512),
                                 start=True, stop=True).then_inc(qk_product.sem, 1)

            def project_v(n, u, i):
                pe.wait_ge(rotated.sem, rotated.after(n, 6 + 3 * i))
                nc.tensor.matmul(V_BANKS[i][:, :], xs_T[u][:, :], layer_cols(wqkv, n, 3 * INNER, 2 * INNER + 512 * i, 512),
                                 start=True, stop=True).then_inc(v_product.sem, 1)

            def transposes(which, n, source):
                outs, turned = TURNED[which]
                for i in range(PAIRS):
                    mm = nc.tensor.transpose(outs[i // 4][:, P * (i % 4):P * (i % 4 + 1)], source[:, P * i:P * (i + 1)], ident[:, :])
                    if i % 4 == 3:
                        mm.then_inc(turned.sem, 1)

            def turn_q(n, u):
                pe.wait_ge(qk_made.sem, qk_made.after(n, 1))
                pe.wait_ge(att_sum.sem, att_sum.after(n - 1))
                transposes("q", n, qk[u][:, 0:INNER])

            def turn_k(n, u):
                pe.wait_ge(qk_made.sem, qk_made.after(n, 2))
                pe.wait_ge(oT_made.sem, oT_made.after(n - 1))
                transposes("k", n, qk[u][:, INNER:2 * INNER])

            def scores(n, u):
                pe.wait_ge(qT_made.sem, qT_made.after(n))
                pe.wait_ge(kT_made.sem, kT_made.after(n))
                pe.wait_ge(halo_made.sem, halo_made.after(n))
                mask = mask16[:, ds(n % SEQ_BLOCKS, 1), :].to_broadcast([P, PAIRS, 2 * WINDOW])
                for p in range(2):
                    nc.tensor.matmul(S_BANKS[p][:, :].rearrange("p (a k) -> p a k", a=PAIRS), ident16[:, :], mask,
                                     start=True, stop=False, skip_group_check=True)
                for a_ in range(PAIRS):
                    for w in range(WINDOWS):
                        for p in range(2):
                            at, rows = WINDOW * w, slice(DH * p, DH * (p + 1))
                            mm = nc.tensor.matmul(S_BANKS[p][at:at + WINDOW, 2 * WINDOW * a_:2 * WINDOW * (a_ + 1)],
                                                  q_T[u][rows, a_, at:at + WINDOW], k_T[u][rows, a_, at:at + 2 * WINDOW],
                                                  start=False, stop=True, skip_group_check=True)
                mm.then_inc(s_product.sem, 1)

            def turn_p(n, u):
                pe.wait_ge(exp_made.sem, exp_made.after(n))
                pe.wait_ge(kT_made.sem, kT_made.after(n))
                transposes("p", n, probs[u][:, :, :, :].rearrange("p a b d -> p (a b d)"))

            def outputs(n, u):
                pe.wait_ge(pT_made.sem, pT_made.after(n))
                pe.wait_ge(shifted.sem, shifted.after(n))
                pe.wait_ge(v_placed.sem, v_placed.after(n))
                carry()
                for a_ in range(PAIRS):
                    for w in range(WINDOWS):
                        for p in range(2):
                            at, rows = WINDOW * w, slice(DH * p, DH * (p + 1))
                            mm = nc.tensor.matmul(S_BANKS[p][at:at + WINDOW, DH * a_:DH * (a_ + 1)],
                                                  p_T[u][rows, a_, at:at + WINDOW], v_win[u][rows, w, DH * a_:DH * (a_ + 1)],
                                                  start=True, stop=True, skip_group_check=True)
                mm.then_inc(o_product.sem, 1)

            def turn_o(n, u):
                pe.wait_ge(o_made.sem, o_made.after(n))
                transposes("o", n, probs[u][:, :, :, :].rearrange("p a b d -> p (a b d)"))

            def project_o(n, u):
                pe.wait_ge(oT_made.sem, oT_made.after(n))
                for i in range(PAIRS):
                    mm = nc.tensor.matmul(S_BANKS[0][:, 0:C], o_T[u][:, i, :], layer_cols(wo, n, INNER, C * i, C),
                                          start=(i == 0), stop=(i == PAIRS - 1))
                mm.then_inc(y_product.sem, 1)

            def turn_m(n, u):
                pe.wait_ge(att_sum.sem, att_sum.after(n))
                pe.wait_ge(x_ready.sem, x_ready.after(n - 1))
                nc.tensor.transpose(FF_BANK[:, 0:P], x_att[u][:, :], ident[:, :]).then_inc(m_turned.sem, 1)

            def turn_back(n, u):
                pe.wait_ge(ms_made.sem, ms_made.after(n))
                nc.tensor.transpose(FF_BANK[:, 0:P], ms_T[u][:, :], ident[:, :]).then_inc(ms_back.sem, 1)

            def turn_xn(n, u):
                pe.wait_ge(x_normed.sem, x_normed.after(n))
                nc.tensor.transpose(FF_BANK[:, 0:P], xn[u][:, :], ident[:, :]).then_inc(xn_turned.sem, 1)

            def up_gate(n, u):
                pe.wait_ge(xnT_made.sem, xnT_made.after(n))
                nc.tensor.matmul(FF_BANK[:, 0:FF], xn_T[u][:, :], layer_cols(w1, n, 2 * FF, FF, FF), start=True, stop=True).then_inc(gate_product.sem, 1)

            def up_a(n, u):
                pe.wait_ge(gate_biased.sem, gate_biased.after(n))
                nc.tensor.matmul(FF_BANK[:, 0:FF], xn_T[u][:, :], layer_cols(w1, n, 2 * FF, 0, FF), start=True, stop=True).then_inc(a_product.sem, 1)

            def turn_ff(n, u):
                pe.wait_ge(ff_made.sem, ff_made.after(n))
                for i, (at, m) in enumerate(FF_PARTS):
                    mm = nc.tensor.transpose(FF_BANK[0:m, P * i:P * (i + 1)], gate[u][:, at:at + m], ident[:, :])
                mm.then_inc(ff_turned.sem, 1)

            def down(n, u):
                pe.wait_ge(ffT_made.sem, ffT_made.after(n))
                for i, (_, m) in enumerate(FF_PARTS):
                    w = layer_cols(w2, n, len(FF_PARTS) * C, C * i, C)
                    mm = nc.tensor.matmul(FF_BANK[:, 0:C], ff_T[u][0:m, i, :], w[0:m], start=(i == 0), stop=(i == len(FF_PARTS) - 1))
                mm.then_inc(y2_product.sem, 1)

            def turn(at):
                at(4, outputs)
                at(5, turn_xn)
                at(2, project_v, 1)
                at(5, up_gate)
                at(4, turn_o)
                at(5, up_a)
                at(4, project_o)
                at(1, turn_x)
                at(3, turn_q)
                at(3, turn_k)
                at(5, turn_ff)
                at(1, project_qk, 0)
                at(3, scores)
                at(1, project_qk, 1)
                at(1, project_qk, 2)
                at(5, down)
                at(4, turn_m)
                at(1, project_qk, 3)
                at(3, turn_p)
                at(1, project_v, 0)
                at(4, turn_back)

            stream(pe, turn)

        @block.scalar
        def _(act):
            for s in (xs_made, squared, root_made, v_read, qT_made, kT_made, exp_made, pT_made, oT_made,
                      ms_made, sigma_made, xnT_made, gate_made, ffT_made):
                for _ in range(s.credit * s.per):
                    nc.scalar.drain().then_inc(s.sem, 1)
            act.wait_ge(const_loaded.sem, 16 * 6)
            act.wait_ge(cleared.sem, 4)

            def shift(n, u, bank, out, last, made):
                nc.scalar.activation(out[u][0:64, :], bank[0:64, 0:P], ACT.Copy).then_inc(made.sem, 1)
                nc.scalar.activation(out[u][64:P, 1:P], bank[64:P, 0:P - 1], ACT.Copy).then_inc(made.sem, 1)
                act.wait_ge(made.sem, made.after(n - 1))
                nc.scalar.activation(out[u][64:P, 0:1], last[1 - u][64:P, :], ACT.Copy,
                                     scale=follows[64:P, ds(n % SEQ_BLOCKS, 1)]).then_inc(made.sem, 1)
                nc.scalar.activation(last[u][64:P, :], bank[64:P, P - 1:P], ACT.Copy).then_inc(made.sem, 1)

            def shift_x(n, u):
                act.wait_ge(x_turned.sem, x_turned.after(n))
                act.wait_ge(v_product.sem, v_product.after(n - 2))
                shift(n, u, X_BANK, xs_T, edge, xs_made)

            def square(n, u, i):
                act.wait_ge(ss_made.sem, ss_made.after(n - 1))
                act.wait_ge(qk_product.sem, qk_product.after(n, i + 1))
                nc.scalar.activation(squares[:, 512 * i:512 * (i + 1)], QK_BANKS[i][:, :], ACT.Square).then_inc(squared.sem, 1)

            def root(n, u):
                act.wait_ge(ss_made.sem, ss_made.after(n))
                nc.scalar.activation(rnorm[u][:, :], rnorm[u][:, :], ACT.Sqrt).then_inc(root_made.sem, 1)

            def read_v(n, u, i):
                act.wait_ge(v_placed.sem, v_placed.after(n - 1))
                act.wait_ge(v_product.sem, v_product.after(n, i + 1))
                out = v_tok[u][:, :].rearrange("p (b a d) -> p b a d", b=2, d=DH)[:, :, 4 * i:4 * i + 4, :]
                nc.scalar.activation(out, V_BANKS[i][:, :].rearrange("p (a b d) -> p b a d", b=2, d=DH), ACT.Copy).then_inc(v_read.sem, 1)

            def read_q(n, u):
                act.wait_ge(s_product.sem, s_product.after(n - 2))
                read_turned(n, u, S_BANKS, q_turned, q_T, qT_made)

            def read_k(n, u):
                act.wait_ge(s_product.sem, s_product.after(n - 2))
                act.wait_ge(halo_made.sem, halo_made.after(n - 1))
                for i in range(2):
                    act.wait_ge(k_turned.sem, k_turned.after(n, i + 1))
                    nc.scalar.activation(k_T[u][:, 4 * i:4 * i + 4, WINDOW:], T_BANKS[i][:, :].rearrange("p (a t) -> p a t", a=4), ACT.Copy).then_inc(kT_made.sem, 1)

            def exponent(n, u):
                act.wait_ge(shifted.sem, shifted.after(n))
                pr = probs[u][:, :, :, :].rearrange("p a b d -> p (a b d)")
                nc.scalar.activation(pr, pr, ACT.Exp, scale=QK_SCALE).then_inc(exp_made.sem, 1)

            def read_turned(n, u, banks_, turned, out, made):
                for i in range(2):
                    act.wait_ge(turned.sem, turned.after(n, i + 1))
                    nc.scalar.activation(out[u][:, 4 * i:4 * i + 4, :].rearrange("p a t -> p (a t)"), banks_[i][:, :], ACT.Copy).then_inc(made.sem, 1)

            def read_p(n, u):
                act.wait_ge(o_product.sem, o_product.after(n - 2))
                read_turned(n, u, T_BANKS, p_turned, p_T, pT_made)

            def read_oT(n, u):
                act.wait_ge(y_product.sem, y_product.after(n - 2))
                read_turned(n, u, T_BANKS, o_turned, o_T, oT_made)

            def shift_m(n, u):
                act.wait_ge(m_turned.sem, m_turned.after(n))
                act.wait_ge(ms_back.sem, ms_back.after(n - 2))
                shift(n, u, FF_BANK, ms_T, edge2, ms_made)

            def sigma(n, u):
                act.wait_ge(stat_made.sem, stat_made.after(n))
                nc.scalar.activation(mv[u][:, 1:2], mv[u][:, 1:2], ACT.Sqrt, bias=eps[:, :]).then_inc(sigma_made.sem, 1)

            def affine(n, u):
                act.wait_ge(xn_turned.sem, xn_turned.after(n))
                act.wait_ge(a_product.sem, a_product.after(n - 2))
                layer = n // BLOCKS
                nc.scalar.activation(xn_T[u][:, :], FF_BANK[:, 0:P], ACT.Identity, scale=norm_gb[:, ds(layer, 1)],
                                     bias=norm_gb[:, ds(layer + DEPTH, 1)]).then_inc(xnT_made.sem, 1)

            def gelu(n, u):
                act.wait_ge(gate_biased.sem, gate_biased.after(n))
                nc.scalar.activation(gate[u][:, :], gate[u][:, :], ACT.Gelu).then_inc(gate_made.sem, 1)

            def read_ff(n, u):
                act.wait_ge(ff_turned.sem, ff_turned.after(n))
                act.wait_ge(y2_product.sem, y2_product.after(n - 2))
                nc.scalar.activation(ff_T[u][:, 0:FF_T_FULL, :].rearrange("p i t -> p (i t)"), FF_BANK[:, 0:FF_T_FULL * P], ACT.Copy).then_inc(ffT_made.sem, 1)
                nc.scalar.activation(ff_T[u][0:TAIL, FF_T_FULL, :], FF_BANK[0:TAIL, FF_T_FULL * P:(FF_T_FULL + 1) * P], ACT.Copy).then_inc(ffT_made.sem, 1)

            def turn(at):
                at(1, read_v, 1)
                at(3, read_oT)
                at(4, gelu)
                at(0, shift_x)
                at(2, read_q)
                at(2, read_k)
                at(1, root)
                at(0, square, 0)
                at(4, read_ff)
                at(0, square, 1)
                at(2, exponent)
                at(0, square, 2)
                at(3, shift_m)
                at(2, read_p)
                at(3, sigma)
                at(0, read_v, 0)
                at(0, square, 3)
                at(3, affine)

            stream(act, turn)

        @block.vector
        def _(dve):
            carry = sems.carrier(dve, "st_dve_carried")
            for tile in (edge[1][64:P, :], edge2[1][64:P, :], v_tok[1][P - WINDOW:P, :]):
                nc.vector.memset(tile, 0.0).then_inc(cleared.sem, 1)
            nc.vector.memset(k_T[1][:, :, P:P + WINDOW], 0.0).then_inc(cleared.sem, 1)
            for s in (x_ready, rotated, ss_made, rnorm_made, peak_made, shifted, total_made, o_made, att_sum, stat_made, rsigma_made,
                      x_normed, gate_biased, a_biased):
                for _ in range(s.credit * s.per):
                    nc.vector.engine_nop().then_inc(s.sem, 1)

            def rotate(n, u, i):
                dve.wait_ge(squared.sem, squared.after(n, i + 1))
                if i == 0:
                    dve.wait_ge(gains_made.sem, gains_made.after(n))
                    dve.wait_ge(k_turned.sem, k_turned.after(n - 2))
                if i % 2 == 0:
                    dve.wait_ge(rot_added.sem, rot_added.after(n - 1, i // 2 + 1))
                cols, src = slice(512 * i, 512 * (i + 1)), by_head(QK_BANKS[i][:, :])
                cos, sin = (gains[u][:, 2 * (i // 2) + f:2 * (i // 2) + f + 1, :] for f in range(2))
                nc.vector.tensor_tensor(by_head(qk[u][:, cols]), src, cos.to_broadcast([P, 8, DH]), ALU.mult).then_inc(rotated.sem, 1)
                half = DH // 2
                for f in range(2):
                    to, frm = slice(half * f, half * (f + 1)), slice(half * (1 - f), half * (2 - f))
                    nc.vector.tensor_tensor(by_head(turnedhalf[:, cols])[:, :, to], src[:, :, frm],
                                            sin[:, :, to].to_broadcast([P, 8, half]), ALU.mult).then_inc(rotated.sem, 1)

            def norms(n, u):
                dve.wait_ge(squared.sem, squared.after(n))
                dve.wait_ge(qk_made.sem, qk_made.after(n - 2))
                nc.vector.reduce_sum(rnorm[u][:, :], by_head(squares[:, :]), AX).then_inc(ss_made.sem, 1)

            def rnorms(n, u):
                dve.wait_ge(root_made.sem, root_made.after(n))
                nc.vector.tensor_scalar(rnorm[u][:, :], rnorm[u][:, :], NORM_FLOOR, None, ALU.max).then_inc(rnorm_made.sem, 1)
                dve.wait_ge(rnorm_made.sem, rnorm_made.after(n, 1))
                nc.vector.reciprocal(rnorm[u][:, :], rnorm[u][:, :]).then_inc(rnorm_made.sem, 1)

            def peaks(n, u):
                dve.wait_ge(s_product.sem, s_product.after(n))
                dve.wait_ge(o_turned.sem, o_turned.after(n - 2))
                for p in range(2):
                    s = S_BANKS[p][:, :].rearrange("p (a k) -> p a k", a=PAIRS)
                    nc.vector.reduce_max(peak[u][:, p, :], s, AX).then_inc(peak_made.sem, 1)

            def shifts(n, u):
                for p in range(2):
                    s = S_BANKS[p][:, :].rearrange("p (a k) -> p a k", a=PAIRS)
                    dve.wait_ge(peak_made.sem, peak_made.after(n, p + 1))
                    nc.vector.tensor_tensor(probs[u][:, :, p, :], s, peak[u][:, p, :].unsqueeze(2).to_broadcast([P, PAIRS, DH]),
                                            ALU.subtract).then_inc(shifted.sem, 1)

            def totals(n, u):
                dve.wait_ge(exp_made.sem, exp_made.after(n))
                dve.wait_ge(o_made.sem, o_made.after(n - 2))
                nc.vector.reduce_sum(total[u][:, :], probs[u][:, :, :, :].rearrange("p a b d -> p (a b) d"), AX).then_inc(total_made.sem, 1)
                dve.wait_ge(total_made.sem, total_made.after(n, 1))
                nc.vector.reciprocal(total[u][:, :], total[u][:, :]).then_inc(total_made.sem, 1)

            def scale_outputs(n, u):
                dve.wait_ge(o_product.sem, o_product.after(n))
                dve.wait_ge(total_made.sem, total_made.after(n))
                for p in range(2):
                    rtotal = total[u][:, :].rearrange("p (a b) -> p a b", b=2)[:, :, p:p + 1]
                    nc.vector.tensor_tensor(probs[u][:, :, p, :], S_BANKS[p][:, :].rearrange("p (a d) -> p a d", d=DH),
                                            rtotal.to_broadcast([P, PAIRS, DH]), ALU.mult).then_inc(o_made.sem, 1)

            def add_attention(n, u):
                dve.wait_ge(y_product.sem, y_product.after(n))
                dve.wait_ge(res_made.sem, res_made.after(n - 2))
                dve.wait_ge(m_turned.sem, m_turned.after(n - 2))
                nc.vector.tensor_tensor(x_att[u][:, :], S_BANKS[0][:, 0:C],
                                        x_all[:, ds(n % BLOCKS, 1), :].rearrange("p n c -> p (n c)"), ALU.add).then_inc(att_sum.sem, 1)

            def moments(n, u):
                dve.wait_ge(ms_back.sem, ms_back.after(n))
                nc.vector.bn_stats(stats[u][:, :], FF_BANK[:, 0:C]).then_inc(stat_made.sem, 1)
                dve.wait_ge(stat_made.sem, stat_made.after(n, 1))
                carry()
                nc.vector.bn_aggr(mv[u][:, :], stats[u][:, :]).then_inc(stat_made.sem, 1)

            def norm_x(n, u):
                dve.wait_ge(sigma_made.sem, sigma_made.after(n))
                nc.vector.reciprocal(mv[u][:, 1:2], mv[u][:, 1:2]).then_inc(rsigma_made.sem, 1)
                dve.wait_ge(rsigma_made.sem, rsigma_made.after(n))
                nc.vector.tensor_scalar(xn[u][:, :], FF_BANK[:, 0:C], mv[u][:, 0:1], mv[u][:, 1:2],
                                        ALU.subtract, ALU.mult).then_inc(x_normed.sem, 1)

            def bias_gate(n, u):
                dve.wait_ge(gate_product.sem, gate_product.after(n))
                dve.wait_ge(ff_turned.sem, ff_turned.after(n - 2))
                nc.vector.tensor_tensor(gate[u][:, :], FF_BANK[:, 0:FF], layer_cols(b1, n, 2 * FF, FF, FF), ALU.add).then_inc(gate_biased.sem, 1)

            def bias_a(n, u):
                dve.wait_ge(a_product.sem, a_product.after(n))
                dve.wait_ge(ff_made.sem, ff_made.after(n - 2))
                nc.vector.tensor_tensor(act_in[u][:, :], FF_BANK[:, 0:FF], layer_cols(b1, n, 2 * FF, 0, FF), ALU.add).then_inc(a_biased.sem, 1)

            def add_ffn(n, u):
                dve.wait_ge(y2_product.sem, y2_product.after(n))
                dve.wait_ge(res_made.sem, res_made.after(n))
                nc.vector.tensor_tensor(x_all[:, ds(n % BLOCKS, 1), :].rearrange("p n c -> p (n c)"), FF_BANK[:, 0:C], x_res[u][:, :],
                                        ALU.add).then_inc(x_ready.sem, 1)

            def turn(at):
                at(2, rotate, 2)
                at(5, moments)
                at(5, norm_x)
                at(4, totals)
                at(4, scale_outputs)
                at(5, bias_gate)
                at(4, add_attention)
                at(5, bias_a)
                at(2, rotate, 3)
                at(2, norms)
                at(2, rnorms)
                at(1, rotate, 0)
                at(3, peaks)
                at(3, shifts)
                at(5, add_ffn)
                at(1, rotate, 1)

            stream(dve, turn)


def build_final(nc, banks, a, x_mid, x_all, out):
    with PhaseSignals(nc) as sems, ExitStack() as ctx:
        def sig(name):
            return Signal(sems, name)

        stats = ctx.enter_context(nc.sbuf_tensor("fi_stats", [P, BLOCKS, 6], F32))
        mv = ctx.enter_context(nc.sbuf_tensor("fi_mv", [P, BLOCKS, 2], F32))
        eps = ctx.enter_context(nc.sbuf_tensor("fi_eps", [P, 1], F32))
        added, counted, gathered, rooted, inverted, normed, loaded, stored = (
            sig(n) for n in ("fi_added", "fi_counted", "fi_gathered", "fi_rooted", "fi_inverted", "fi_normed", "fi_loaded", "fi_stored"))
        block = ctx.enter_context(nc.Block())

        @block.sync
        def _(sp):
            sp.dma_start(eps[:, :], a["eps"]).then_inc(loaded.sem, 16)
            halves = 2
            for h in range(halves):
                part = slice(BLOCKS // halves * h, BLOCKS // halves * (h + 1))
                sp.wait_ge(normed.sem, BLOCKS // halves * (h + 1))
                sp.dma_start(out.rearrange("(n p) c -> p n c", p=P)[:, part, :], x_all[:, part, :]).then_inc(stored.sem, 16)
            sp.wait_ge(stored.sem, 16 * halves)

        @block.vector
        def _(dve):
            nc.vector.tensor_tensor(x_all[:, :, :], x_all[:, :, :], x_mid[:, :, :], ALU.add).then_inc(added.sem, 1)
            dve.wait_ge(added.sem, 1)
            for n in range(BLOCKS):
                nc.vector.bn_stats(stats[:, n, :], x_all[:, n, :]).then_inc(counted.sem, 1)
            for n in range(BLOCKS):
                dve.wait_ge(counted.sem, n + 1)
                nc.vector.bn_aggr(mv[:, n, :], stats[:, n, :]).then_inc(gathered.sem, 1)
            dve.wait_ge(rooted.sem, 1)
            nc.vector.reciprocal(mv[:, :, 1], mv[:, :, 1]).then_inc(inverted.sem, 1)
            dve.wait_ge(inverted.sem, 1)
            for n in range(BLOCKS):
                nc.vector.tensor_scalar(x_all[:, n, :], x_all[:, n, :], mv[:, n, 0:1], mv[:, n, 1:2],
                                        ALU.subtract, ALU.mult).then_inc(normed.sem, 1)

        @block.scalar
        def _(act):
            act.wait_ge(loaded.sem, 16)
            act.wait_ge(gathered.sem, BLOCKS)
            nc.scalar.activation(mv[:, :, 1], mv[:, :, 1], ACT.Sqrt, bias=eps[:, :]).then_inc(rooted.sem, 1)


def build_program(nc, a, out):
    with ExitStack() as ctx:
        banks = [ctx.enter_context(nc.psum_tensor(f"bank{i}", [P, GROUP], F32)) for i in range(8)]
        x_mid, x_all = (ctx.enter_context(nc.sbuf_tensor(n, [P, BLOCKS, C], F32)) for n in ("x_mid", "x_all"))
        build_mixing(nc, a, banks, x_mid, x_all)
        with nc.sbuf_tensor("masks_f", [P, SEQ_BLOCKS * 2 * WINDOW], F32) as masks_f:
            build_stream(nc, a, banks, x_all, masks_f)
        build_final(nc, banks, a, x_mid, x_all, out)


def layouts(L):
    f = np.float32

    def asn(name, shape=None):
        v = np.asarray(L[name])
        return v if shape is None else v.reshape(shape)

    out = {}
    x = asn("L0_attn_x")
    out["xT"] = np.ascontiguousarray(x.reshape(N, C).T)
    out["x_tok"] = np.ascontiguousarray(x.reshape(BLOCKS, P, C).transpose(1, 0, 2))
    vecs = np.zeros((P, 16), f)
    vecs[:, V_MAAX] = asn("L0_attn_time_maa_x")
    vecs[:, V_MAA:V_MAA + 4] = asn("L0_attn_time_maa", (4, C)).T
    for col, name in ((V_DECAY, "time_decay"), (V_AAAAA, "time_aaaaa"), (V_MISCA, "time_misc_a"), (V_MISCK, "time_misc_k"),
                      (V_FAAAA, "time_faaaa"), (V_LNW, "ln_w"), (V_LNB, "ln_b")):
        vecs[:, col] = asn("L0_attn_" + name)
    vecs[:, V_ONE], vecs[:, V_YEPS], vecs[:, V_LNEPS] = 1.0, Y_EPS, LN_EPS
    out["vecs"] = vecs
    out["ident"] = np.eye(P, dtype=f)
    for name, src in (("w_lo", "maa_w1"), ("w_r", "Wr"), ("w_g1", "gate_w1"), ("w_k", "Wk"), ("w_v", "Wv"), ("w_o", "Wo")):
        out[name] = np.ascontiguousarray(asn("L0_attn_" + src).T)
    out["w_maa"] = np.ascontiguousarray(asn("L0_attn_maa_w2", (P, C)))
    out["w_g2"] = np.ascontiguousarray(asn("L0_attn_gate_w2"))
    w = np.zeros((P, P), f)
    w[:, 0:64], w[:, AAA_AT:AAA_AT + 16], w[:, MA_AT:MA_AT + 16] = (asn("L0_attn_" + n).T for n in ("decay_w1", "aaa_w1", "ma_w1"))
    out["w_xwa"] = w
    w = np.zeros((P, P), f)
    w[0:64], w[AAA_AT:AAA_AT + 16], w[MA_AT:MA_AT + 16] = (asn("L0_attn_" + n) for n in ("decay_w2", "aaa_w2", "ma_w2"))
    out["w_second"] = w
    w = np.zeros((P, 64), f)
    w[:, 0:16], w[:, MK_AT:MK_AT + 16] = (asn("L0_attn_" + n).T for n in ("kkk_w1", "mk_w1"))
    out["w_xk"] = w
    w = np.zeros((64, P), f)
    w[0:16], w[MK_AT:MK_AT + 16] = (asn("L0_attn_" + n) for n in ("kkk_w2", "mk_w2"))
    out["w_xk2"] = w
    head, row = np.arange(P) // HS, np.arange(P) % HS
    same = head[:, None] == head[None, :]
    out["headones"] = same.astype(f)
    out["spread"] = np.concatenate([(same & (row == i)[:, None]).astype(f) for i in range(HS)], 1)
    out["collect"] = np.concatenate([(same & (row == i)[None, :]).astype(f) for i in range(HS)], 1)
    out["headmask"] = (head[:, None] == np.arange(HEADS)[None, :]).astype(f)
    out["rowmask"] = (row[:, None] == np.arange(HS)[None, :]).astype(f)
    return out


def stream_layouts(L):
    f = np.float32
    out = {}

    def asn(name):
        return np.asarray(L["L0_ffn_" + name])

    out["wqkv"] = np.ascontiguousarray(asn("Wqkv"))
    out["wo"] = np.ascontiguousarray(asn("Wo").reshape(DEPTH, PAIRS, P, C).transpose(0, 2, 1, 3).reshape(DEPTH, P, INNER))
    out["w1"] = np.ascontiguousarray(asn("W1"))
    w2 = np.zeros((DEPTH, len(FF_PARTS) * P, C), f)
    w2[:, 0:FF] = asn("W2")
    out["w2"] = np.ascontiguousarray(w2.reshape(DEPTH, len(FF_PARTS), P, C).transpose(0, 2, 1, 3).reshape(DEPTH, P, len(FF_PARTS) * C))
    out["b1"], out["b2"] = np.ascontiguousarray(asn("b1")), np.ascontiguousarray(asn("b2"))
    qs, ks, half = asn("q_scale"), asn("k_scale"), DH // 2

    def swapped(v):
        return np.concatenate([v[:, half:], v[:, :half]], 1)

    out["qk_gain"] = np.ascontiguousarray(np.concatenate([qs, swapped(qs), ks, swapped(ks)], 1))
    out["norm_gb"] = np.ascontiguousarray(np.concatenate([asn("ln_g"), asn("ln_b")], 0).T)
    ar = np.arange(0, DH, 2, dtype=f)
    freqs = np.arange(T, dtype=f)[:, None] * (f(1.0) / f(10000.0) ** (ar / f(DH)))[None, :]
    base = (ar + f(0.4 * DH)) / f(1.4 * DH)
    scale = base[None, :] ** ((np.arange(T, dtype=f) - T // 2) / f(WINDOW // 2))[:, None]
    cos, sin = np.cos(freqs), np.sin(freqs)
    parts = []
    for s in (scale, f(1.0) / scale):
        parts += [cos * s, cos * s, -sin * s, sin * s]
    tab = np.concatenate(parts, 1).astype(f)
    out["tables"] = np.ascontiguousarray(tab.reshape(SEQ_BLOCKS, P, 4 * DH).transpose(1, 0, 2))
    i, j = (np.arange(P) % WINDOW)[:, None], np.arange(2 * WINDOW)[None, :]
    allowed = (j >= i) & (j <= i + WINDOW)
    mask = np.where(allowed, 0.0, MASKED).astype(f)
    full = np.repeat(mask[:, None, :], SEQ_BLOCKS, 1)
    full[0:WINDOW, 0, 0:WINDOW] = MASKED
    out["mask"] = np.ascontiguousarray(full.reshape(P, -1))
    follows = np.ones((P, SEQ_BLOCKS), f)
    follows[:, 0] = 0.0
    out["follows"] = follows
    out["eps"] = np.full((P, 1), LN_EPS, f)
    return out


def kernel(**inputs):
    from concourse import bacc
    from concourse.bass_utils import run_bass_kernel_spmd

    arrays = {**layouts(inputs), **stream_layouts(inputs)}
    nc = bacc.Bacc("TRN2", target_bir_lowering=False, num_devices=1)
    a = {name: nc.dram_tensor(f"in_{name}", list(v.shape), mybir.dt.from_np(v.dtype), kind="ExternalInput").ap()
         for name, v in arrays.items()}
    out = nc.dram_tensor("out", [N, C], F32, kind="ExternalOutput").ap()
    build_program(nc, a, out)
    r = run_bass_kernel_spmd(nc, [{f"in_{name}": v for name, v in arrays.items()}], core_ids=[0])
    return r.results[0]["out"].reshape(B, T, C)
```

```python
from contextlib import ExitStack

import numpy as np

import concourse.bass as bass
from concourse import mybir
from concourse.bass import ds

F32 = mybir.dt.float32
BF16 = mybir.dt.bfloat16
ALU = mybir.AluOpType
ACT = mybir.ActivationFunctionType
AX = mybir.AxisListType.X

P = 128
B, T, C = 2, 1024, 128
N = B * T
HEADS, HS = 16, 8
GROUP = 512
GROUPS = N // GROUP
CHUNK = 32
CHUNKS = N // CHUNK
SEQ_CHUNKS = T // CHUNK
Y_EPS, NORM_FLOOR, LN_EPS = 0.00064, 1e-12, 1e-5

DEPTH, DH, WINDOW = 6, 64, 32
AH = 16
INNER = AH * DH
PAIRS = AH // 2
FF = int(C * 4 * 2 / 3)
FF_PARTS = [(at, min(P, FF - at)) for at in range(0, FF, P)]
BLOCKS = N // P
SEQ_BLOCKS = T // P
WINDOWS = P // WINDOW
QK_SCALE = 8.0
MASKED = -1e30
STREAM = DEPTH * BLOCKS


class Signal:

    def __init__(self, signals, name, per=1, credit=0):
        self.sem, self.per, self.credit = signals.semaphore(name), per, credit

    def after(self, turn, part=None):
        return (turn + self.credit) * self.per + (self.per if part is None else part)


class PhaseSignals(ExitStack):

    def __init__(self, nc):
        super().__init__()
        self.nc, self.sems = nc, []

    def semaphore(self, name):
        self.sems.append(self.enter_context(self.nc.semaphore(name)))
        return self.sems[-1]

    def carrier(self, engine, name):
        sem = self.semaphore(name)
        return lambda: engine.sem_inc(sem, 1)

    def __exit__(self, *raised):
        if raised[0] is None:
            with self.nc.Block() as block:
                @block.sync
                def _(sp):
                    for sem in self.sems:
                        sp.sem_clear(sem)
        return super().__exit__(*raised)


def mix_inputs(sb):
    t = {}
    for name, shape in (("xT", (P, N)), ("vecs", (P, 16)), ("ident", (P, P)), ("w_lo", (P, P)), ("w_maa", (P, P)),
                        ("w_r", (P, P)), ("w_g1", (P, P)), ("w_g2", (P, P)), ("w_xwa", (P, P)), ("w_k", (P, P)),
                        ("w_xk", (P, 64)), ("w_v", (P, P)), ("w_second", (P, P)), ("w_xk2", (64, P)),
                        ("w_o", (P, P)), ("headones", (P, P)), ("spread", (P, HS * P)), ("collect", (P, HS * P)),
                        ("headmask", (P, HEADS)), ("rowmask", (P, HS))):
        t[name] = sb(name, shape)
    return t


V_MAAX, V_MAA, V_DECAY, V_AAAAA, V_MISCA, V_MISCK, V_FAAAA, V_LNW, V_LNB, V_ONE, V_YEPS, V_LNEPS = \
    0, 1, 5, 6, 7, 8, 9, 10, 11, 12, 13, 14
AAA_AT, MA_AT = 64, 96
MK_AT = 32


def build_projections(nc, a, t, loads, banks):
    with PhaseSignals(nc) as sems, ExitStack() as ctx:
        def sig(name, **kw):
            return Signal(sems, name, **kw)

        xx, mix, lo, gt, h1, h2 = (ctx.enter_context(nc.sbuf_tensor(n, [P, N], F32))
                                   for n in ("xx", "mix", "lo", "gt", "h1", "h2"))
        xm = [ctx.enter_context(nc.sbuf_tensor(f"xm{g}", [P, N], F32)) for g in range(4)]
        xT, vecs = t["xT"], t["vecs"]
        loaded = sig("p_loaded")
        loaded_x = sig("p_loaded_x")
        xx_made, mix_made, lo_made, gt_made = sig("xx_made"), sig("mix_made"), sig("lo_made"), sig("gt_made")
        h1_made, h2_made, k_made = sig("h1_made", per=2), sig("h2_made", per=2), sig("k_made")
        xm_scaled = [sig(f"xm_scaled{g}") for g in range(4)]
        xm_made = [sig(f"xm_made{g}") for g in range(4)]
        r_made, v_made, g_made, z_made = sig("r_made"), sig("v_made"), sig("g_made"), sig("z_made", per=2)
        a_made, ma_made, mk_made, kk_made = sig("a_made"), sig("ma_made"), sig("mk_made"), sig("kk_made")

        products = {"lo": (t["w_lo"], mix, (0, P), mix_made, lo_made),
                    "r": (t["w_r"], xm[0], (0, P), xm_made[0], r_made),
                    "g1": (t["w_g1"], xm[0], (0, P), xm_made[0], gt_made),
                    "xwa": (t["w_xwa"], xm[1], (0, P), xm_made[1], h1_made),
                    "k": (t["w_k"], xm[2], (0, P), xm_made[2], k_made),
                    "xk": (t["w_xk"], xm[2], (0, P), xm_made[2], h2_made),
                    "v": (t["w_v"], xm[3], (0, P), xm_made[3], v_made),
                    "g2": (t["w_g2"], gt, (0, P), gt_made, g_made),
                    "z": (t["w_second"], h1, (0, 64), h1_made, z_made),
                    "a": (t["w_second"], h1, (AAA_AT, AAA_AT + 16), h1_made, a_made),
                    "ma": (t["w_second"], h1, (MA_AT, MA_AT + 16), h1_made, ma_made),
                    "kk": (t["w_xk2"], h2, (0, 16), h2_made, kk_made),
                    "mk": (t["w_xk2"], h2, (MK_AT, MK_AT + 16), h2_made, mk_made)}
        products.update({f"maa{g}": (t["w_maa"], lo, (32 * g, 32 * g + 32), lo_made, xm_scaled[g]) for g in range(4)})
        MAA, FIRST = ("maa0", "maa1", "maa2", "maa3"), ("r", "g1", "xwa", "k", "xk", "v")
        SECOND = ("g2", "z", "a", "ma", "kk", "mk")
        order = [("lo", j) for j in range(GROUPS)]
        for names, j in ((MAA, 0), (MAA, 1), (FIRST, 0), (MAA, 2), (FIRST, 1), (SECOND, 0), (MAA, 3), (FIRST, 2),
                         (SECOND, 1), (FIRST, 3), (SECOND, 2), (SECOND, 3)):
            order += [(name, j) for name in names]
        done = {name: sig(f"{name}_product") for name in products}
        place = {what: i for i, what in enumerate(order)}
        g_of = [slice(GROUP * j, GROUP * (j + 1)) for j in range(GROUPS)]

        def bank(name, j):
            return banks[place[name, j] % 8]

        block = ctx.enter_context(nc.Block())
        small = [n for n in loads if n != "xT"]

        @block.sync
        def _(sp):
            sp.dma_start(t["vecs"][:, :], a["vecs"]).then_inc(loaded.sem, 16)
            sp.dma_start(xT[:, :], a["xT"]).then_inc(loaded_x.sem, 16)
            for name in small:
                if name != "vecs":
                    sp.dma_start(t[name][:, :], a[name]).then_inc(loaded.sem, 16)

        @block.tensor
        def _(pe):
            pe.wait_ge(loaded.sem, 16 * len(small))
            for i, (name, j) in enumerate(order):
                w, moving, (r0, r1), ready, _ = products[name]
                pe.wait_ge(ready.sem, ready.after(j))
                if i >= 8:
                    before, at = order[i - 8]
                    freed = products[before][4]
                    pe.wait_ge(freed.sem, freed.after(at))
                nc.tensor.matmul(bank(name, j)[0:w.shape[1], :], w[r0:r1, :], moving[r0:r1, g_of[j]],
                                 start=True, stop=True).then_inc(done[name].sem, 1)

        @block.vector
        def _(dve):
            dve.wait_ge(loaded_x.sem, 16)
            dve.wait_ge(loaded.sem, 16 * len(small))
            for s in range(B):
                lo_, hi = s * T, (s + 1) * T
                nc.vector.tensor_scalar(xx[:, lo_:lo_ + 1], xT[:, lo_:lo_ + 1], -1.0, None, ALU.mult).then_inc(xx_made.sem, 1)
                nc.vector.tensor_tensor(xx[:, lo_ + 1:hi], xT[:, lo_:hi - 1], xT[:, lo_ + 1:hi],
                                        ALU.subtract).then_inc(xx_made.sem, 1)
            dve.wait_ge(xx_made.sem, 2 * B)
            for j in range(GROUPS):
                nc.vector.scalar_tensor_tensor(out=mix[:, g_of[j]], in0=xx[:, g_of[j]], scalar=vecs[:, V_MAAX:V_MAAX + 1],
                                               in1=xT[:, g_of[j]], op0=ALU.mult, op1=ALU.add).then_inc(mix_made.sem, 1)

            def mix_in(j):
                for g in range(4):
                    dve.wait_ge(done[f"maa{g}"].sem, j + 1)
                    nc.vector.scalar_tensor_tensor(out=xm[g][:, g_of[j]], in0=bank(f"maa{g}", j)[:, :],
                                                   scalar=vecs[:, V_MAA + g:V_MAA + g + 1], in1=xx[:, g_of[j]],
                                                   op0=ALU.add, op1=ALU.mult).then_inc(xm_scaled[g].sem, 1)
                for g in (2, 3):
                    dve.wait_ge(xm_scaled[g].sem, j + 1)
                    nc.vector.tensor_tensor(xm[g][:, g_of[j]], xm[g][:, g_of[j]], xT[:, g_of[j]], ALU.add).then_inc(xm_made[g].sem, 1)

            def raw_kk(j):
                dve.wait_ge(done["kk"].sem, j + 1)
                dve.wait_ge(k_made.sem, k_made.after(j))
                nc.vector.tensor_tensor(t["kkraw"][:, g_of[j]], bank("kk", j)[:, :], t["k"][:, g_of[j]],
                                        ALU.add).then_inc(kk_made.sem, 1)

            for j in range(3):
                mix_in(j)
            raw_kk(0)
            mix_in(3)
            for j in range(1, GROUPS):
                raw_kk(j)

        @block.gpsimd
        def _(pool):
            for j in range(GROUPS):
                for g in (0, 1):
                    pool.wait_ge(xm_scaled[g].sem, j + 1)
                    nc.gpsimd.tensor_tensor(out=xm[g][:, g_of[j]], in0=xm[g][:, g_of[j]], in1=xT[:, g_of[j]],
                                            op=ALU.add).then_inc(xm_made[g].sem, 1)

        @block.scalar
        def _(act):
            nc.scalar.preload_act_table_set("sigmoid_and_others")
            act.wait_ge(loaded.sem, 16 * len(small))

            whole = (0, P)
            reads = {"lo": ([(lo, whole, ACT.Tanh, None)], lo_made), "r": ([(t["r"], whole, ACT.Copy, None)], r_made),
                     "g1": ([(gt, whole, ACT.Tanh, None)], gt_made),
                     "xwa": ([(h1, (0, 64), ACT.Tanh, None), (h1, (64, P), ACT.Copy, None)], h1_made),
                     "k": ([(t["k"], whole, ACT.Copy, None)], k_made),
                     "xk": ([(h2, (0, 32), ACT.Tanh, None), (h2, (32, 64), ACT.Copy, None)], h2_made),
                     "v": ([(t["v"], whole, ACT.Copy, None)], v_made), "g2": ([(t["g"], whole, ACT.Copy, None)], g_made),
                     "z": ([(t["z"], whole, ACT.Identity, V_DECAY), (t["w"], whole, ACT.Sigmoid, V_DECAY)], z_made),
                     "a": ([(t["a"], whole, ACT.Sigmoid, V_AAAAA)], a_made),
                     "ma": ([(t["ma"], whole, ACT.Sigmoid, V_MISCA)], ma_made),
                     "mk": ([(t["mk"], whole, ACT.Sigmoid, V_MISCK)], mk_made)}
            for name, j in order:
                if name not in reads:
                    continue
                outs, made = reads[name]
                act.wait_ge(done[name].sem, j + 1)
                for out, (r0, r1), func, column in outs:
                    bias = 0.0 if column is None else vecs[r0:r1, column:column + 1]
                    nc.scalar.activation(out[r0:r1, g_of[j]], bank(name, j)[r0:r1, :], func, bias=bias).then_inc(made.sem, 1)


def build_gates(nc, t, banks, vk):
    with PhaseSignals(nc) as sems, ExitStack() as ctx:
        def sig(name, **kw):
            return Signal(sems, name, **kw)

        vecs = t["vecs"]
        e, norm = (ctx.enter_context(nc.sbuf_tensor(n, [P, N], F32)) for n in ("gate_e", "kk_inverse"))
        sq = t["xT"]
        squared, floored, ss_product, log_made, decay_made = sig("kk_squared"), sig("floored"), sig("ss_product"), sig("log_made"), sig("decay_made")
        kk_norm, soft, act_step = sig("kk_norm"), sig("soft"), sig("act_step")
        gain_made, k_scaled, key_gain = sig("gain_made"), sig("k_scaled"), sig("key_gain")
        v_spread, vk_made = sig("v_spread"), sig("vk_made")
        block = ctx.enter_context(nc.Block())
        g_of = [slice(GROUP * j, GROUP * (j + 1)) for j in range(GROUPS)]

        @block.scalar
        def _(act):
            nc.scalar.activation(sq[:, :], t["kkraw"][:, :], ACT.Square).then_inc(squared.sem, 1)
            nc.scalar.activation(e[:, :], t["z"][:, :], ACT.Abs).then_inc(act_step.sem, 1)
            act.wait_ge(act_step.sem, 1)
            nc.scalar.activation(e[:, :], e[:, :], ACT.Exp, scale=-1.0).then_inc(act_step.sem, 1)
            nc.scalar.activation(t["w"][:, :], t["w"][:, :], ACT.Exp, scale=-float(np.exp(-0.5))).then_inc(decay_made.sem, 1)
            act.wait_ge(act_step.sem, 2)
            nc.scalar.activation(e[:, :], e[:, :], ACT.Ln, bias=vecs[:, V_ONE:V_ONE + 1]).then_inc(act_step.sem, 1)
            act.wait_ge(floored.sem, GROUPS)
            nc.scalar.activation(norm[:, :], norm[:, :], ACT.Ln).then_inc(log_made.sem, 1)
            act.wait_ge(log_made.sem, 1)
            nc.scalar.activation(norm[:, :], norm[:, :], ACT.Exp, scale=-0.5).then_inc(kk_norm.sem, 1)
            act.wait_ge(soft.sem, 3)
            nc.scalar.activation(e[:, :], e[:, :], ACT.Exp, scale=-1.0).then_inc(key_gain.sem, 1)

        @block.tensor
        def _(pe):
            pe.wait_ge(squared.sem, 1)
            for j in range(GROUPS):
                nc.tensor.matmul(banks[j][:, :], t["headones"][:, :], sq[:, g_of[j]], start=True, stop=True).then_inc(ss_product.sem, 1)
            for i in range(HS):
                for j in range(GROUPS):
                    n = i * GROUPS + j
                    if n >= 4:
                        if n < 8:
                            pe.wait_ge(floored.sem, n - 3)
                        else:
                            pe.wait_ge(vk_made.sem, n - 7)
                    nc.tensor.matmul(banks[(4 + n) % 8][:, :], t["spread"][:, P * i:P * (i + 1)], t["v"][:, g_of[j]],
                                     start=True, stop=True).then_inc(v_spread.sem, 1)

        @block.vector
        def _(dve):
            nc.vector.tensor_scalar(vk[:, 0:N], t["a"][:, :], -1.0, 1.0, ALU.mult, ALU.add).then_inc(gain_made.sem, 1)
            dve.wait_ge(act_step.sem, 1)
            nc.vector.tensor_scalar(t["z"][:, :], t["z"][:, :], -1.0, 0.0, ALU.mult, ALU.max).then_inc(soft.sem, 1)
            for j in range(GROUPS):
                dve.wait_ge(ss_product.sem, j + 1)
                nc.vector.tensor_scalar(norm[:, g_of[j]], banks[j][:, :], NORM_FLOOR ** 2, None, ALU.max).then_inc(floored.sem, 1)
            dve.wait_ge(gain_made.sem, 1)
            nc.vector.tensor_tensor(vk[:, 0:N], vk[:, 0:N], t["ma"][:, :], ALU.mult).then_inc(gain_made.sem, 1)
            dve.wait_ge(act_step.sem, 3)
            dve.wait_ge(soft.sem, 1)
            nc.vector.tensor_tensor(e[:, :], e[:, :], t["z"][:, :], ALU.add).then_inc(soft.sem, 1)
            dve.wait_ge(soft.sem, 2)
            nc.vector.scalar_tensor_tensor(out=e[:, :], in0=e[:, :], scalar=0.5, in1=t["mk"][:, :],
                                           op0=ALU.add, op1=ALU.mult).then_inc(soft.sem, 1)
            dve.wait_ge(gain_made.sem, 2)
            nc.vector.tensor_tensor(vk[:, 0:N], vk[:, 0:N], t["a"][:, :], ALU.add).then_inc(gain_made.sem, 1)
            dve.wait_ge(gain_made.sem, 3)
            nc.vector.tensor_tensor(t["k"][:, :], t["k"][:, :], vk[:, 0:N], ALU.mult).then_inc(k_scaled.sem, 1)
            dve.wait_ge(key_gain.sem, 1)
            dve.wait_ge(k_scaled.sem, 1)
            nc.vector.tensor_tensor(t["k"][:, :], t["k"][:, :], e[:, :], ALU.mult).then_inc(k_scaled.sem, 1)
            dve.wait_ge(k_scaled.sem, 2)
            per = GROUP // CHUNK
            view = vk[:, :].rearrange("p (l i c) -> p l i c", i=HS, c=CHUNKS)
            for i in range(HS):
                for j in range(GROUPS):
                    n = i * GROUPS + j
                    dve.wait_ge(v_spread.sem, n + 1)
                    nc.vector.tensor_tensor(view[:, :, i, per * j:per * (j + 1)],
                                            banks[(4 + n) % 8][:, :].rearrange("p (c l) -> p l c", l=CHUNK),
                                            t["k"][:, g_of[j]].rearrange("p (c l) -> p l c", l=CHUNK),
                                            ALU.mult).then_inc(vk_made.sem, 1)

        @block.gpsimd
        def _(pool):
            pool.wait_ge(kk_norm.sem, 1)
            nc.gpsimd.tensor_tensor(out=t["kkraw"][:, :], in0=t["kkraw"][:, :], in1=norm[:, :], op=ALU.mult).then_inc(kk_norm.sem, 1)
            pool.wait_ge(kk_norm.sem, 2)
            nc.gpsimd.tensor_tensor(out=norm[:, :], in0=t["kkraw"][:, :], in1=t["a"][:, :], op=ALU.mult).then_inc(kk_norm.sem, 1)
            pool.wait_ge(kk_norm.sem, 3)
            pool.wait_ge(gain_made.sem, 3)
            nc.gpsimd.tensor_scalar(t["b"][:, :], norm[:, :], -1.0, None, ALU.mult).then_inc(kk_norm.sem, 1)


def build_scan(nc, t, banks, vk, state):
    with PhaseSignals(nc) as sems, ExitStack() as ctx:
        def sig(name, **kw):
            return Signal(sems, name, **kw)

        W = HS * CHUNKS
        at_end = (CHUNK - 1) % 2
        ahead = ctx.enter_context(nc.sbuf_tensor("sc_ahead", [P, 2, W], F32))
        states = (ahead, state) if at_end else (state, ahead)
        m, sw, ub = (ctx.enter_context(nc.sbuf_tensor(n, [P, 2, W], F32)) for n in ("sc_m", "sc_sw", "sc_ub"))
        m2 = t["xT"][:, 0:4 * W].rearrange("p (s n) -> p s n", s=4)
        s_set = sig("s_set", per=2)
        s_new = [sig(f"s_new{p}", credit=1) for p in range(2)]
        s_kk = [sig(f"s_kk{p}", credit=1) for p in range(2)]
        u_product = [sig(f"u_product{p}", credit=1) for p in range(2)]
        ub_made = [sig(f"ub_made{p}", credit=1) for p in range(2)]
        decayed = [sig(f"decayed{p}") for p in range(2)]
        s_sum = sig("s_sum")
        s_r = [sig(f"s_r{p}", credit=1) for p in range(2)]
        y_product = [sig(f"y_product{p}", credit=2) for p in range(2)]
        y_read = [sig(f"y_read{p}", credit=1) for p in range(2)]
        block = ctx.enter_context(nc.Block())

        def step(name, l):
            v = t[name][:, :].rearrange("p (c l) -> p l c", l=CHUNK)[:, ds(l, 1), :]
            return v.to_broadcast([P, HS, CHUNKS])

        def rows(buf, p):
            return buf[:, p, :].rearrange("p (r c) -> p r c", c=CHUNKS)

        y_of = (t["y"], t["zy"])

        def unrolled(engine, stage):
            with engine.Fori(0, CHUNK - 4, 2) as k:
                for odd in range(2):
                    stage(k + 2 + odd, odd)

        @block.vector
        def _(dve):
            nc.vector.memset(states[1][:, 0, :], 0.0).then_inc(s_set.sem, 1)
            nc.vector.tensor_copy(rows(states[1], 1), t["rowmask"][:, :].unsqueeze(2).to_broadcast([P, HS, CHUNKS])).then_inc(s_set.sem, 1)
            dve.wait_ge(s_set.sem, 2)
            for p in range(2):
                for s in (s_new[p], s_kk[p], ub_made[p]):
                    nc.vector.engine_nop().then_inc(s.sem, 1)
            nc.vector.engine_nop().then_inc(s_r[1].sem, 1)

            def times_kk(p, l, odd):
                dve.wait_ge(s_new[p].sem, s_new[p].after(l - 1))
                dve.wait_ge(u_product[p].sem, u_product[p].after(l - 1))
                nc.vector.tensor_tensor(rows(m, p), rows(states[1 - odd], p), step("kkraw", l), ALU.mult).then_inc(s_kk[p].sem, 1)

            def add_vk(l):
                dve.wait_ge(decayed[0].sem, decayed[0].after(l))
                nc.vector.tensor_tensor(sw[:, 0, :], sw[:, 0, :], vk[:, ds(l * W, W)], ALU.add).then_inc(s_sum.sem, 1)

            def times_b(p, l):
                dve.wait_ge(u_product[p].sem, u_product[p].after(l))
                nc.vector.tensor_tensor(rows(ub, p), banks[p][:, :].rearrange("p (r c) -> p r c", c=CHUNKS),
                                        step("b", l), ALU.mult).then_inc(ub_made[p].sem, 1)

            def renew(p, l, odd):
                dve.wait_ge(ub_made[p].sem, ub_made[p].after(l))
                if p == 0:
                    dve.wait_ge(s_sum.sem, s_sum.after(l))
                else:
                    dve.wait_ge(decayed[p].sem, decayed[p].after(l))
                dve.wait_ge(s_r[p].sem, s_r[p].after(l - 2))
                nc.vector.tensor_tensor(states[odd][:, p, :], sw[:, p, :], ub[:, p, :], ALU.add).then_inc(s_new[p].sem, 1)

            def times_r(l, odd):
                dve.wait_ge(s_new[1].sem, s_new[1].after(l))
                dve.wait_ge(y_product[1].sem, y_product[1].after(l - 2))
                nc.vector.tensor_tensor(rows(m2, 2 + odd), rows(states[odd], 1), step("r", l), ALU.mult).then_inc(s_r[1].sem, 1)

            def stage(l, odd, first=False):
                times_kk(1, l, odd)
                times_kk(0, l + 1, 1 - odd)
                if not first:
                    times_r(l - 1, 1 - odd)
                add_vk(l + 1)
                times_b(1, l)
                times_b(0, l + 1)
                renew(1, l, odd)
                renew(0, l + 1, 1 - odd)

            times_kk(0, 0, 0)
            add_vk(0)
            times_b(0, 0)
            renew(0, 0, 0)
            stage(0, 0, first=True)
            stage(1, 1)
            unrolled(dve, stage)
            stage(CHUNK - 2, 0)
            times_kk(1, CHUNK - 1, 1)
            times_r(CHUNK - 2, 0)
            times_b(1, CHUNK - 1)
            renew(1, CHUNK - 1, 1)
            times_r(CHUNK - 1, 1)

        @block.gpsimd
        def _(pool):
            carry = sems.carrier(pool, "pool_carried")
            nc.gpsimd.engine_nop().then_inc(s_r[0].sem, 1)
            pool.wait_ge(s_set.sem, 2)

            def decay(p, l, odd):
                pool.wait_ge(s_new[p].sem, s_new[p].after(l - 1))
                carry()
                nc.gpsimd.tensor_tensor(out=rows(sw, p), in0=rows(states[1 - odd], p), in1=step("w", l), op=ALU.mult).then_inc(decayed[p].sem, 1)

            def times_r(l, odd):
                pool.wait_ge(s_new[0].sem, s_new[0].after(l))
                pool.wait_ge(y_product[0].sem, y_product[0].after(l - 2))
                carry()
                nc.gpsimd.tensor_tensor(out=rows(m2, odd), in0=rows(states[odd], 0), in1=step("r", l), op=ALU.mult).then_inc(s_r[0].sem, 1)

            def stage(l, odd):
                decay(0, l + 1, 1 - odd)
                decay(1, l, odd)
                times_r(l, odd)

            decay(0, 0, 0)
            for l in range(2):
                stage(l, l)
            unrolled(pool, stage)
            stage(CHUNK - 2, 0)
            decay(1, CHUNK - 1, 1)
            times_r(CHUNK - 1, 1)

        @block.tensor
        def _(pe):
            for p in range(2):
                nc.tensor.drain().then_inc(u_product[p].sem, 1)
                for _ in range(y_product[p].credit):
                    nc.tensor.drain().then_inc(y_product[p].sem, 1)

            def products_u(p, l):
                pe.wait_ge(s_kk[p].sem, s_kk[p].after(l))
                pe.wait_ge(ub_made[p].sem, ub_made[p].after(l - 1))
                nc.tensor.matmul(banks[p][:, :], t["headones"][:, :], m[:, p, :], start=True, stop=True).then_inc(u_product[p].sem, 1)

            def products_y(p, l, odd):
                pe.wait_ge(s_r[p].sem, s_r[p].after(l))
                pe.wait_ge(y_read[p].sem, y_read[p].after(l - 1))
                for i in range(HS):
                    last = nc.tensor.matmul(banks[2 + p][:, 0:CHUNKS], t["collect"][:, P * i:P * (i + 1)],
                                            m2[:, 2 * p + odd, CHUNKS * i:CHUNKS * (i + 1)], start=(i == 0), stop=(i == HS - 1))
                last.then_inc(y_product[p].sem, 1)

            def stage(l, odd):
                products_u(1, l)
                products_u(0, l + 1)
                for p in range(2):
                    products_y(p, l - 1, 1 - odd)

            products_u(0, 0)
            products_u(1, 0)
            products_u(0, 1)
            stage(1, 1)
            unrolled(pe, stage)
            stage(CHUNK - 2, 0)
            products_u(1, CHUNK - 1)
            for odd in range(2):
                for p in range(2):
                    products_y(p, CHUNK - 2 + odd, odd)

        @block.scalar
        def _(act):
            for p in range(2):
                nc.scalar.drain().then_inc(y_read[p].sem, 1)
            with act.Fori(0, CHUNK) as l:
                for p in range(2):
                    act.wait_ge(y_product[p].sem, y_product[p].after(l))
                    out = y_of[p][:, :].rearrange("p (c l) -> p l c", l=CHUNK)[:, ds(l, 1), :]
                    nc.scalar.activation(out, banks[2 + p][:, 0:CHUNKS].unsqueeze(1), ACT.Copy).then_inc(y_read[p].sem, 1)


def build_mix_output(nc, a, t, banks, state, x_mid, x_all):
    with PhaseSignals(nc) as sems, ExitStack() as ctx:
        def sig(name, **kw):
            return Signal(sems, name, **kw)

        vecs, y = t["vecs"], t["y"]
        spreadG, prop = (ctx.enter_context(nc.sbuf_tensor(n, [P, CHUNKS, P], F32)) for n in ("spreadG", "prop"))
        start = ctx.enter_context(nc.sbuf_tensor("start", [P, CHUNKS, HS], F32))
        stats = ctx.enter_context(nc.sbuf_tensor("ln_stats", [P, BLOCKS, 6], F32))
        mv = ctx.enter_context(nc.sbuf_tensor("ln_mv", [P, BLOCKS, 2], F32))
        x_tok = ctx.enter_context(nc.sbuf_tensor("x_tok_sb", [P, BLOCKS, C], F32))
        yc, ysq, bonus = t["z"], t["w"], t["kkraw"]
        EIGHT = 8
        PER = BLOCKS // GROUPS
        BEHIND = 2 * EIGHT
        expanded, turned, prop_read = sig("expanded"), sig("turned"), sig("prop_read")
        start_set, chain_product, started = sig("start_set"), sig("chain_product"), sig("started")
        s_expanded, last_expanded, y_part, y_full = sig("s_expanded"), sig("last_expanded"), sig("y_part"), sig("y_full")
        mean_product, centred, y_squared, var_product, y_log = (sig(n) for n in ("mean_product", "centred", "y_squared", "var_product", "y_log"))
        y_recip, y_step, rk_made, rk_product = sig("y_recip"), sig("y_step"), sig("rk_made"), sig("rk_product")
        bonus_made, gated, o_product, summed = sig("bonus_made"), sig("gated"), sig("o_product"), sig("summed")
        stat_made, mv_made, ln_root, ln_recip, normed, copied, x_loaded = (sig(n) for n in ("stat_made", "mv_made", "ln_root", "ln_recip", "normed", "copied", "x_loaded"))
        g_of = [slice(GROUP * j, GROUP * (j + 1)) for j in range(GROUPS)]
        hm = t["headmask"][:, :].unsqueeze(1).unsqueeze(3).to_broadcast([P, EIGHT, HEADS, HS])
        block = ctx.enter_context(nc.Block())

        @block.sync
        def _(sp):
            sp.dma_start(x_tok[:, :, :], a["x_tok"]).then_inc(x_loaded.sem, 16)

        @block.gpsimd
        def _(pool):
            pool.wait_ge(start_set.sem, B)
            pool.wait_ge(turned.sem, CHUNKS)
            for group in range(SEQ_CHUNKS // EIGHT - 1):
                for s in range(B):
                    pool.wait_ge(started.sem, B * (EIGHT * (group + 1) - 1))
                    cs = slice(s * SEQ_CHUNKS + EIGHT * group, s * SEQ_CHUNKS + EIGHT * (group + 1))
                    nc.gpsimd.tensor_tensor(out=spreadG[:, cs, :].rearrange("p c (h r) -> p c h r", h=HEADS),
                                            in0=start[:, cs, :].unsqueeze(2).to_broadcast([P, EIGHT, HEADS, HS]), in1=hm,
                                            op=ALU.mult).then_inc(s_expanded.sem, 1)

        @block.vector
        def _(dve):
            nc.vector.scalar_tensor_tensor(out=bonus[:, :], in0=t["r"][:, :], scalar=vecs[:, V_FAAAA:V_FAAAA + 1], in1=t["k"][:, :],
                                           op0=ALU.mult, op1=ALU.mult).then_inc(rk_made.sem, 1)
            G = state[:, 1, :].rearrange("p (r c) -> p c r", c=CHUNKS)
            for e in range(CHUNKS // EIGHT):
                cs = slice(EIGHT * e, EIGHT * (e + 1))
                nc.vector.tensor_tensor(spreadG[:, cs, :].rearrange("p c (h r) -> p c h r", h=HEADS),
                                        G[:, cs, :].unsqueeze(2).to_broadcast([P, EIGHT, HEADS, HS]), hm,
                                        ALU.mult).then_inc(expanded.sem, 1)
            for s in range(B):
                nc.vector.memset(start[:, s * SEQ_CHUNKS, :], 0.0).then_inc(start_set.sem, 1)
            for j in range(GROUPS):
                dve.wait_ge(rk_product.sem, j + 1)
                nc.vector.tensor_tensor(bonus[:, g_of[j]], banks[4 + j % 2][:, :], t["v"][:, g_of[j]],
                                        ALU.mult).then_inc(bonus_made.sem, 1)
            H = state[:, 0, :].rearrange("p (r c) -> p c r", c=CHUNKS)
            for n in range(SEQ_CHUNKS - 1):
                for s in range(B):
                    c = s * SEQ_CHUNKS + n
                    dve.wait_ge(chain_product.sem, B * n + s + 1)
                    nc.vector.tensor_tensor(start[:, c + 1, :], banks[6 + s][:, 0:HS], H[:, c, :], ALU.add).then_inc(started.sem, 1)
            dve.wait_ge(start_set.sem, B)
            dve.wait_ge(started.sem, B * (SEQ_CHUNKS - 1))
            dve.wait_ge(turned.sem, CHUNKS)
            for s in range(B):
                cs = slice((s + 1) * SEQ_CHUNKS - EIGHT, (s + 1) * SEQ_CHUNKS)
                nc.vector.tensor_tensor(spreadG[:, cs, :].rearrange("p c (h r) -> p c h r", h=HEADS),
                                        start[:, cs, :].unsqueeze(2).to_broadcast([P, EIGHT, HEADS, HS]), hm,
                                        ALU.mult).then_inc(last_expanded.sem, 1)
            for j in range(GROUPS):
                dve.wait_ge(y_part.sem, B * (j % (GROUPS // B)) + j // (GROUPS // B) + 1)
                nc.vector.tensor_tensor(y[:, g_of[j]], banks[j][:, :], y[:, g_of[j]], ALU.add).then_inc(y_full.sem, 1)
            for j in range(GROUPS):
                dve.wait_ge(mean_product.sem, j + 1)
                dve.wait_ge(y_full.sem, j + 1)
                nc.vector.scalar_tensor_tensor(out=yc[:, g_of[j]], in0=banks[4 + j % 2][:, :], scalar=-1.0 / HS,
                                               in1=y[:, g_of[j]], op0=ALU.mult, op1=ALU.add).then_inc(centred.sem, 1)
            dve.wait_ge(bonus_made.sem, GROUPS)
            dve.wait_ge(x_loaded.sem, 16)

            def gate_group(j):
                g, y_j = g_of[j], yc[:, g_of[j]]
                dve.wait_ge(y_recip.sem, j + 1)
                nc.vector.tensor_tensor(y_j, y_j, ysq[:, g], ALU.mult).then_inc(y_step.sem, 1)
                dve.wait_ge(y_step.sem, 3 * j + 1)
                nc.vector.tensor_scalar(y_j, y_j, vecs[:, V_LNW:V_LNW + 1], vecs[:, V_LNB:V_LNB + 1],
                                        ALU.mult, ALU.add).then_inc(y_step.sem, 1)
                dve.wait_ge(y_step.sem, 3 * j + 2)
                nc.vector.tensor_tensor(y_j, y_j, bonus[:, g], ALU.add).then_inc(y_step.sem, 1)
                dve.wait_ge(y_step.sem, 3 * j + 3)
                nc.vector.tensor_tensor(y_j, y_j, t["g"][:, g], ALU.mult).then_inc(gated.sem, 1)

            def add_x(j):
                group = range(PER * j, PER * (j + 1))
                for n in group:
                    dve.wait_ge(o_product.sem, n + 1)
                    nc.vector.tensor_tensor(x_tok[:, n, :], banks[n % 4][:, 0:C], x_tok[:, n, :], ALU.add).then_inc(summed.sem, 1)
                for n in group:
                    dve.wait_ge(summed.sem, n + 1)
                    nc.vector.bn_stats(stats[:, n, :], x_tok[:, n, :]).then_inc(stat_made.sem, 1)
                for n in group:
                    dve.wait_ge(stat_made.sem, n + 1)
                    nc.vector.bn_aggr(mv[:, n, :], stats[:, n, :]).then_inc(mv_made.sem, 1)

            for j in range(GROUPS):
                gate_group(j)
                if j:
                    add_x(j - 1)
            add_x(GROUPS - 1)
            dve.wait_ge(ln_root.sem, 1)
            nc.vector.reciprocal(mv[:, :, 1], mv[:, :, 1]).then_inc(ln_recip.sem, 1)
            dve.wait_ge(ln_recip.sem, 1)
            for n in range(BLOCKS):
                nc.vector.tensor_scalar(x_mid[:, n, :], x_tok[:, n, :], mv[:, n, 0:1], mv[:, n, 1:2],
                                        ALU.subtract, ALU.mult).then_inc(normed.sem, 1)

        @block.tensor
        def _(pe):
            for c in range(CHUNKS):
                pe.wait_ge(expanded.sem, c // EIGHT + 1)
                if c >= 4 and c % 4 == 0 and c >= 16:
                    pe.wait_ge(prop_read.sem, c // 4 - 3)
                nc.tensor.transpose(banks[(c // 4) % 4][:, P * (c % 4):P * (c % 4 + 1)], spreadG[:, c, :], t["ident"][:, :]).then_inc(turned.sem, 1)
            pe.wait_ge(rk_made.sem, 1)
            for j in range(GROUPS):
                if j >= 2:
                    pe.wait_ge(bonus_made.sem, j - 1)
                nc.tensor.matmul(banks[4 + j % 2][:, :], t["headones"][:, :], bonus[:, g_of[j]], start=True, stop=True).then_inc(rk_product.sem, 1)
            pe.wait_ge(start_set.sem, B)
            pe.wait_ge(prop_read.sem, CHUNKS // 4)

            def part_of_starts(c):
                at = CHUNK * c
                mm = nc.tensor.matmul(banks[at // GROUP][:, at % GROUP:at % GROUP + CHUNK], spreadG[:, c, :],
                                      t["zy"][:, at:at + CHUNK], start=True, stop=True)
                if (at + CHUNK) % GROUP == 0:
                    mm.then_inc(y_part.sem, 1)

            for n in range(SEQ_CHUNKS + BEHIND):
                for s in range(B):
                    c = s * SEQ_CHUNKS + n
                    if n < SEQ_CHUNKS - 1:
                        if n:
                            pe.wait_ge(started.sem, B * (n - 1) + s + 1)
                        nc.tensor.matmul(banks[6 + s][:, 0:HS], prop[:, c, :], start[:, c, :], start=True, stop=True).then_inc(chain_product.sem, 1)
                for s in range(B):
                    if n >= BEHIND:
                        group = (n - BEHIND) // EIGHT
                        if group < SEQ_CHUNKS // EIGHT - 1:
                            pe.wait_ge(s_expanded.sem, B * (group + 1))
                        else:
                            pe.wait_ge(last_expanded.sem, B)
                        part_of_starts(s * SEQ_CHUNKS + n - BEHIND)
            for j in range(GROUPS):
                pe.wait_ge(y_full.sem, j + 1)
                if j >= 2:
                    pe.wait_ge(centred.sem, j - 1)
                else:
                    pe.wait_ge(bonus_made.sem, GROUPS)
                nc.tensor.matmul(banks[4 + j % 2][:, :], t["headones"][:, :], y[:, g_of[j]], start=True, stop=True).then_inc(mean_product.sem, 1)
            for j in range(GROUPS):
                pe.wait_ge(y_squared.sem, j + 1)
                nc.tensor.matmul(banks[j][:, :], t["headones"][:, :], ysq[:, g_of[j]], start=True, stop=True).then_inc(var_product.sem, 1)
            for n in range(BLOCKS):
                pe.wait_ge(gated.sem, n // PER + 1)
                if n >= 4:
                    pe.wait_ge(summed.sem, n - 3)
                nc.tensor.matmul(banks[n % 4][:, 0:C], yc[:, P * n:P * (n + 1)], t["w_o"][:, :], start=True, stop=True).then_inc(o_product.sem, 1)

        @block.scalar
        def _(act):
            for q in range(CHUNKS // 4):
                act.wait_ge(turned.sem, 4 * q + 4)
                nc.scalar.activation(prop[:, 4 * q:4 * q + 4, :].rearrange("p c m -> p (c m)"), banks[q % 4][:, :], ACT.Copy).then_inc(prop_read.sem, 1)
            for j in range(GROUPS):
                act.wait_ge(centred.sem, j + 1)
                nc.scalar.activation(ysq[:, g_of[j]], yc[:, g_of[j]], ACT.Square).then_inc(y_squared.sem, 1)
            for j in range(GROUPS):
                act.wait_ge(var_product.sem, j + 1)
                nc.scalar.activation(ysq[:, g_of[j]], banks[j][:, :], ACT.Ln, scale=1.0 / HS,
                                     bias=vecs[:, V_YEPS:V_YEPS + 1]).then_inc(y_log.sem, 1)
            for j in range(GROUPS):
                act.wait_ge(y_log.sem, j + 1)
                nc.scalar.activation(ysq[:, g_of[j]], ysq[:, g_of[j]], ACT.Exp, scale=-0.5).then_inc(y_recip.sem, 1)
            act.wait_ge(mv_made.sem, BLOCKS)
            nc.scalar.activation(mv[:, :, 1], mv[:, :, 1], ACT.Sqrt, bias=vecs[:, V_LNEPS:V_LNEPS + 1]).then_inc(ln_root.sem, 1)
            for n in range(BLOCKS):
                act.wait_ge(normed.sem, n + 1)
                nc.scalar.activation(x_all[:, n, :], x_mid[:, n, :], ACT.Copy).then_inc(copied.sem, 1)


def build_mixing(nc, a, banks, x_mid, x_all):
    with ExitStack() as ctx:
        def sb(name, shape):
            return ctx.enter_context(nc.sbuf_tensor(name + "_sb", list(shape), F32))

        t = mix_inputs(sb)
        loads = list(t)
        for name in ("r", "k", "v", "g", "z", "w", "a", "ma", "mk", "kkraw"):
            t[name] = sb(name, (P, N))
        state = sb("state", (P, 2, HS * CHUNKS))
        build_projections(nc, a, t, loads, banks)
        t["b"], t["y"], t["zy"] = t["ma"], t["a"], t["mk"]
        with nc.sbuf_tensor("vk_sb", [P, CHUNK * HS * CHUNKS], F32) as vk:
            build_gates(nc, t, banks, vk)
            build_scan(nc, t, banks, vk, state)
        build_mix_output(nc, a, t, banks, state, x_mid, x_all)


LAG = 6


def build_stream(nc, a, banks, x_all, masks_f):
    with PhaseSignals(nc) as sems, ExitStack() as ctx:
        def sb(name, shape, dt=F32):
            return ctx.enter_context(nc.sbuf_tensor(name, list(shape), dt))

        def sig(name, per=1, credit=2):
            return Signal(sems, name, per, credit)

        def two(name, shape):
            return [sb(f"{name}{u}", shape) for u in range(2)]

        ident, ident16 = sb("st_ident", (P, P)), sb("st_ident16", (P, P), BF16)
        mask16 = sb("mask16", (P, SEQ_BLOCKS, 2 * WINDOW), BF16)
        tables = sb("tables", (P, SEQ_BLOCKS, 4 * DH))
        follows = sb("follows", (P, SEQ_BLOCKS))
        norm_gb = sb("norm_gb", (P, 2 * DEPTH))
        eps = sb("eps", (P, 1))
        wqkv, wo, w1 = sb("wqkv", (P, 2 * 3 * INNER)), sb("wo", (P, 2 * INNER)), sb("w1", (P, 2 * 2 * FF))
        w2, b1, b2 = sb("w2", (P, 2 * len(FF_PARTS) * C)), sb("b1", (P, 2 * 2 * FF)), sb("b2", (P, 2 * C))
        qk_gain = sb("qk_gain", (P, 2 * 4 * DH))
        x_in, xs_T, gains, v_tok = two("x_in", (P, C)), two("xs_T", (P, P)), two("gains", (P, 4, DH)), two("v_tok", (P, INNER))
        edge, edge2 = two("edge", (P, 1)), two("edge2", (P, 1))
        squares, turnedhalf = sb("squares", (P, 2 * INNER)), sb("turnedhalf", (P, 2 * INNER))
        qk, rnorm = two("qk", (P, 2 * INNER)), two("rnorm", (P, 2 * AH))
        q_T, k_T = two("q_T", (P, PAIRS, P)), two("k_T", (P, PAIRS, WINDOW + P))
        v_win = two("v_win", (P, WINDOWS, INNER // 2))
        probs, p_T, o_T = two("probs", (P, PAIRS, 2, DH)), two("p_T", (P, PAIRS, P)), two("o_T", (P, PAIRS, P))
        peak, total = two("peak", (P, 2, PAIRS)), two("total", (P, AH))
        x_att = two("x_att", (P, C))
        ms_T, xn, xn_T, x_res = two("ms_T", (P, P)), two("xn", (P, C)), two("xn_T", (P, P)), two("x_res", (P, C))
        stats, mv = two("st_stats", (P, 6)), two("st_mv", (P, 2))
        gate, act_in = two("gate", (P, FF)), two("act_in", (P, FF))
        ff_T = two("ff_T", (P, len(FF_PARTS), P))

        const_loaded, masks_made = sig("const_loaded", credit=0), sig("masks_made", credit=0)
        LAYER_LOADS = 7
        w_loaded = sig("w_loaded", per=16 * LAYER_LOADS, credit=0)
        cleared = sig("cleared", credit=0)
        x_ready = sig("x_ready", credit=BLOCKS)
        x_taken, gains_made, x_turned, xs_made = sig("x_taken"), sig("gains_made"), sig("x_turned"), sig("xs_made", per=4)
        qk_product, v_product, squared = sig("qk_product", per=4), sig("st_v_product", per=2), sig("squared", per=4)
        rotated, rot_added, ss_made, root_made = sig("rotated", per=12), sig("rot_added", per=2), sig("ss_made"), sig("st_root_made")
        rnorm_made, qk_made, v_read = sig("rnorm_made", per=2), sig("qk_made", per=2), sig("v_read", per=2)
        v_placed = sig("v_placed", per=16 * 16)
        q_turned, qT_made, k_turned, kT_made, halo_made = sig("q_turned", per=2), sig("qT_made", per=2), sig("k_turned", per=2), sig("kT_made", per=2), sig("halo_made")
        s_product, peak_made, shifted, exp_made = sig("s_product"), sig("peak_made", per=2), sig("shifted", per=2), sig("exp_made")
        total_made, p_turned, pT_made = sig("total_made", per=2), sig("p_turned", per=2), sig("pT_made", per=2)
        o_product, o_made, o_turned, oT_made = sig("st_o_product"), sig("o_made", per=2), sig("o_turned", per=2), sig("oT_made", per=2)
        y_product, att_sum = sig("st_y_product"), sig("att_sum")
        m_turned, ms_made, ms_back = sig("m_turned"), sig("ms_made", per=4), sig("ms_back")
        stat_made, sigma_made, rsigma_made, x_normed = sig("stat_made", per=2), sig("sigma_made"), sig("rsigma_made"), sig("x_normed")
        xn_turned, xnT_made, gate_product, a_product = sig("xn_turned"), sig("xnT_made"), sig("up_gate_product"), sig("up_a_product")
        gate_biased, gate_made, a_biased, ff_made = sig("gate_biased"), sig("gate_made"), sig("a_biased"), sig("ff_made")
        ff_turned, ffT_made, y2_product, res_made = sig("ff_turned"), sig("ffT_made", per=2), sig("y2_product"), sig("res_made")

        Q_BANKS, K_BANKS, V_BANKS, X_BANK, FF_BANK = (banks[1], banks[2]), (banks[0], banks[1]), (banks[2], banks[0]), banks[0], banks[3]
        QK_BANKS = Q_BANKS + K_BANKS
        S_BANKS, T_BANKS = (banks[4], banks[5]), (banks[6], banks[7])
        FF_T_FULL = sum(m == P for _, m in FF_PARTS)
        TAIL = FF_PARTS[-1][1]
        TURNED = {"q": (S_BANKS, q_turned), "k": (T_BANKS, k_turned), "p": (T_BANKS, p_turned), "o": (T_BANKS, o_turned)}

        def layer_cols(tile, n, width, at=0, size=None):
            slot = (n // BLOCKS) % 2
            return tile[:, ds(slot * width + at, width if size is None else size)]

        def by_head(ap):
            return ap.rearrange("p (h d) -> p h d", d=DH)

        block = ctx.enter_context(nc.Block())


        def stream(engine, turn):
            def run(n, parity, peeled):
                def at(lag, stage, *which):
                    if not peeled or 0 <= n - lag < STREAM:
                        stage(n - lag, (parity + lag) % 2, *which)
                turn(at)

            for n in range(LAG):
                run(n, n % 2, True)
            with engine.Fori(LAG, STREAM, 2) as n:
                for parity in range(2):
                    run(n + parity, parity, False)
            for n in range(STREAM, STREAM + LAG):
                run(n, n % 2, True)

        @block.sync
        def _(sp):
            carry = sems.carrier(sp, "st_sp_carried")
            for tile, name in ((ident, "ident"), (masks_f, "mask"), (follows, "follows"), (norm_gb, "norm_gb"), (eps, "eps")):
                sp.dma_start(tile[:, :], a[name]).then_inc(const_loaded.sem, 16)
            sp.dma_start(tables[:, :, :], a["tables"]).then_inc(const_loaded.sem, 16)

            def load_layer(layer, slot):
                for tile, name, width in ((wqkv, "wqkv", 3 * INNER), (wo, "wo", INNER), (w1, "w1", 2 * FF), (w2, "w2", len(FF_PARTS) * C)):
                    sp.dma_start(tile[:, slot * width:(slot + 1) * width], a[name][ds(layer, 1), :, :].rearrange("l p n -> p (l n)")).then_inc(w_loaded.sem, 16)
                for tile, name, width in ((b1, "b1", 2 * FF), (b2, "b2", C), (qk_gain, "qk_gain", 4 * DH)):
                    sp.dma_start(tile[:, slot * width:(slot + 1) * width],
                                 a[name][ds(layer, 1), :].to_broadcast([P, width])).then_inc(w_loaded.sem, 16)

            def place_v(n, u):
                sp.wait_ge(v_read.sem, v_read.after(n))
                carry()
                sp.wait_ge(o_product.sem, o_product.after(n - 2))
                carry()
                sp.wait_ge(v_placed.sem, v_placed.after(n - 1))
                for p in range(2):
                    cols = slice(p * INNER // 2, (p + 1) * INNER // 2)
                    for w in range(WINDOWS):
                        own, before = slice(WINDOW * w, WINDOW * (w + 1)), slice(WINDOW * (w - 1), WINDOW * w)
                        sp.dma_start(v_win[u][DH * p + WINDOW:DH * (p + 1), w, :], v_tok[u][own, cols]).then_inc(v_placed.sem, 16)
                        src = v_tok[u][before, cols] if w else v_tok[1 - u][P - WINDOW:P, cols]
                        sp.dma_start(v_win[u][DH * p:DH * p + WINDOW, w, :], src).then_inc(v_placed.sem, 16)

            sp.wait_ge(cleared.sem, 4)
            sp.sem_inc(v_placed.sem, v_placed.credit * v_placed.per)
            load_layer(0, 0)
            sp.wait_ge(w_loaded.sem, w_loaded.after(0))
            load_layer(1, 1)
            EARLY = 4
            for n in range(BLOCKS):
                place_v(n, n % 2)
            with sp.Fori(0, DEPTH // 2 - 1) as pair:
                for half in range(2):
                    layer = pair * 2 + 1 + half
                    for n in range(EARLY):
                        place_v(layer * BLOCKS + n, n % 2)
                    sp.wait_ge(x_ready.sem, x_ready.after(layer * BLOCKS - 1))
                    sp.wait_ge(w_loaded.sem, w_loaded.after(layer))
                    carry()
                    load_layer(layer + 1, half)
                    for n in range(EARLY, BLOCKS):
                        place_v(layer * BLOCKS + n, n % 2)
            for n in range(BLOCKS):
                place_v((DEPTH - 1) * BLOCKS + n, n % 2)

        @block.gpsimd
        def _(pool):
            carry = sems.carrier(pool, "st_pool_carried")
            for s in (x_taken, gains_made, rot_added, qk_made, halo_made, res_made, ff_made):
                pool.sem_inc(s.sem, s.credit * s.per)
            pool.wait_ge(const_loaded.sem, 16 * 6)
            nc.gpsimd.tensor_copy(ident16[:, :], ident[:, :]).then_inc(masks_made.sem, 1)
            nc.gpsimd.tensor_copy(mask16[:, :, :].rearrange("p n k -> p (n k)"), masks_f[:, :]).then_inc(masks_made.sem, 1)
            pool.wait_ge(cleared.sem, 4)

            def take(n, u):
                pool.wait_ge(x_ready.sem, x_ready.after(n - BLOCKS))
                pool.wait_ge(x_turned.sem, x_turned.after(n - 2))
                carry()
                nc.gpsimd.tensor_copy(x_in[u][:, :], x_all[:, ds(n % BLOCKS, 1), :].rearrange("p n c -> p (n c)")).then_inc(x_taken.sem, 1)

            def table_gains(n, u):
                pool.wait_ge(w_loaded.sem, w_loaded.after(n // BLOCKS))
                pool.wait_ge(rotated.sem, rotated.after(n - 2))
                carry()
                nc.gpsimd.tensor_tensor(out=gains[u][:, :, :].rearrange("p f d -> p (f d)"),
                                        in0=tables[:, ds(n % SEQ_BLOCKS, 1), :].rearrange("p n c -> p (n c)"),
                                        in1=layer_cols(qk_gain, n, 4 * DH), op=ALU.mult).then_inc(gains_made.sem, 1)

            def add_turned(n, u, i):
                half = slice(INNER * i, INNER * (i + 1))
                pool.wait_ge(rotated.sem, rotated.after(n, 6 * (i + 1)))
                nc.gpsimd.tensor_tensor(out=qk[u][:, half], in0=qk[u][:, half], in1=turnedhalf[:, half], op=ALU.add).then_inc(rot_added.sem, 1)

            def unit(n, u, i):
                half = slice(INNER * i, INNER * (i + 1))
                pool.wait_ge(rnorm_made.sem, rnorm_made.after(n))
                pool.wait_ge(rot_added.sem, rot_added.after(n, i + 1))
                nc.gpsimd.tensor_tensor(out=by_head(qk[u][:, half]), in0=by_head(qk[u][:, half]),
                                        in1=rnorm[u][:, AH * i:AH * (i + 1)].unsqueeze(2).to_broadcast([P, AH, DH]),
                                        op=ALU.mult).then_inc(qk_made.sem, 1)

            def halo(n, u):
                pool.wait_ge(kT_made.sem, kT_made.after(n - 1))
                pool.wait_ge(s_product.sem, s_product.after(n - 2))
                carry()
                nc.gpsimd.tensor_tensor(out=k_T[u][:, :, 0:WINDOW], in0=k_T[1 - u][:, :, P:P + WINDOW],
                                        in1=follows[:, ds(n % SEQ_BLOCKS, 1)].unsqueeze(2).to_broadcast([P, PAIRS, WINDOW]),
                                        op=ALU.mult).then_inc(halo_made.sem, 1)

            def residual(n, u):
                pool.wait_ge(att_sum.sem, att_sum.after(n))
                pool.wait_ge(x_ready.sem, x_ready.after(n - 2))
                carry()
                nc.gpsimd.tensor_tensor(out=x_res[u][:, :], in0=x_att[u][:, :], in1=layer_cols(b2, n, C), op=ALU.add).then_inc(res_made.sem, 1)

            def glu(n, u):
                pool.wait_ge(gate_made.sem, gate_made.after(n))
                pool.wait_ge(a_biased.sem, a_biased.after(n))
                nc.gpsimd.tensor_tensor(out=gate[u][:, :], in0=gate[u][:, :], in1=act_in[u][:, :], op=ALU.mult).then_inc(ff_made.sem, 1)

            def turn(at):
                at(5, residual)
                at(1, table_gains)
                at(3, unit, 1)
                at(1, take)
                at(2, add_turned, 0)
                at(5, glu)
                at(2, add_turned, 1)
                at(2, halo)
                at(2, unit, 0)

            stream(pool, turn)

        @block.tensor
        def _(pe):
            carry = sems.carrier(pe, "st_pe_carried")
            for s in (x_turned, qk_product, v_product, q_turned, k_turned, s_product, p_turned, o_product, o_turned, y_product,
                      m_turned, ms_back, xn_turned, gate_product, a_product, ff_turned, y2_product):
                pe.sem_inc(s.sem, s.credit * s.per)
            pe.wait_ge(masks_made.sem, 2)

            def turn_x(n, u):
                pe.wait_ge(x_taken.sem, x_taken.after(n))
                pe.wait_ge(v_read.sem, v_read.after(n - 1))
                nc.tensor.transpose(X_BANK[:, 0:P], x_in[u][:, :], ident[:, :]).then_inc(x_turned.sem, 1)

            def project_qk(n, u, i):
                if i == 0:
                    pe.wait_ge(xs_made.sem, xs_made.after(n))
                    pe.wait_ge(w_loaded.sem, w_loaded.after(n // BLOCKS))
                    pe.wait_ge(rotated.sem, rotated.after(n - 1))
                if i == 1:
                    pe.wait_ge(v_read.sem, v_read.after(n - 1, 1))
                if i == 3:
                    pe.wait_ge(rotated.sem, rotated.after(n, 3))
                nc.tensor.matmul(QK_BANKS[i][:, :], xs_T[u][:, :], layer_cols(wqkv, n, 3 * INNER, 512 * i, 512),
                                 start=True, stop=True).then_inc(qk_product.sem, 1)

            def project_v(n, u, i):
                pe.wait_ge(rotated.sem, rotated.after(n, 6 + 3 * i))
                nc.tensor.matmul(V_BANKS[i][:, :], xs_T[u][:, :], layer_cols(wqkv, n, 3 * INNER, 2 * INNER + 512 * i, 512),
                                 start=True, stop=True).then_inc(v_product.sem, 1)

            def transposes(which, n, source):
                outs, turned = TURNED[which]
                for i in range(PAIRS):
                    mm = nc.tensor.transpose(outs[i // 4][:, P * (i % 4):P * (i % 4 + 1)], source[:, P * i:P * (i + 1)], ident[:, :])
                    if i % 4 == 3:
                        mm.then_inc(turned.sem, 1)

            def turn_q(n, u):
                pe.wait_ge(qk_made.sem, qk_made.after(n, 1))
                pe.wait_ge(o_made.sem, o_made.after(n - 1))
                transposes("q", n, qk[u][:, 0:INNER])

            def turn_k(n, u):
                pe.wait_ge(qk_made.sem, qk_made.after(n, 2))
                pe.wait_ge(oT_made.sem, oT_made.after(n - 1))
                transposes("k", n, qk[u][:, INNER:2 * INNER])

            def scores(n, u):
                pe.wait_ge(qT_made.sem, qT_made.after(n))
                pe.wait_ge(kT_made.sem, kT_made.after(n))
                pe.wait_ge(halo_made.sem, halo_made.after(n))
                mask = mask16[:, ds(n % SEQ_BLOCKS, 1), :].to_broadcast([P, PAIRS, 2 * WINDOW])
                for p in range(2):
                    nc.tensor.matmul(S_BANKS[p][:, :].rearrange("p (a k) -> p a k", a=PAIRS), ident16[:, :], mask,
                                     start=True, stop=False, skip_group_check=True)
                for a_ in range(PAIRS):
                    for w in range(WINDOWS):
                        for p in range(2):
                            at, rows = WINDOW * w, slice(DH * p, DH * (p + 1))
                            mm = nc.tensor.matmul(S_BANKS[p][at:at + WINDOW, 2 * WINDOW * a_:2 * WINDOW * (a_ + 1)],
                                                  q_T[u][rows, a_, at:at + WINDOW], k_T[u][rows, a_, at:at + 2 * WINDOW],
                                                  start=False, stop=True, skip_group_check=True)
                mm.then_inc(s_product.sem, 1)

            def turn_p(n, u):
                pe.wait_ge(exp_made.sem, exp_made.after(n))
                pe.wait_ge(kT_made.sem, kT_made.after(n))
                transposes("p", n, probs[u][:, :, :, :].rearrange("p a b d -> p (a b d)"))

            def outputs(n, u):
                pe.wait_ge(pT_made.sem, pT_made.after(n))
                pe.wait_ge(shifted.sem, shifted.after(n))
                pe.wait_ge(v_placed.sem, v_placed.after(n))
                carry()
                for a_ in range(PAIRS):
                    for w in range(WINDOWS):
                        for p in range(2):
                            at, rows = WINDOW * w, slice(DH * p, DH * (p + 1))
                            mm = nc.tensor.matmul(S_BANKS[p][at:at + WINDOW, DH * a_:DH * (a_ + 1)],
                                                  p_T[u][rows, a_, at:at + WINDOW], v_win[u][rows, w, DH * a_:DH * (a_ + 1)],
                                                  start=True, stop=True, skip_group_check=True)
                mm.then_inc(o_product.sem, 1)

            def turn_o(n, u):
                pe.wait_ge(o_made.sem, o_made.after(n))
                transposes("o", n, probs[u][:, :, :, :].rearrange("p a b d -> p (a b d)"))

            def project_o(n, u):
                pe.wait_ge(oT_made.sem, oT_made.after(n))
                pe.wait_ge(x_ready.sem, x_ready.after(n - 1))
                for i in range(PAIRS):
                    mm = nc.tensor.matmul(FF_BANK[:, 0:C], o_T[u][:, i, :], layer_cols(wo, n, INNER, C * i, C),
                                          start=(i == 0), stop=(i == PAIRS - 1))
                mm.then_inc(y_product.sem, 1)

            def turn_m(n, u):
                pe.wait_ge(att_sum.sem, att_sum.after(n))
                nc.tensor.transpose(FF_BANK[:, 0:P], x_att[u][:, :], ident[:, :]).then_inc(m_turned.sem, 1)

            def turn_back(n, u):
                pe.wait_ge(ms_made.sem, ms_made.after(n))
                nc.tensor.transpose(FF_BANK[:, 0:P], ms_T[u][:, :], ident[:, :]).then_inc(ms_back.sem, 1)

            def turn_xn(n, u):
                pe.wait_ge(x_normed.sem, x_normed.after(n))
                nc.tensor.transpose(FF_BANK[:, 0:P], xn[u][:, :], ident[:, :]).then_inc(xn_turned.sem, 1)

            def up_gate(n, u):
                pe.wait_ge(xnT_made.sem, xnT_made.after(n))
                nc.tensor.matmul(FF_BANK[:, 0:FF], xn_T[u][:, :], layer_cols(w1, n, 2 * FF, FF, FF), start=True, stop=True).then_inc(gate_product.sem, 1)

            def up_a(n, u):
                pe.wait_ge(gate_biased.sem, gate_biased.after(n))
                nc.tensor.matmul(FF_BANK[:, 0:FF], xn_T[u][:, :], layer_cols(w1, n, 2 * FF, 0, FF), start=True, stop=True).then_inc(a_product.sem, 1)

            def turn_ff(n, u):
                pe.wait_ge(ff_made.sem, ff_made.after(n))
                for i, (at, m) in enumerate(FF_PARTS):
                    mm = nc.tensor.transpose(FF_BANK[0:m, P * i:P * (i + 1)], gate[u][:, at:at + m], ident[:, :])
                mm.then_inc(ff_turned.sem, 1)

            def down(n, u):
                pe.wait_ge(ffT_made.sem, ffT_made.after(n))
                for i, (_, m) in enumerate(FF_PARTS):
                    w = layer_cols(w2, n, len(FF_PARTS) * C, C * i, C)
                    mm = nc.tensor.matmul(FF_BANK[:, 0:C], ff_T[u][0:m, i, :], w[0:m], start=(i == 0), stop=(i == len(FF_PARTS) - 1))
                mm.then_inc(y2_product.sem, 1)

            def turn(at):
                at(5, turn_back)
                at(4, outputs)
                at(5, turn_xn)
                at(2, project_v, 1)
                at(5, up_gate)
                at(4, turn_o)
                at(1, turn_x)
                at(3, turn_q)
                at(3, turn_k)
                at(1, project_qk, 0)
                at(5, up_a)
                at(3, scores)
                at(5, turn_ff)
                at(1, project_qk, 1)
                at(5, down)
                at(1, project_qk, 2)
                at(4, project_o)
                at(3, turn_p)
                at(4, turn_m)
                at(1, project_qk, 3)
                at(1, project_v, 0)

            stream(pe, turn)

        @block.scalar
        def _(act):
            for s in (xs_made, squared, root_made, v_read, qT_made, kT_made, exp_made, pT_made, oT_made,
                      ms_made, sigma_made, xnT_made, gate_made, ffT_made):
                act.sem_inc(s.sem, s.credit * s.per)
            act.wait_ge(const_loaded.sem, 16 * 6)
            act.wait_ge(cleared.sem, 4)

            def shift(n, u, bank, out, last, made):
                nc.scalar.activation(out[u][0:64, :], bank[0:64, 0:P], ACT.Copy).then_inc(made.sem, 1)
                nc.scalar.activation(out[u][64:P, 1:P], bank[64:P, 0:P - 1], ACT.Copy).then_inc(made.sem, 1)
                act.wait_ge(made.sem, made.after(n - 1))
                nc.scalar.activation(out[u][64:P, 0:1], last[1 - u][64:P, :], ACT.Copy,
                                     scale=follows[64:P, ds(n % SEQ_BLOCKS, 1)]).then_inc(made.sem, 1)
                nc.scalar.activation(last[u][64:P, :], bank[64:P, P - 1:P], ACT.Copy).then_inc(made.sem, 1)

            def shift_x(n, u):
                act.wait_ge(x_turned.sem, x_turned.after(n))
                act.wait_ge(v_product.sem, v_product.after(n - 2))
                shift(n, u, X_BANK, xs_T, edge, xs_made)

            def square(n, u, i):
                act.wait_ge(ss_made.sem, ss_made.after(n - 1))
                act.wait_ge(qk_product.sem, qk_product.after(n, i + 1))
                nc.scalar.activation(squares[:, 512 * i:512 * (i + 1)], QK_BANKS[i][:, :], ACT.Square).then_inc(squared.sem, 1)

            def root(n, u):
                act.wait_ge(ss_made.sem, ss_made.after(n))
                nc.scalar.activation(rnorm[u][:, :], rnorm[u][:, :], ACT.Sqrt).then_inc(root_made.sem, 1)

            def read_v(n, u, i):
                act.wait_ge(v_placed.sem, v_placed.after(n - 1))
                act.wait_ge(v_product.sem, v_product.after(n, i + 1))
                out = v_tok[u][:, :].rearrange("p (b a d) -> p b a d", b=2, d=DH)[:, :, 4 * i:4 * i + 4, :]
                nc.scalar.activation(out, V_BANKS[i][:, :].rearrange("p (a b d) -> p b a d", b=2, d=DH), ACT.Copy).then_inc(v_read.sem, 1)

            def read_q(n, u):
                act.wait_ge(s_product.sem, s_product.after(n - 2))
                read_turned(n, u, S_BANKS, q_turned, q_T, qT_made)

            def read_k(n, u):
                act.wait_ge(s_product.sem, s_product.after(n - 2))
                act.wait_ge(halo_made.sem, halo_made.after(n - 1))
                for i in range(2):
                    act.wait_ge(k_turned.sem, k_turned.after(n, i + 1))
                    nc.scalar.activation(k_T[u][:, 4 * i:4 * i + 4, WINDOW:], T_BANKS[i][:, :].rearrange("p (a t) -> p a t", a=4), ACT.Copy).then_inc(kT_made.sem, 1)

            def exponent(n, u):
                act.wait_ge(shifted.sem, shifted.after(n))
                pr = probs[u][:, :, :, :].rearrange("p a b d -> p (a b d)")
                nc.scalar.activation(pr, pr, ACT.Exp, scale=QK_SCALE).then_inc(exp_made.sem, 1)

            def read_turned(n, u, banks_, turned, out, made):
                for i in range(2):
                    act.wait_ge(turned.sem, turned.after(n, i + 1))
                    nc.scalar.activation(out[u][:, 4 * i:4 * i + 4, :].rearrange("p a t -> p (a t)"), banks_[i][:, :], ACT.Copy).then_inc(made.sem, 1)

            def read_p(n, u):
                act.wait_ge(o_product.sem, o_product.after(n - 2))
                read_turned(n, u, T_BANKS, p_turned, p_T, pT_made)

            def read_oT(n, u):
                act.wait_ge(y_product.sem, y_product.after(n - 2))
                read_turned(n, u, T_BANKS, o_turned, o_T, oT_made)

            def shift_m(n, u):
                act.wait_ge(m_turned.sem, m_turned.after(n))
                act.wait_ge(ms_back.sem, ms_back.after(n - 2))
                shift(n, u, FF_BANK, ms_T, edge2, ms_made)

            def sigma(n, u):
                act.wait_ge(stat_made.sem, stat_made.after(n))
                nc.scalar.activation(mv[u][:, 1:2], mv[u][:, 1:2], ACT.Sqrt, bias=eps[:, :]).then_inc(sigma_made.sem, 1)

            def affine(n, u):
                act.wait_ge(xn_turned.sem, xn_turned.after(n))
                act.wait_ge(a_product.sem, a_product.after(n - 2))
                layer = n // BLOCKS
                nc.scalar.activation(xn_T[u][:, :], FF_BANK[:, 0:P], ACT.Identity, scale=norm_gb[:, ds(layer, 1)],
                                     bias=norm_gb[:, ds(layer + DEPTH, 1)]).then_inc(xnT_made.sem, 1)

            def gelu(n, u):
                act.wait_ge(gate_biased.sem, gate_biased.after(n))
                nc.scalar.activation(gate[u][:, :], gate[u][:, :], ACT.Gelu).then_inc(gate_made.sem, 1)

            def read_ff(n, u):
                act.wait_ge(ff_turned.sem, ff_turned.after(n))
                act.wait_ge(y2_product.sem, y2_product.after(n - 2))
                nc.scalar.activation(ff_T[u][:, 0:FF_T_FULL, :].rearrange("p i t -> p (i t)"), FF_BANK[:, 0:FF_T_FULL * P], ACT.Copy).then_inc(ffT_made.sem, 1)
                nc.scalar.activation(ff_T[u][0:TAIL, FF_T_FULL, :], FF_BANK[0:TAIL, FF_T_FULL * P:(FF_T_FULL + 1) * P], ACT.Copy).then_inc(ffT_made.sem, 1)

            def turn(at):
                at(3, read_oT)
                at(0, shift_x)
                at(2, read_q)
                at(2, read_k)
                at(0, square, 0)
                at(1, root)
                at(4, gelu)
                at(4, read_ff)
                at(0, square, 1)
                at(2, exponent)
                at(2, read_p)
                at(3, shift_m)
                at(0, square, 2)
                at(3, sigma)
                at(0, read_v, 0)
                at(0, square, 3)
                at(3, affine)
                at(0, read_v, 1)

            stream(act, turn)

        @block.vector
        def _(dve):
            carry = sems.carrier(dve, "st_dve_carried")
            for tile in (edge[1][64:P, :], edge2[1][64:P, :], v_tok[1][P - WINDOW:P, :]):
                nc.vector.memset(tile, 0.0).then_inc(cleared.sem, 1)
            nc.vector.memset(k_T[1][:, :, P:P + WINDOW], 0.0).then_inc(cleared.sem, 1)
            for s in (x_ready, rotated, ss_made, rnorm_made, peak_made, shifted, total_made, o_made, att_sum, stat_made, rsigma_made,
                      x_normed, gate_biased, a_biased):
                dve.sem_inc(s.sem, s.credit * s.per)

            def rotate(n, u, i):
                dve.wait_ge(squared.sem, squared.after(n, i + 1))
                if i == 0:
                    dve.wait_ge(gains_made.sem, gains_made.after(n))
                    dve.wait_ge(k_turned.sem, k_turned.after(n - 2))
                if i % 2 == 0:
                    dve.wait_ge(rot_added.sem, rot_added.after(n - 1, i // 2 + 1))
                cols, src = slice(512 * i, 512 * (i + 1)), by_head(QK_BANKS[i][:, :])
                cos, sin = (gains[u][:, 2 * (i // 2) + f:2 * (i // 2) + f + 1, :] for f in range(2))
                nc.vector.tensor_tensor(by_head(qk[u][:, cols]), src, cos.to_broadcast([P, 8, DH]), ALU.mult).then_inc(rotated.sem, 1)
                half = DH // 2
                for f in range(2):
                    to, frm = slice(half * f, half * (f + 1)), slice(half * (1 - f), half * (2 - f))
                    nc.vector.tensor_tensor(by_head(turnedhalf[:, cols])[:, :, to], src[:, :, frm],
                                            sin[:, :, to].to_broadcast([P, 8, half]), ALU.mult).then_inc(rotated.sem, 1)

            def norms(n, u):
                dve.wait_ge(squared.sem, squared.after(n))
                dve.wait_ge(qk_made.sem, qk_made.after(n - 2))
                nc.vector.reduce_sum(rnorm[u][:, :], by_head(squares[:, :]), AX).then_inc(ss_made.sem, 1)

            def rnorms(n, u):
                dve.wait_ge(root_made.sem, root_made.after(n))
                nc.vector.tensor_scalar(rnorm[u][:, :], rnorm[u][:, :], NORM_FLOOR, None, ALU.max).then_inc(rnorm_made.sem, 1)
                dve.wait_ge(rnorm_made.sem, rnorm_made.after(n, 1))
                nc.vector.reciprocal(rnorm[u][:, :], rnorm[u][:, :]).then_inc(rnorm_made.sem, 1)

            def peaks(n, u):
                dve.wait_ge(s_product.sem, s_product.after(n))
                dve.wait_ge(o_turned.sem, o_turned.after(n - 2))
                for p in range(2):
                    s = S_BANKS[p][:, :].rearrange("p (a k) -> p a k", a=PAIRS)
                    nc.vector.reduce_max(peak[u][:, p, :], s, AX).then_inc(peak_made.sem, 1)

            def shifts(n, u):
                for p in range(2):
                    s = S_BANKS[p][:, :].rearrange("p (a k) -> p a k", a=PAIRS)
                    dve.wait_ge(peak_made.sem, peak_made.after(n, p + 1))
                    nc.vector.tensor_tensor(probs[u][:, :, p, :], s, peak[u][:, p, :].unsqueeze(2).to_broadcast([P, PAIRS, DH]),
                                            ALU.subtract).then_inc(shifted.sem, 1)

            def totals(n, u):
                dve.wait_ge(exp_made.sem, exp_made.after(n))
                dve.wait_ge(o_made.sem, o_made.after(n - 2))
                nc.vector.reduce_sum(total[u][:, :], probs[u][:, :, :, :].rearrange("p a b d -> p (a b) d"), AX).then_inc(total_made.sem, 1)
                dve.wait_ge(total_made.sem, total_made.after(n, 1))
                nc.vector.reciprocal(total[u][:, :], total[u][:, :]).then_inc(total_made.sem, 1)

            def scale_outputs(n, u):
                dve.wait_ge(o_product.sem, o_product.after(n))
                dve.wait_ge(total_made.sem, total_made.after(n))
                for p in range(2):
                    rtotal = total[u][:, :].rearrange("p (a b) -> p a b", b=2)[:, :, p:p + 1]
                    nc.vector.tensor_tensor(probs[u][:, :, p, :], S_BANKS[p][:, :].rearrange("p (a d) -> p a d", d=DH),
                                            rtotal.to_broadcast([P, PAIRS, DH]), ALU.mult).then_inc(o_made.sem, 1)

            def add_attention(n, u):
                dve.wait_ge(y_product.sem, y_product.after(n))
                dve.wait_ge(res_made.sem, res_made.after(n - 2))
                dve.wait_ge(m_turned.sem, m_turned.after(n - 2))
                nc.vector.tensor_tensor(x_att[u][:, :], FF_BANK[:, 0:C],
                                        x_all[:, ds(n % BLOCKS, 1), :].rearrange("p n c -> p (n c)"), ALU.add).then_inc(att_sum.sem, 1)

            def moments(n, u):
                dve.wait_ge(ms_back.sem, ms_back.after(n))
                nc.vector.bn_stats(stats[u][:, :], FF_BANK[:, 0:C]).then_inc(stat_made.sem, 1)
                dve.wait_ge(stat_made.sem, stat_made.after(n, 1))
                carry()
                nc.vector.bn_aggr(mv[u][:, :], stats[u][:, :]).then_inc(stat_made.sem, 1)

            def norm_x(n, u):
                dve.wait_ge(sigma_made.sem, sigma_made.after(n))
                nc.vector.reciprocal(mv[u][:, 1:2], mv[u][:, 1:2]).then_inc(rsigma_made.sem, 1)
                dve.wait_ge(rsigma_made.sem, rsigma_made.after(n))
                nc.vector.tensor_scalar(xn[u][:, :], FF_BANK[:, 0:C], mv[u][:, 0:1], mv[u][:, 1:2],
                                        ALU.subtract, ALU.mult).then_inc(x_normed.sem, 1)

            def bias_gate(n, u):
                dve.wait_ge(gate_product.sem, gate_product.after(n))
                dve.wait_ge(ff_turned.sem, ff_turned.after(n - 2))
                nc.vector.tensor_tensor(gate[u][:, :], FF_BANK[:, 0:FF], layer_cols(b1, n, 2 * FF, FF, FF), ALU.add).then_inc(gate_biased.sem, 1)

            def bias_a(n, u):
                dve.wait_ge(a_product.sem, a_product.after(n))
                dve.wait_ge(ff_made.sem, ff_made.after(n - 2))
                nc.vector.tensor_tensor(act_in[u][:, :], FF_BANK[:, 0:FF], layer_cols(b1, n, 2 * FF, 0, FF), ALU.add).then_inc(a_biased.sem, 1)

            def add_ffn(n, u):
                dve.wait_ge(y2_product.sem, y2_product.after(n))
                dve.wait_ge(res_made.sem, res_made.after(n))
                nc.vector.tensor_tensor(x_all[:, ds(n % BLOCKS, 1), :].rearrange("p n c -> p (n c)"), FF_BANK[:, 0:C], x_res[u][:, :],
                                        ALU.add).then_inc(x_ready.sem, 1)

            def turn(at):
                at(5, norm_x)
                at(4, scale_outputs)
                at(2, rotate, 3)
                at(5, bias_gate)
                at(2, norms)
                at(1, rotate, 0)
                at(5, bias_a)
                at(3, peaks)
                at(5, add_ffn)
                at(3, shifts)
                at(1, rotate, 1)
                at(4, add_attention)
                at(3, totals)
                at(2, rnorms)
                at(4, moments)
                at(1, rotate, 2)

            stream(dve, turn)


def build_final(nc, banks, a, x_mid, x_all, out):
    with PhaseSignals(nc) as sems, ExitStack() as ctx:
        def sig(name):
            return Signal(sems, name)

        stats = ctx.enter_context(nc.sbuf_tensor("fi_stats", [P, BLOCKS, 6], F32))
        mv = ctx.enter_context(nc.sbuf_tensor("fi_mv", [P, BLOCKS, 2], F32))
        eps = ctx.enter_context(nc.sbuf_tensor("fi_eps", [P, 1], F32))
        added, counted, gathered, rooted, inverted, normed, loaded, stored = (
            sig(n) for n in ("fi_added", "fi_counted", "fi_gathered", "fi_rooted", "fi_inverted", "fi_normed", "fi_loaded", "fi_stored"))
        block = ctx.enter_context(nc.Block())

        @block.sync
        def _(sp):
            sp.dma_start(eps[:, :], a["eps"]).then_inc(loaded.sem, 16)
            halves = 2
            for h in range(halves):
                part = slice(BLOCKS // halves * h, BLOCKS // halves * (h + 1))
                sp.wait_ge(normed.sem, BLOCKS // halves * (h + 1))
                sp.dma_start(out.rearrange("(n p) c -> p n c", p=P)[:, part, :], x_all[:, part, :]).then_inc(stored.sem, 16)
            sp.wait_ge(stored.sem, 16 * halves)

        @block.vector
        def _(dve):
            nc.vector.tensor_tensor(x_all[:, :, :], x_all[:, :, :], x_mid[:, :, :], ALU.add).then_inc(added.sem, 1)
            dve.wait_ge(added.sem, 1)
            for n in range(BLOCKS):
                nc.vector.bn_stats(stats[:, n, :], x_all[:, n, :]).then_inc(counted.sem, 1)
            for n in range(BLOCKS):
                dve.wait_ge(counted.sem, n + 1)
                nc.vector.bn_aggr(mv[:, n, :], stats[:, n, :]).then_inc(gathered.sem, 1)
            dve.wait_ge(rooted.sem, 1)
            nc.vector.reciprocal(mv[:, :, 1], mv[:, :, 1]).then_inc(inverted.sem, 1)
            dve.wait_ge(inverted.sem, 1)
            for n in range(BLOCKS):
                nc.vector.tensor_scalar(x_all[:, n, :], x_all[:, n, :], mv[:, n, 0:1], mv[:, n, 1:2],
                                        ALU.subtract, ALU.mult).then_inc(normed.sem, 1)

        @block.scalar
        def _(act):
            act.wait_ge(loaded.sem, 16)
            act.wait_ge(gathered.sem, BLOCKS)
            nc.scalar.activation(mv[:, :, 1], mv[:, :, 1], ACT.Sqrt, bias=eps[:, :]).then_inc(rooted.sem, 1)


def build_program(nc, a, out):
    with ExitStack() as ctx:
        banks = [ctx.enter_context(nc.psum_tensor(f"bank{i}", [P, GROUP], F32)) for i in range(8)]
        x_mid, x_all = (ctx.enter_context(nc.sbuf_tensor(n, [P, BLOCKS, C], F32)) for n in ("x_mid", "x_all"))
        build_mixing(nc, a, banks, x_mid, x_all)
        with nc.sbuf_tensor("masks_f", [P, SEQ_BLOCKS * 2 * WINDOW], F32) as masks_f:
            build_stream(nc, a, banks, x_all, masks_f)
        build_final(nc, banks, a, x_mid, x_all, out)


def layouts(L):
    f = np.float32

    def asn(name, shape=None):
        v = np.asarray(L[name])
        return v if shape is None else v.reshape(shape)

    out = {}
    x = asn("L0_attn_x")
    out["xT"] = np.ascontiguousarray(x.reshape(N, C).T)
    out["x_tok"] = np.ascontiguousarray(x.reshape(BLOCKS, P, C).transpose(1, 0, 2))
    vecs = np.zeros((P, 16), f)
    vecs[:, V_MAAX] = asn("L0_attn_time_maa_x")
    vecs[:, V_MAA:V_MAA + 4] = asn("L0_attn_time_maa", (4, C)).T
    for col, name in ((V_DECAY, "time_decay"), (V_AAAAA, "time_aaaaa"), (V_MISCA, "time_misc_a"), (V_MISCK, "time_misc_k"),
                      (V_FAAAA, "time_faaaa"), (V_LNW, "ln_w"), (V_LNB, "ln_b")):
        vecs[:, col] = asn("L0_attn_" + name)
    vecs[:, V_ONE], vecs[:, V_YEPS], vecs[:, V_LNEPS] = 1.0, Y_EPS, LN_EPS
    out["vecs"] = vecs
    out["ident"] = np.eye(P, dtype=f)
    for name, src in (("w_lo", "maa_w1"), ("w_r", "Wr"), ("w_g1", "gate_w1"), ("w_k", "Wk"), ("w_v", "Wv"), ("w_o", "Wo")):
        out[name] = np.ascontiguousarray(asn("L0_attn_" + src).T)
    out["w_maa"] = np.ascontiguousarray(asn("L0_attn_maa_w2", (P, C)))
    out["w_g2"] = np.ascontiguousarray(asn("L0_attn_gate_w2"))
    w = np.zeros((P, P), f)
    w[:, 0:64], w[:, AAA_AT:AAA_AT + 16], w[:, MA_AT:MA_AT + 16] = (asn("L0_attn_" + n).T for n in ("decay_w1", "aaa_w1", "ma_w1"))
    out["w_xwa"] = w
    w = np.zeros((P, P), f)
    w[0:64], w[AAA_AT:AAA_AT + 16], w[MA_AT:MA_AT + 16] = (asn("L0_attn_" + n) for n in ("decay_w2", "aaa_w2", "ma_w2"))
    out["w_second"] = w
    w = np.zeros((P, 64), f)
    w[:, 0:16], w[:, MK_AT:MK_AT + 16] = (asn("L0_attn_" + n).T for n in ("kkk_w1", "mk_w1"))
    out["w_xk"] = w
    w = np.zeros((64, P), f)
    w[0:16], w[MK_AT:MK_AT + 16] = (asn("L0_attn_" + n) for n in ("kkk_w2", "mk_w2"))
    out["w_xk2"] = w
    head, row = np.arange(P) // HS, np.arange(P) % HS
    same = head[:, None] == head[None, :]
    out["headones"] = same.astype(f)
    out["spread"] = np.concatenate([(same & (row == i)[:, None]).astype(f) for i in range(HS)], 1)
    out["collect"] = np.concatenate([(same & (row == i)[None, :]).astype(f) for i in range(HS)], 1)
    out["headmask"] = (head[:, None] == np.arange(HEADS)[None, :]).astype(f)
    out["rowmask"] = (row[:, None] == np.arange(HS)[None, :]).astype(f)
    return out


def stream_layouts(L):
    f = np.float32
    out = {}

    def asn(name):
        return np.asarray(L["L0_ffn_" + name])

    out["wqkv"] = np.ascontiguousarray(asn("Wqkv"))
    out["wo"] = np.ascontiguousarray(asn("Wo").reshape(DEPTH, PAIRS, P, C).transpose(0, 2, 1, 3).reshape(DEPTH, P, INNER))
    out["w1"] = np.ascontiguousarray(asn("W1"))
    w2 = np.zeros((DEPTH, len(FF_PARTS) * P, C), f)
    w2[:, 0:FF] = asn("W2")
    out["w2"] = np.ascontiguousarray(w2.reshape(DEPTH, len(FF_PARTS), P, C).transpose(0, 2, 1, 3).reshape(DEPTH, P, len(FF_PARTS) * C))
    out["b1"], out["b2"] = np.ascontiguousarray(asn("b1")), np.ascontiguousarray(asn("b2"))
    qs, ks, half = asn("q_scale"), asn("k_scale"), DH // 2

    def swapped(v):
        return np.concatenate([v[:, half:], v[:, :half]], 1)

    out["qk_gain"] = np.ascontiguousarray(np.concatenate([qs, swapped(qs), ks, swapped(ks)], 1))
    out["norm_gb"] = np.ascontiguousarray(np.concatenate([asn("ln_g"), asn("ln_b")], 0).T)
    ar = np.arange(0, DH, 2, dtype=f)
    freqs = np.arange(T, dtype=f)[:, None] * (f(1.0) / f(10000.0) ** (ar / f(DH)))[None, :]
    base = (ar + f(0.4 * DH)) / f(1.4 * DH)
    scale = base[None, :] ** ((np.arange(T, dtype=f) - T // 2) / f(WINDOW // 2))[:, None]
    cos, sin = np.cos(freqs), np.sin(freqs)
    parts = []
    for s in (scale, f(1.0) / scale):
        parts += [cos * s, cos * s, -sin * s, sin * s]
    tab = np.concatenate(parts, 1).astype(f)
    out["tables"] = np.ascontiguousarray(tab.reshape(SEQ_BLOCKS, P, 4 * DH).transpose(1, 0, 2))
    i, j = (np.arange(P) % WINDOW)[:, None], np.arange(2 * WINDOW)[None, :]
    allowed = (j >= i) & (j <= i + WINDOW)
    mask = np.where(allowed, 0.0, MASKED).astype(f)
    full = np.repeat(mask[:, None, :], SEQ_BLOCKS, 1)
    full[0:WINDOW, 0, 0:WINDOW] = MASKED
    out["mask"] = np.ascontiguousarray(full.reshape(P, -1))
    follows = np.ones((P, SEQ_BLOCKS), f)
    follows[:, 0] = 0.0
    out["follows"] = follows
    out["eps"] = np.full((P, 1), LN_EPS, f)
    return out


def kernel(**inputs):
    from concourse import bacc
    from concourse.bass_utils import run_bass_kernel_spmd

    arrays = {**layouts(inputs), **stream_layouts(inputs)}
    nc = bacc.Bacc("TRN2", target_bir_lowering=False, num_devices=1)
    a = {name: nc.dram_tensor(f"in_{name}", list(v.shape), mybir.dt.from_np(v.dtype), kind="ExternalInput").ap()
         for name, v in arrays.items()}
    out = nc.dram_tensor("out", [N, C], F32, kind="ExternalOutput").ap()
    build_program(nc, a, out)
    r = run_bass_kernel_spmd(nc, [{f"in_{name}": v for name, v in arrays.items()}], core_ids=[0])
    return r.results[0]["out"].reshape(B, T, C)
```
